# Optimizing a Trainium2 kernel written in Bass

```python
import numpy as np
import jax
import jax.numpy as jnp

def _softmax(x, axis=-1):
    return jax.nn.softmax(x, axis=axis)

def _gelu(x):
    return jax.nn.gelu(x, approximate=True)

def _silu(x):
    return jax.nn.silu(x)

def _sigmoid(x):
    return jax.nn.sigmoid(x)

def _layernorm(x, axis=-1, eps=1e-05):
    m = jnp.mean(x, axis=axis, keepdims=True)
    v = jnp.var(x, axis=axis, keepdims=True)
    return (x - m) / jnp.sqrt(v + eps)

def _scatter_add(tgt, idx, src, axis=0):
    return tgt.at[idx].add(src)

def _segment_sum(src, seg, n):
    return jax.ops.segment_sum(src, seg, n)
kernel_name = 'mk_decoder_postln_d1_seqx_r8_180b69'

def setup_inputs(seed: int=0):
    np.random.seed(seed)
    _w = jnp.asarray

    def _rec_inputs():
        import jax
        import jax.numpy as jnp
        _rk = jax.random.key(seed)
        x = -0.000125 + 0.9999 * jax.random.normal(jax.random.fold_in(_rk, 1), (4, 256, 256), jnp.float32)
        _lenS = 256 - jax.random.randint(jax.random.fold_in(_rk, 7), (4,), 0, max(1, 256 // 4) + 1, jnp.int32)
        _lenS2 = 256 - jax.random.randint(jax.random.fold_in(_rk, 8), (4,), 0, max(1, 256 // 4) + 1, jnp.int32)
        _ctx_2048P = jax.random.normal(jax.random.fold_in(_rk, 11), (4, 16, 256), jnp.float32)
        _ctx_2048c = jax.random.dirichlet(jax.random.fold_in(_rk, 511), 0.3 * jnp.ones((16,), jnp.float32), (4, 256))
        _ctx_2048t = jnp.einsum('bsk,bkd->bsd', _ctx_2048c, _ctx_2048P)
        _ctx_2048t = _ctx_2048t * jax.lax.rsqrt(jnp.mean(jnp.square(_ctx_2048t)) + 1e-12) * 0.953939
        ctx_2048 = 1.72703e-05 + 1.00003 * (_ctx_2048t + 0.3 * jax.random.normal(jax.random.fold_in(_rk, 611), (4, 256, 256), jnp.float32))
        return (x, ctx_2048)
    x, ctx_2048 = _rec_inputs()

    def _L0_attn_setup():
        import jax, jax.numpy as jnp
        import numpy as np
        key = jax.random.key(seed)
        ks = jax.random.split(key, 5)
        B, S, D = (1, 512, 256)
        H, Dh = (16, 128)
        scale = 1.0 / np.sqrt(D).astype(np.float32)
        return {'x': jax.random.normal(ks[0], (B, S, D), dtype=jnp.float32), 'W_K': jax.random.normal(ks[1], (H, Dh, D), dtype=jnp.float32) * scale, 'W_Q': jax.random.normal(ks[2], (H, Dh, D), dtype=jnp.float32) * scale, 'W_V': jax.random.normal(ks[3], (H, Dh, D), dtype=jnp.float32) * scale, 'W_O': jax.random.normal(ks[4], (D, H * Dh), dtype=jnp.float32) * scale}
    _L0_attn_all = _L0_attn_setup()
    _L0_attn_in = {k: v for k, v in _L0_attn_all.items() if k in ('W_K', 'W_Q', 'W_V', 'W_O')}
    del _L0_attn_all

    def _L0_xattn_setup():
        import jax, jax.numpy as jnp
        import numpy as np
        DIM = 256
        NH = 16
        HD = DIM // NH
        EPS = 1e-06
        IMG_LEN = 257

        def rms_norm(x, w, eps=EPS):
            xf = x.astype(jnp.float32)
            y = xf * jax.lax.rsqrt(jnp.mean(xf * xf, axis=-1, keepdims=True) + eps)
            return y.astype(x.dtype) * w

        def linear(x, w, b):
            return jnp.einsum('blc,oc->blo', x, w) + b

        def attention(q, k, v):
            scale = 1.0 / jnp.sqrt(jnp.asarray(HD, q.dtype))
            scores = jnp.einsum('bqhd,bkhd->bhqk', q, k) * scale
            probs = jax.nn.softmax(scores, axis=-1)
            return jnp.einsum('bhqk,bkhd->bqhd', probs, v)
        key = jax.random.key(seed)
        ks = jax.random.split(key, 12)
        B, L = (2, 1024)
        s = 0.02
        inp = {'x': jax.random.normal(ks[0], (B, L, DIM), jnp.float32), 'context': jax.random.normal(ks[1], (B, 769, DIM), jnp.float32), 'q_w': jax.random.normal(ks[2], (DIM, DIM), jnp.float32) * s, 'q_b': jnp.zeros((DIM,), jnp.float32), 'k_w': jax.random.normal(ks[3], (DIM, DIM), jnp.float32) * s, 'k_b': jnp.zeros((DIM,), jnp.float32), 'v_w': jax.random.normal(ks[4], (DIM, DIM), jnp.float32) * s, 'v_b': jnp.zeros((DIM,), jnp.float32), 'k_img_w': jax.random.normal(ks[5], (DIM, DIM), jnp.float32) * s, 'k_img_b': jnp.zeros((DIM,), jnp.float32), 'v_img_w': jax.random.normal(ks[6], (DIM, DIM), jnp.float32) * s, 'v_img_b': jnp.zeros((DIM,), jnp.float32), 'o_w': jax.random.normal(ks[7], (DIM, DIM), jnp.float32) * s, 'o_b': jnp.zeros((DIM,), jnp.float32), 'norm_q_w': jnp.ones((DIM,), jnp.float32), 'norm_k_w': jnp.ones((DIM,), jnp.float32), 'norm_k_img_w': jnp.ones((DIM,), jnp.float32)}
        return inp
    _L0_xattn_all = _L0_xattn_setup()
    _L0_xattn_in = {k: v for k, v in _L0_xattn_all.items() if k in ('q_w', 'q_b', 'k_w', 'k_b', 'v_w', 'v_b', 'k_img_w', 'k_img_b', 'v_img_w', 'v_img_b', 'o_w', 'o_b', 'norm_q_w', 'norm_k_w', 'norm_k_img_w')}
    del _L0_xattn_all

    def _L0_ffn_setup():
        import jax, jax.numpy as jnp
        import numpy as np
        B, S, D, F, E, K = (2, 256, 256, 1024, 8, 2)
        key = jax.random.key(seed)
        k0, k1, k2, k3 = jax.random.split(key, 4)
        scale = lambda k, shape, fan_in: jax.random.normal(k, shape, jnp.float32) * fan_in ** (-0.5)
        return {'inputs': jax.random.normal(k0, (B, S, D), jnp.float32), 'gate_w': scale(k1, (D, E), D), 'gate_b': jnp.zeros((E,), jnp.float32), 'w1': scale(k2, (E, D, F), D), 'b1': jnp.zeros((E, F), jnp.float32), 'w2': scale(k3, (E, F, D), F), 'b2': jnp.zeros((E, D), jnp.float32)}
    _L0_ffn_all = _L0_ffn_setup()
    _L0_ffn_in = {k: v for k, v in _L0_ffn_all.items() if k in ('gate_w', 'gate_b', 'w1', 'b1', 'w2', 'b2')}
    del _L0_ffn_all
    return {'x': x, 'ctx_2048': ctx_2048, 'L0_attn_W_K': _L0_attn_in['W_K'], 'L0_attn_W_Q': _L0_attn_in['W_Q'], 'L0_attn_W_V': _L0_attn_in['W_V'], 'L0_attn_W_O': _L0_attn_in['W_O'], 'L0_xattn_q_w': _L0_xattn_in['q_w'], 'L0_xattn_q_b': _L0_xattn_in['q_b'], 'L0_xattn_k_w': _L0_xattn_in['k_w'], 'L0_xattn_k_b': _L0_xattn_in['k_b'], 'L0_xattn_v_w': _L0_xattn_in['v_w'], 'L0_xattn_v_b': _L0_xattn_in['v_b'], 'L0_xattn_k_img_w': _L0_xattn_in['k_img_w'], 'L0_xattn_k_img_b': _L0_xattn_in['k_img_b'], 'L0_xattn_v_img_w': _L0_xattn_in['v_img_w'], 'L0_xattn_v_img_b': _L0_xattn_in['v_img_b'], 'L0_xattn_o_w': _L0_xattn_in['o_w'], 'L0_xattn_o_b': _L0_xattn_in['o_b'], 'L0_xattn_norm_q_w': _L0_xattn_in['norm_q_w'], 'L0_xattn_norm_k_w': _L0_xattn_in['norm_k_w'], 'L0_xattn_norm_k_img_w': _L0_xattn_in['norm_k_img_w'], 'L0_ffn_gate_w': _L0_ffn_in['gate_w'], 'L0_ffn_gate_b': _L0_ffn_in['gate_b'], 'L0_ffn_w1': _L0_ffn_in['w1'], 'L0_ffn_b1': _L0_ffn_in['b1'], 'L0_ffn_w2': _L0_ffn_in['w2'], 'L0_ffn_b2': _L0_ffn_in['b2']}

def reference(x, ctx_2048, L0_attn_W_K, L0_attn_W_Q, L0_attn_W_V, L0_attn_W_O, L0_xattn_q_w, L0_xattn_q_b, L0_xattn_k_w, L0_xattn_k_b, L0_xattn_v_w, L0_xattn_v_b, L0_xattn_k_img_w, L0_xattn_k_img_b, L0_xattn_v_img_w, L0_xattn_v_img_b, L0_xattn_o_w, L0_xattn_o_b, L0_xattn_norm_q_w, L0_xattn_norm_k_w, L0_xattn_norm_k_img_w, L0_ffn_gate_w, L0_ffn_gate_b, L0_ffn_w1, L0_ffn_b1, L0_ffn_w2, L0_ffn_b2):
    import jax
    import jax.numpy as jnp

    def _L0_attn_ref(x, W_K, W_Q, W_V, W_O):
        import jax, jax.numpy as jnp
        import numpy as np
        b, pos, d_model = x.shape
        d_head = W_K.shape[1]
        k = jnp.einsum('ihd,bpd->biph', W_K, x)
        q = jnp.einsum('ihd,bpd->biph', W_Q, x)
        v = jnp.einsum('ihd,bpd->biph', W_V, x)
        scores = jnp.einsum('biph,biqh->biqp', k, q)
        mask = jnp.tril(jnp.ones((pos, pos), dtype=x.dtype))
        masked = scores * mask - jnp.float32(10000000000.0) * (1.0 - mask)
        attn = jax.nn.softmax(masked / jnp.sqrt(jnp.float32(d_head)), axis=-1)
        z = jnp.einsum('biqp,biph->biqh', attn, v)
        z_flat = jnp.transpose(z, (0, 2, 1, 3)).reshape(b, pos, -1)
        out = jnp.einsum('df,bqf->bqd', W_O, z_flat)
        return out

    def _L0_xattn_ref(x, context, q_w, q_b, k_w, k_b, v_w, v_b, k_img_w, k_img_b, v_img_w, v_img_b, o_w, o_b, norm_q_w, norm_k_w, norm_k_img_w):
        import jax, jax.numpy as jnp
        import numpy as np
        DIM = 256
        NH = 16
        HD = DIM // NH
        EPS = 1e-06
        IMG_LEN = 257

        def rms_norm(x, w, eps=EPS):
            xf = x.astype(jnp.float32)
            y = xf * jax.lax.rsqrt(jnp.mean(xf * xf, axis=-1, keepdims=True) + eps)
            return y.astype(x.dtype) * w

        def linear(x, w, b):
            return jnp.einsum('blc,oc->blo', x, w) + b

        def attention(q, k, v):
            scale = 1.0 / jnp.sqrt(jnp.asarray(HD, q.dtype))
            scores = jnp.einsum('bqhd,bkhd->bhqk', q, k) * scale
            probs = jax.nn.softmax(scores, axis=-1)
            return jnp.einsum('bhqk,bkhd->bqhd', probs, v)
        B, L, _ = x.shape
        ctx_img = context[:, :IMG_LEN]
        ctx_txt = context[:, IMG_LEN:]
        q = rms_norm(linear(x, q_w, q_b), norm_q_w).reshape(B, L, NH, HD)
        k = rms_norm(linear(ctx_txt, k_w, k_b), norm_k_w).reshape(B, -1, NH, HD)
        v = linear(ctx_txt, v_w, v_b).reshape(B, -1, NH, HD)
        k_img = rms_norm(linear(ctx_img, k_img_w, k_img_b), norm_k_img_w).reshape(B, -1, NH, HD)
        v_img = linear(ctx_img, v_img_w, v_img_b).reshape(B, -1, NH, HD)
        img_x = attention(q, k_img, v_img)
        txt_x = attention(q, k, v)
        out = (txt_x + img_x).reshape(B, L, DIM)
        return linear(out, o_w, o_b)

    def _L0_ffn_ref(inputs, gate_w, gate_b, w1, b1, w2, b2):
        import jax, jax.numpy as jnp
        import numpy as np
        B, S, D, F, E, K = (2, 256, 256, 1024, 8, 2)
        x = inputs.reshape(-1, inputs.shape[-1])
        n = x.shape[0]
        gate_probs = jax.nn.softmax(x @ gate_w + gate_b, axis=-1)
        weights, selected = jax.lax.top_k(gate_probs, K)
        weights = weights / jnp.sum(weights, axis=-1, keepdims=True)
        comb = jnp.zeros((n, E), x.dtype).at[jnp.arange(n)[:, None], selected].set(weights)
        h = jax.nn.gelu(jnp.einsum('nd,edf->enf', x, w1) + b1[:, None, :])
        expert_out = jnp.einsum('enf,efd->end', h, w2) + b2[:, None, :]
        out = jnp.einsum('ne,end->nd', comb, expert_out)
        return out.reshape(inputs.shape[:-1] + (out.shape[-1],))
    x = _layernorm(x + _L0_attn_ref(x, L0_attn_W_K, L0_attn_W_Q, L0_attn_W_V, L0_attn_W_O), axis=-1)
    x = _layernorm(x + _L0_xattn_ref(x, ctx_2048, L0_xattn_q_w, L0_xattn_q_b, L0_xattn_k_w, L0_xattn_k_b, L0_xattn_v_w, L0_xattn_v_b, L0_xattn_k_img_w, L0_xattn_k_img_b, L0_xattn_v_img_w, L0_xattn_v_img_b, L0_xattn_o_w, L0_xattn_o_b, L0_xattn_norm_q_w, L0_xattn_norm_k_w, L0_xattn_norm_k_img_w), axis=-1)
    x = _layernorm(x + _L0_ffn_ref(x, L0_ffn_gate_w, L0_ffn_gate_b, L0_ffn_w1, L0_ffn_b1, L0_ffn_w2, L0_ffn_b2), axis=-1)
    return x

_drawn_inputs = setup_inputs


def setup_inputs(seed=0):
    import zlib

    import numpy as np

    out = dict(_drawn_inputs(seed))
    spreads = {'L0_xattn_q_b': (0.0, 0.312),
     'L0_xattn_k_b': (0.0, 0.1),
     'L0_xattn_v_b': (0.0, 0.1),
     'L0_xattn_k_img_b': (0.0, 0.61),
     'L0_xattn_v_img_b': (0.0, 0.1),
     'L0_xattn_o_b': (0.0, 0.1),
     'L0_xattn_norm_q_w': (1.0, 0.6),
     'L0_xattn_norm_k_w': (1.0, 0.2),
     'L0_xattn_norm_k_img_w': (1.0, 0.6),
     'L0_ffn_gate_b': (0.0, 0.1),
     'L0_ffn_b1': (0.0, 0.1),
     'L0_ffn_b2': (0.0, 0.1)}
    factors = {}
    for name, (base, spread) in spreads.items():
        noise = np.random.default_rng([zlib.crc32(name.encode()), seed]).standard_normal(out[name].shape)
        drawn = base * np.exp(spread * noise) if base else spread * noise
        out[name] = jnp.asarray(drawn.astype(out[name].dtype))
    for name, factor in factors.items():
        out[name] = (out[name] * factor).astype(out[name].dtype)
    return out
```

```python
import concourse.bass as bass
from concourse import mybir
from contextlib import ExitStack


def build_decoder_layer(nc, xT_d, x_d, w_attn_d, ctxT_d, w_x_d, qb_d, kb_d, vb_d, ob_d, nq_d, nk_d,
                        gate_w_d, gate_b_d, w1_d, b1_d, w2_d, b2_d, out_d):
    f32 = mybir.dt.float32
    f32r = mybir.dt.float32r
    bf16 = mybir.dt.bfloat16
    u32 = mybir.dt.uint32
    ALU = mybir.AluOpType
    ACT = mybir.ActivationFunctionType
    AX = mybir.AxisListType

    P = 128
    D = 256
    DC = D // P
    B = x_d.shape[1] // 2
    TT = x_d.shape[1]
    N = TT * P
    S = N // B
    PAIRS = w_attn_d.shape[0]
    H = 2 * PAIRS
    DH = P
    STEPS = H * B
    XH = 16
    XD = D // XH
    ITEMS = XH * B
    E = w1_d.shape[0]
    F = w1_d.shape[3]
    FC = F // P
    SCALE = float(DH) ** -0.5
    XSCALE = float(XD) ** -0.5
    MASKED = 1e10 * SCALE
    LN_EPS = 1e-5
    RMS_EPS = 1e-6
    QKV = 1536
    BIG = 3.0e38

    ctx = ExitStack()
    with ctx:
        def sem(name):
            return ctx.enter_context(nc.semaphore(name))

        def sb(stack, name, shape, dt=f32):
            return stack.enter_context(nc.sbuf_tensor(name, shape, dt))

        acc = sb(ctx, "acc", [P, TT, D])
        ident = sb(ctx, "ident", [P, P])
        stats = sb(ctx, "stats", [P, TT, 6])
        mv = sb(ctx, "mv", [P, TT, 2])
        rstd = sb(ctx, "rstd", [P, TT])
        sd = sb(ctx, "sd", [P, TT])
        eps_ln = sb(ctx, "eps_ln", [P, 1])
        eps_rms = sb(ctx, "eps_rms", [P, 1])
        kss = sb(ctx, "kss", [P, TT])
        qss = sb(ctx, "qss", [P, TT])
        ctxT = sb(ctx, "ctxT", [P, DC, N])
        w_x = sb(ctx, "w_x", [P, 4, DC, D])
        rows_bc = sb(ctx, "rows_bc", [P, 6, D])
        xT1 = sb(ctx, "xT1", [P, DC, N])

        s1 = ExitStack()
        xT_raw = sb(s1, "xT_raw", [P, DC, N])
        xT_hi = sb(s1, "xT_hi", [P, DC, N], f32r)
        xT_lo = sb(s1, "xT_lo", [P, DC, N], f32r)
        qkv_raw = [sb(s1, f"qkv_raw{i}", [P, QKV]) for i in range(2)]
        wo_raw = [sb(s1, f"wo_raw{i}", [P, 2 * D]) for i in range(2)]
        qkv_hi = [sb(s1, f"qkv_hi{i}", [P, QKV], f32r) for i in range(2)]
        qkv_lo = [sb(s1, f"qkv_lo{i}", [P, QKV], f32r) for i in range(2)]
        wo_hi = [sb(s1, f"wo_hi{i}", [P, 2 * D], f32r) for i in range(2)]
        wo_lo = [sb(s1, f"wo_lo{i}", [P, 2 * D], f32r) for i in range(2)]
        QT = [sb(s1, f"QT{i}", [P, N]) for i in range(2)]
        KT = [sb(s1, f"KT{i}", [P, N]) for i in range(2)]
        V = [sb(s1, f"V{i}", [P, TT, 2 * DH]) for i in range(2)]
        Sm = [sb(s1, f"Sm{i}", [P, 384]) for i in range(2)]
        Pr = [sb(s1, f"Pr{i}", [P, 384]) for i in range(2)]
        PT = [sb(s1, f"PT{i}", [P, 384]) for i in range(2)]
        nmax = [sb(s1, f"nmax{i}", [P, 2]) for i in range(2)]
        rsum = [sb(s1, f"rsum{i}", [P, 2]) for i in range(2)]
        rinv = [sb(s1, f"rinv{i}", [P, 2]) for i in range(2)]
        z_hi = [sb(s1, f"z_hi{i}", [P, 2, N], f32r) for i in range(2)]
        z_lo = [sb(s1, f"z_lo{i}", [P, 2, N], f32r) for i in range(2)]
        mask = sb(s1, "mask", [P, 384])
        s1.close()

        s2 = ExitStack()
        k_tok = sb(s2, "k_tok", [P, TT, D])
        v_tok = sb(s2, "v_tok", [P, TT, D])
        q_tok = sb(s2, "q_tok", [P, TT, D])
        sq_junk = sb(s2, "sq_junk", [P, D])
        krs = sb(s2, "krs", [P, TT])
        qrs = sb(s2, "qrs", [P, TT])
        qn = sb(s2, "qn", [P, D])
        stack = [sb(s2, f"stack{i}", [P, XH, 4 * XD], f32r) for i in range(2)]
        QA = [sb(s2, f"QA{i}", [P, XH // 2, S], f32r) for i in range(2)]
        QB = [sb(s2, f"QB{i}", [P, XH // 2, S], f32r) for i in range(2)]
        XK = [sb(s2, f"XK{i}", [P, XH // 2, S], f32r) for i in range(2)]
        Vd = [sb(s2, f"Vd{i}", [P, 2, XH, P]) for i in range(2)]
        xP = [sb(s2, f"xP{i}", [P, 2, S]) for i in range(2)]
        xPT = [sb(s2, f"xPT{i}", [P, 2, S]) for i in range(2)]
        xnmax = [sb(s2, f"xnmax{i}", [P, 2]) for i in range(2)]
        xrsum = [sb(s2, f"xrsum{i}", [P, 2]) for i in range(2)]
        xrinv = [sb(s2, f"xrinv{i}", [P, 2]) for i in range(2)]
        xz = [sb(s2, f"xz{i}", [P, DC, S]) for i in range(2)]
        s2.close()

        s3 = ExitStack()
        w1 = [sb(s3, f"w1_{i}", [P, DC, F]) for i in range(2)]
        w2 = [sb(s3, f"w2_{i}", [P, FC, D]) for i in range(2)]
        b1 = [sb(s3, f"b1_{i}", [P, FC]) for i in range(2)]
        b2 = [sb(s3, f"b2_{i}", [P, D]) for i in range(2)]
        hT = [sb(s3, f"hT{i}", [P, FC, N // 2]) for i in range(2)]
        ysum = sb(s3, "ysum", [P, D])
        gate_w = sb(s3, "gate_w", [P, DC, E])
        gate_b = sb(s3, "gate_b", [P, E])
        logits = sb(s3, "logits", [P, TT, E])
        lmax = sb(s3, "lmax", [P, TT])
        probs = sb(s3, "probs", [P, TT, E])
        psum_ = sb(s3, "psum_", [P, TT])
        top = sb(s3, "top", [P, TT, 8])
        top_i = sb(s3, "top_i", [P, TT, 8], u32)
        top_f = sb(s3, "top_f", [P, TT, 2])
        w12 = sb(s3, "w12", [P, TT])
        wts = sb(s3, "wts", [P, TT, 2])
        iota_e = sb(s3, "iota_e", [P, E])
        oneh = sb(s3, "oneh", [P, TT, E])
        comb = sb(s3, "comb", [P, TT, E])
        s3.close()

        bank = [ctx.enter_context(nc.psum_tensor(f"bank{i}", [P, 512], f32)) for i in range(8)]
        ps_qk = bank[0:2]
        ps_s = bank[2:4]
        ps_t = bank[4]
        ps_v = bank[5]
        ps_o = bank[6]
        ps_z = bank[7]

        names = """x_in0 x_in1 acc_in w_in0 w_in1 wo_in0 wo_in1 misc_in
            ident_zeroed ident_ready mask_ready x_split w_split wo_split
            qk_done qk_evac v_done v_evac s_done s_masked exp_done rinv_ready p_norm pt_done pt_evac
            pv_done zhi_ready zlo_ready o_done o_added
            eps_ready ln_stats ln_mv ln_sd ln_rstd x1_ready xt_done xt_evac
            kv_done k_ready v_ready q_done q_ready kq_ss rms_sd w_hi wo_hi w0_split chain
            normed hi_ready lo_ready stack_ready stk_done stk_evac_act stk_evac_dve zero_ready zero2 vd_ready
            xs_done xmax_ready xexp_done xrinv_ready xp_norm xpt_done xpt_evac xpv_done xz_evac
            xo_done x1b_ready xo_added
            ln2_chain ln2_sd x2_ready x2t_done x2t_evac
            g_done g_in r_chain gexp_done iota_ready
            w1_in0 w1_in1 h_done h_gelu y_done y_sum y_added ln3_chain ln3_sd out_ready out_written""".split()
        s = {n: sem(n) for n in names}

        block = ctx.enter_context(nc.Block())

        def wq_at(hh, c):
            return hh * 256 + c * 128

        def wk_at(hh, c):
            return 512 + hh * 256 + c * 128

        def wv_at(c):
            return 1024 + c * 256

        @block.sync
        def _(sp):
            sp.dma_start(xT_raw[:, :, 0:N // 2], xT_d[:, :, 0:N // 2]).then_inc(s["x_in0"], 16)
            sp.dma_start(qkv_raw[0][:, :], w_attn_d[0, :, 0:QKV]).then_inc(s["w_in0"], 16)
            sp.dma_start(xT_raw[:, :, N // 2:N], xT_d[:, :, N // 2:N]).then_inc(s["x_in1"], 16)
            sp.dma_start(wo_raw[0][:, :], w_attn_d[0, :, QKV:]).then_inc(s["wo_in0"], 16)
            sp.dma_start(acc[:, :, :], x_d).then_inc(s["acc_in"], 16)
            sp.dma_start(qkv_raw[1][:, :], w_attn_d[1, :, 0:QKV]).then_inc(s["w_in1"], 16)
            sp.dma_start(wo_raw[1][:, :], w_attn_d[1, :, QKV:]).then_inc(s["wo_in1"], 16)
            sp.dma_start(ctxT[:, :, :], ctxT_d).then_inc(s["misc_in"], 16)
            sp.dma_start(w_x[:, :, :, :], w_x_d).then_inc(s["misc_in"], 16)
            for n, row in enumerate((qb_d, kb_d, vb_d, ob_d, nq_d, nk_d)):
                sp.dma_start(rows_bc[:, n, :], row.partition_broadcast(P)).then_inc(s["misc_in"], 16)
            for q in range(2, PAIRS):
                if q == 2:
                    sp.wait_ge(s["w0_split"], 1)
                else:
                    sp.wait_ge(s["w_split"], q - 2)
                sp.dma_start(qkv_raw[q % 2][:, :], w_attn_d[q, :, 0:QKV]).then_inc(s[f"w_in{q % 2}"], 16)
                sp.wait_ge(s["wo_split"], q - 1)
                sp.dma_start(wo_raw[q % 2][:, :], w_attn_d[q, :, QKV:]).then_inc(s[f"wo_in{q % 2}"], 16)
            sp.wait_ge(s["xo_added"], TT)
            sp.dma_start(gate_w[:, :, :], gate_w_d).then_inc(s["g_in"], 16)
            sp.dma_start(gate_b[:, :], gate_b_d.partition_broadcast(P)).then_inc(s["g_in"], 16)
            for e in range(E):
                if e >= 2:
                    sp.wait_ge(s["y_done"], TT * (e - 1))
                    sp.wait_ge(s["y_sum"], TT * (e - 1))
                    sp.wait_ge(s["h_gelu"], 2 * FC * (e - 1))
                d = s[f"w1_in{e % 2}"]
                sp.dma_start(w1[e % 2][:, :, :], w1_d[e]).then_inc(d, 16)
                sp.dma_start(w2[e % 2][:, :, :], w2_d[e]).then_inc(d, 16)
                sp.dma_start(b1[e % 2][:, :], b1_d[:, e, :]).then_inc(d, 16)
                sp.dma_start(b2[e % 2][:, :], b2_d[e].partition_broadcast(P)).then_inc(d, 16)
            for t in range(TT):
                sp.wait_ge(s["out_ready"], t + 1)
                sp.dma_start(out_d[:, t, :], acc[:, t, :]).then_inc(s["out_written"], 16)
            sp.wait_ge(s["out_written"], 16 * TT)

        @block.gpsimd
        def _(pool):
            nc.gpsimd.memset(ident[:, :], 0.0).then_inc(s["ident_zeroed"], 1)
            nc.gpsimd.memset(mask[:, :], 0.0).then_inc(s["ident_zeroed"], 1)
            pool.wait_ge(s["ident_zeroed"], 2)
            nc.gpsimd.affine_select(out=ident[:, :], in_=ident[:, :], compare_op=ALU.not_equal, fill=1.0,
                                    base=0, pattern=[[-1, P]], channel_multiplier=1).then_inc(s["ident_ready"], 1)
            for at in (0, 256):
                nc.gpsimd.affine_select(out=mask[:, at:at + P], in_=mask[:, at:at + P], compare_op=ALU.is_ge,
                                        fill=MASKED, base=0, pattern=[[-1, P]],
                                        channel_multiplier=1).then_inc(s["mask_ready"], 1)

            def split_wo(q):
                pool.wait_ge(s[f"wo_in{q % 2}"], 16 * (q // 2 + 1))
                if q >= 2:
                    pool.wait_ge(s["o_done"], 8 * (q - 1))
                nc.gpsimd.tensor_copy(wo_hi[q % 2][:, :], wo_raw[q % 2][:, :]).then_inc(s["wo_hi"], 1)
                pool.wait_ge(s["wo_hi"], q + 1)
                nc.gpsimd.tensor_tensor(wo_lo[q % 2][:, :], wo_raw[q % 2][:, :], wo_hi[q % 2][:, :].bitcast(f32),
                                        ALU.subtract).then_inc(s["wo_split"], 1)

            for q in range(1, PAIRS):
                pool.wait_ge(s[f"w_in{q % 2}"], 16 * (q // 2 + 1))
                if q >= 2:
                    pool.wait_ge(s["qk_done"], 8 * q - 8)
                    pool.wait_ge(s["v_done"], 8 * (q - 1))
                nc.gpsimd.tensor_copy(qkv_hi[q % 2][:, :], qkv_raw[q % 2][:, :]).then_inc(s["w_hi"], 1)
                pool.wait_ge(s["w_hi"], q)
                nc.gpsimd.tensor_tensor(qkv_lo[q % 2][:, :], qkv_raw[q % 2][:, :], qkv_hi[q % 2][:, :].bitcast(f32),
                                        ALU.subtract).then_inc(s["w_split"], 1)
                split_wo(q - 1)
            split_wo(PAIRS - 1)

            pool.wait_ge(s["o_added"], STEPS)
            pool.wait_ge(s["zlo_ready"], STEPS)
            for i in range(2):
                nc.gpsimd.memset(Vd[i][:, :, :, :], 0.0).then_inc(s["zero_ready"], 1)
            pool.wait_ge(s["zero_ready"], 2)
            for b in range(B):
                if b >= 2:
                    pool.wait_ge(s["xpv_done"], XH * (b - 1))
                pool.wait_ge(s["v_ready"], 2 * b + 2)
                for kc in range(2):
                    for u in range(2):
                        blocks = Vd[b % 2][:, kc, 8 * u:8 * u + 8, :].rearrange("p h n -> p (h n)")
                        diag = bass.AP(blocks.tensor, blocks.offset, [blocks.ap[0], [P + XD, 8], [1, XD]])
                        src = v_tok[:, 2 * b + kc, u * P:(u + 1) * P].rearrange("p (h d) -> p h d", h=8)
                        nc.gpsimd.tensor_copy(diag, src).then_inc(s["vd_ready"], 1)

        @block.tensor
        def _(pe):
            mm = nc.tensor.matmul

            def three(out, lh, ll, rh, rl, start, stop):
                mm(out, lh, rh, start=start, stop=False)
                mm(out, lh, rl, start=False, stop=False)
                return mm(out, ll, rh, start=False, stop=stop)

            def qk_unit(n):
                h, u = n // 4, n % 4
                hh, q, half = h % 2, h // 2, u // 2
                w_at = wq_at if u % 2 == 0 else wk_at
                if hh == 0 and u == 0 and q >= 1:
                    pe.wait_ge(s["w_split"], q)
                if n >= 2:
                    pe.wait_ge(s["qk_evac"], n - 1)
                cols = slice(half * 512, half * 512 + 512)
                for c in range(DC):
                    a = w_at(hh, c)
                    last = three(ps_qk[n % 2][:, :], qkv_hi[q % 2][:, a:a + P], qkv_lo[q % 2][:, a:a + P],
                                 xT_hi[:, c, cols], xT_lo[:, c, cols], c == 0, c == DC - 1)
                last.then_inc(s["qk_done"], 1)

            def v_unit(m):
                q, t = m // TT, m % TT
                if t == 0 and q >= 1:
                    pe.wait_ge(s["w_split"], q)
                if m >= 1:
                    pe.wait_ge(s["v_evac"], m)
                for c in range(DC):
                    a = wv_at(c)
                    last = three(ps_v[:, 0:D], xT_hi[:, c, t * P:(t + 1) * P],
                                 xT_lo[:, c, t * P:(t + 1) * P], qkv_hi[q % 2][:, a:a + 256],
                                 qkv_lo[q % 2][:, a:a + 256], c == 0, c == DC - 1)
                last.then_inc(s["v_done"], 1)

            def scores(i):
                h, b = i // B, i % B
                pe.wait_ge(s["qk_evac"], 4 * h + 2 * (b // 2) + 2)
                if i >= 2:
                    pe.wait_ge(s["s_masked"], i - 1)
                ps = ps_s[i % 2]
                at = b * S
                q_, k_ = QT[h % 2], KT[h % 2]
                mm(ps[:, 0:P], q_[:, at:at + P], k_[:, at:at + P], start=True, stop=True)
                mm(ps[:, P:P + S], q_[:, at + P:at + S], k_[:, at:at + S], start=True, stop=True)\
                    .then_inc(s["s_done"], 1)

            def transposes(i):
                pe.wait_ge(s["p_norm"], i + 1)
                if i >= 1:
                    pe.wait_ge(s["pt_evac"], i)
                for k in range(3):
                    last = nc.tensor.transpose(ps_t[:, k * P:(k + 1) * P], Pr[i % 2][:, k * P:(k + 1) * P], ident[:, :])
                last.then_inc(s["pt_done"], 1)

            def pv(i):
                h, b = i // B, i % B
                q, hh = h // 2, h % 2
                pe.wait_ge(s["v_evac"], TT * q + 2 * b + 2)
                pe.wait_ge(s["pt_evac"], i + 1)
                if i >= 1:
                    pe.wait_ge(s["zlo_ready"], i)
                v_ = V[q % 2]
                mm(ps_z[:, 0:S], v_[:, 2 * b, hh * DH:(hh + 1) * DH], PT[i % 2][:, 0:S], start=True, stop=False)
                mm(ps_z[:, P:S], v_[:, 2 * b + 1, hh * DH:(hh + 1) * DH], PT[i % 2][:, S:S + P],
                   start=False, stop=True).then_inc(s["pv_done"], 1)

            def o_unit(m):
                q, t = m // TT, m % TT
                if t == 0:
                    pe.wait_ge(s["wo_split"], q + 1)
                pe.wait_ge(s["zlo_ready"], 8 * q + 4 + t // 2 + 1)
                if m >= 1:
                    pe.wait_ge(s["o_added"], m)
                for hh in range(2):
                    last = three(ps_o[:, 0:D], z_hi[q % 2][:, hh, t * P:(t + 1) * P],
                                 z_lo[q % 2][:, hh, t * P:(t + 1) * P], wo_hi[q % 2][:, hh * D:(hh + 1) * D],
                                 wo_lo[q % 2][:, hh * D:(hh + 1) * D], hh == 0, hh == 1)
                last.then_inc(s["o_done"], 1)

            pe.wait_ge(s["x_split"], 4)
            pe.wait_ge(s["w0_split"], 1)
            for n in range(4):
                qk_unit(n)
            for m in range(TT):
                v_unit(m)
            pe.wait_ge(s["ident_ready"], 1)
            for i in range(STEPS):
                if i + 4 < 4 * H:
                    qk_unit(i + 4)
                scores(i)
                if i >= 1:
                    transposes(i - 1)
                if i + 8 < TT * PAIRS:
                    v_unit(i + 8)
                if i >= 8:
                    o_unit(i - 8)
                if i >= 1:
                    pv(i - 1)
            transposes(STEPS - 1)
            def kv_unit(m):
                t = m // 2
                if m >= 2:
                    pe.wait_ge(s["k_ready"], (m - 1) // 2 if m % 2 else m // 2)
                    pe.wait_ge(s["v_ready"], (m - 1) // 2)
                for c in range(DC):
                    last = mm(ps_qk[m % 2][:, 0:D], ctxT[:, c, t * P:(t + 1) * P], w_x[:, 1 + m % 2, c, :],
                              start=c == 0, stop=c == DC - 1)
                last.then_inc(s["kv_done"], 1)

            pv(STEPS - 1)
            for t in range(TT):
                o_unit(8 * (PAIRS - 1) + t)
            pe.wait_ge(s["misc_in"], 16 * 8)
            pe.wait_ge(s["qk_evac"], 4 * H)
            for m in range(2 * TT):
                kv_unit(m)

            def xt_unit(t, ready, done, evac):
                pe.wait_ge(ready, t + 1)
                if t >= 2:
                    pe.wait_ge(evac, t - 1)
                for c in range(DC):
                    last = nc.tensor.transpose(ps_s[t % 2][:, c * P:(c + 1) * P], acc[:, t, c * P:(c + 1) * P],
                                               ident[:, :])
                last.then_inc(done, 1)

            def q_unit(t):
                pe.wait_ge(s["xt_evac"], t + 1)
                if t >= 1:
                    pe.wait_ge(s["q_ready"], t)
                for c in range(DC):
                    last = mm(ps_v[:, 0:D], xT1[:, c, t * P:(t + 1) * P], w_x[:, 0, c, :],
                              start=c == 0, stop=c == DC - 1)
                last.then_inc(s["q_done"], 1)

            for t in range(TT):
                xt_unit(t, s["x1_ready"], s["xt_done"], s["xt_evac"])
                if t >= 1:
                    q_unit(t - 1)
            q_unit(TT - 1)

            def stack_unit(p):
                pe.wait_ge(s["stack_ready"], p + 1)
                if p >= 1:
                    pe.wait_ge(s["stk_evac_act"], p)
                    pe.wait_ge(s["stk_evac_dve"], p)
                for hp in range(XH // 2):
                    last = nc.tensor.transpose(bank[6 + hp // 4][:, (hp % 4) * P:(hp % 4 + 1) * P],
                                               stack[p % 2][:, 2 * hp:2 * hp + 2, :].rearrange("p a n -> p (a n)").bitcast(f32),
                                               ident[:, :])
                last.then_inc(s["stk_done"], 1)

            def x_scores(j):
                b, h = j // XH, j % XH
                if h == 0:
                    pe.wait_ge(s["stk_evac_act"], 4 * b + 4)
                    pe.wait_ge(s["stk_evac_dve"], 4 * b + 4)
                if j >= 2:
                    pe.wait_ge(s["xmax_ready"], j - 1)
                    pe.wait_ge(s["xexp_done"], j - 1)
                q_ = (QA, QB)[h % 2][b % 2]
                for qt in range(2):
                    last = mm(ps_s[j % 2][:, qt * S:(qt + 1) * S], q_[:, h // 2, qt * P:(qt + 1) * P],
                              XK[b % 2][:, h // 2, :], start=True, stop=True)
                last.then_inc(s["xs_done"], 1)

            def x_transposes(j):
                pe.wait_ge(s["xp_norm"], j + 1)
                if j >= 2:
                    pe.wait_ge(s["xpt_evac"], j - 1)
                for kc in range(2):
                    for qt in range(2):
                        last = nc.tensor.transpose(ps_qk[j % 2][:, kc * S + qt * P:kc * S + (qt + 1) * P],
                                                   xP[j % 2][:, qt, kc * P:(kc + 1) * P], ident[:, :])
                last.then_inc(s["xpt_done"], 1)

            def x_pv(j):
                b, h = j // XH, j % XH
                if h == 0:
                    pe.wait_ge(s["vd_ready"], 4 * b + 4)
                pe.wait_ge(s["xpt_evac"], j + 1)
                g = j // 8
                if h % 8 == 0 and g >= 2:
                    pe.wait_ge(s["xz_evac"], g - 1)
                for kc in range(2):
                    last = mm(bank[4 + g % 2][:, 0:S], Vd[b % 2][:, kc, h, :], xPT[j % 2][:, kc, :],
                              start=h % 8 == 0 and kc == 0, stop=h % 8 == 7 and kc == 1)
                last.then_inc(s["xpv_done"], 1)

            def xo_unit(t):
                b = t // 2
                pe.wait_ge(s["xz_evac"], 2 * b + 2)
                pe.wait_ge(s["stk_evac_act"], min(4 * b + 8, 4 * B))
                pe.wait_ge(s["stk_evac_dve"], min(4 * b + 8, 4 * B))
                for c in range(DC):
                    last = mm(bank[6 + t % 2][:, 0:D], xz[b % 2][:, c, (t % 2) * P:(t % 2 + 1) * P], w_x[:, 3, c, :],
                              start=c == 0, stop=c == DC - 1)
                last.then_inc(s["xo_done"], 1)

            for p in range(4):
                stack_unit(p)
            for j in range(ITEMS):
                b, h = j // XH, j % XH
                x_scores(j)
                if j >= 1:
                    x_transposes(j - 1)
                if b + 1 < B and h % 4 == 2:
                    if h == 2 and b >= 1:
                        pe.wait_ge(s["xo_added"], 2 * b)
                    stack_unit(4 * (b + 1) + h // 4)
                if j >= 2:
                    x_pv(j - 2)
                if b >= 1 and h == 1:
                    xo_unit(2 * b - 2)
                    xo_unit(2 * b - 1)
            x_transposes(ITEMS - 1)
            x_pv(ITEMS - 2)
            x_pv(ITEMS - 1)
            xo_unit(TT - 2)
            xo_unit(TT - 1)

            for t in range(TT):
                xt_unit(t, s["x2_ready"], s["x2t_done"], s["x2t_evac"])
                if t == 0:
                    pe.wait_ge(s["g_in"], 32)
            for t in range(TT):
                pe.wait_ge(s["x2t_evac"], t + 1)
                for c in range(DC):
                    last = mm(ps_t[:, t * E:(t + 1) * E], xT1[:, c, t * P:(t + 1) * P], gate_w[:, c, :],
                              start=c == 0, stop=c == DC - 1)
            last.then_inc(s["g_done"], 1)

            def h_unit(u):
                e, half, fc = u // (2 * FC), u // FC % 2, u % FC
                if half == 0 and fc == 0:
                    pe.wait_ge(s[f"w1_in{e % 2}"], 64 * (e // 2 + 1))
                if u >= 2:
                    pe.wait_ge(s["h_gelu"], u - 1)
                for c in range(DC):
                    last = mm(ps_qk[u % 2][:, :], w1[e % 2][:, c, fc * P:(fc + 1) * P],
                              xT1[:, c, half * 512:(half + 1) * 512], start=c == 0, stop=c == DC - 1)
                last.then_inc(s["h_done"], 1)

            def y_unit(v):
                e, t = v // TT, v % TT
                half = t // 4
                pe.wait_ge(s["h_gelu"], 2 * FC * e + FC * (half + 1))
                if v >= 2:
                    pe.wait_ge(s["y_sum"], v - 1)
                for fc in range(FC):
                    last = mm(ps_s[v % 2][:, 0:D], hT[half][:, fc, (t % 4) * P:(t % 4 + 1) * P], w2[e % 2][:, fc, :],
                              start=fc == 0, stop=fc == FC - 1)
                last.then_inc(s["y_done"], 1)

            for e in range(E):
                for u in range(FC):
                    h_unit(2 * FC * e + u)
                if e >= 1:
                    for t in range(4, 8):
                        y_unit(TT * (e - 1) + t)
                for u in range(FC, 2 * FC):
                    h_unit(2 * FC * e + u)
                for t in range(4):
                    y_unit(TT * e + t)
            for t in range(4, 8):
                y_unit(TT * (E - 1) + t)

        @block.scalar
        def _(act):
            A = nc.scalar.activation

            def qk_evac(n):
                h, u = n // 4, n % 4
                half = u // 2
                dst = (QT if u % 2 == 0 else KT)[h % 2][:, half * 512:(half + 1) * 512]
                act.wait_ge(s["qk_done"], n + 1)
                A(dst, ps_qk[n % 2][:, :], ACT.Copy, scale=1.0 if u % 2 == 0 else -SCALE).then_inc(s["qk_evac"], 1)

            def v_evac(m):
                act.wait_ge(s["v_done"], m + 1)
                A(V[m // TT % 2][:, m % TT, :], ps_v[:, 0:D], ACT.Copy).then_inc(s["v_evac"], 1)

            def z_high(i):
                h, b = i // B, i % B
                act.wait_ge(s["pv_done"], i + 1)
                A(z_hi[h // 2 % 2][:, h % 2, b * S:(b + 1) * S], ps_z[:, 0:S],
                  ACT.Copy).then_inc(s["zhi_ready"], 1)

            def exps(i):
                act.wait_ge(s["s_masked"], i + 1)
                if i >= 2:
                    act.wait_ge(s["pt_done"], i - 1)
                A(Pr[i % 2][:, 0:P], Sm[i % 2][:, 0:P], ACT.Exp, bias=nmax[i % 2][:, 0:1], scale=-1.0,
                  accum_out=rsum[i % 2][:, 0:1])
                A(Pr[i % 2][:, P:384], Sm[i % 2][:, P:384], ACT.Exp, bias=nmax[i % 2][:, 1:2], scale=-1.0,
                  accum_out=rsum[i % 2][:, 1:2]).then_inc(s["exp_done"], 1)

            for n in range(4):
                qk_evac(n)
            for m in range(TT):
                v_evac(m)
            for i in range(STEPS):
                if i + 4 < 4 * H:
                    qk_evac(i + 4)
                if i >= 1 and i + 7 < TT * PAIRS:
                    v_evac(i + 7)
                if i >= 2:
                    z_high(i - 2)
                exps(i)
            for i in (STEPS - 2, STEPS - 1):
                z_high(i)

            act.wait_ge(s["ln_mv"], TT)
            act.wait_ge(s["eps_ready"], 2)
            A(sd[:, :], mv[:, :, 1], ACT.Sqrt, bias=eps_ln[:, 0:1]).then_inc(s["ln_sd"], 1)
            for t in range(TT):
                act.wait_ge(s["xt_done"], t + 1)
                A(xT1[:, :, t * P:(t + 1) * P], ps_s[t % 2][:, 0:D].rearrange("p (c n) -> p c n", c=DC),
                  ACT.Copy).then_inc(s["xt_evac"], 1)
            act.wait_ge(s["kq_ss"], 2 * TT)
            A(krs[:, :], kss[:, :], ACT.Sqrt, bias=eps_rms[:, 0:1], scale=1.0 / D)
            A(qrs[:, :], qss[:, :], ACT.Sqrt, bias=eps_rms[:, 0:1], scale=1.0 / D).then_inc(s["rms_sd"], 1)

            def stack_evac(p):
                b, k, j = p // 4, p // 2 % 2, p % 2
                cols = slice(j * P, (j + 1) * P)
                act.wait_ge(s["stk_done"], p + 1)
                if k == 0:
                    if p < 2:
                        act.wait_ge(s["zero2"], 2)
                    for q in range(2):
                        last = A(QA[b % 2][0:64, 4 * q:4 * q + 4, cols],
                                 bank[6 + q][0:64, :].rearrange("p (a n) -> p a n", a=4), ACT.Copy)
                else:
                    last = A(XK[b % 2][:, 0:4, cols], bank[6][:, :].rearrange("p (a n) -> p a n", a=4), ACT.Copy)
                last.then_inc(s["stk_evac_act"], 1)

            def x_exps(j):
                act.wait_ge(s["xmax_ready"], j + 1)
                if j >= 2:
                    act.wait_ge(s["xpt_done"], j - 1)
                for qt in range(2):
                    last = A(xP[j % 2][:, qt, :], ps_s[j % 2][:, qt * S:(qt + 1) * S], ACT.Exp,
                             bias=xnmax[j % 2][:, qt:qt + 1], accum_out=xrsum[j % 2][:, qt:qt + 1])
                last.then_inc(s["xexp_done"], 1)

            def xpt_evac(j):
                act.wait_ge(s["xpt_done"], j + 1)
                if j >= 2:
                    act.wait_ge(s["xpv_done"], j - 1)
                A(xPT[j % 2][:, :, :], ps_qk[j % 2][:, :].rearrange("p (a n) -> p a n", a=2), ACT.Copy)\
                    .then_inc(s["xpt_evac"], 1)

            def xz_evac(g):
                b = g // 2
                act.wait_ge(s["xpv_done"], 8 * (g + 1))
                if b >= 2:
                    act.wait_ge(s["xo_done"], 2 * (b - 1))
                A(xz[b % 2][:, g % 2, :], bank[4 + g % 2][:, 0:S], ACT.Copy).then_inc(s["xz_evac"], 1)

            for p in range(4):
                stack_evac(p)
            for j in range(ITEMS):
                b, h = j // XH, j % XH
                if j >= 1:
                    xpt_evac(j - 1)
                x_exps(j)
                if b + 1 < B and h % 4 == 2:
                    stack_evac(4 * (b + 1) + h // 4)
                if j >= 9 and (j - 2) % 8 == 7:
                    xz_evac((j - 9) // 8)
            xpt_evac(ITEMS - 1)
            xz_evac(2 * B - 1)
            act.wait_ge(s["ln2_chain"], 1)
            A(sd[:, :], mv[:, :, 1], ACT.Sqrt, bias=eps_ln[:, 0:1]).then_inc(s["ln2_sd"], 1)
            for t in range(TT):
                act.wait_ge(s["x2t_done"], t + 1)
                A(xT1[:, :, t * P:(t + 1) * P], ps_s[t % 2][:, 0:D].rearrange("p (c n) -> p c n", c=DC),
                  ACT.Copy).then_inc(s["x2t_evac"], 1)
            act.wait_ge(s["r_chain"], 3)
            A(probs[:, :, :], logits[:, :, :], ACT.Exp).then_inc(s["gexp_done"], 1)
            for u in range(2 * FC * E):
                e, half, fc = u // (2 * FC), u // FC % 2, u % FC
                act.wait_ge(s["h_done"], u + 1)
                if fc == 0:
                    if e >= 1:
                        act.wait_ge(s["y_done"], TT * (e - 1) + 4 * (half + 1))
                    act.wait_ge(s[f"w1_in{e % 2}"], 64 * (e // 2 + 1))
                A(hT[half][:, fc, :], ps_qk[u % 2][:, :], ACT.Gelu_apprx_tanh, bias=b1[e % 2][:, fc:fc + 1])\
                    .then_inc(s["h_gelu"], 1)
            act.wait_ge(s["ln3_chain"], 1)
            A(sd[:, :], mv[:, :, 1], ACT.Sqrt, bias=eps_ln[:, 0:1]).then_inc(s["ln3_sd"], 1)

        @block.vector
        def _(dve):
            v = nc.vector
            chain_count = [0]

            def chained(ins):
                chain_count[0] += 1
                ins.then_inc(s["chain"], 1)
                dve.wait_ge(s["chain"], chain_count[0])

            def split_x(half):
                cols = slice(half * 512, (half + 1) * 512)
                dve.wait_ge(s[f"x_in{half}"], 16)
                for c in range(DC):
                    chained(v.tensor_copy(xT_hi[:, c, cols], xT_raw[:, c, cols]))
                    v.tensor_tensor(xT_lo[:, c, cols], xT_raw[:, c, cols], xT_hi[:, c, cols].bitcast(f32),
                                    ALU.subtract).then_inc(s["x_split"], 1)

            def mask_max(i):
                dve.wait_ge(s["s_done"], i + 1)
                if i >= 2:
                    dve.wait_ge(s["exp_done"], i - 1)
                for a, z in ((0, P), (P, 384)):
                    last = v.tensor_tensor_reduce(out=Sm[i % 2][:, a:z], in0=ps_s[i % 2][:, a:z], in1=mask[:, a:z],
                                                  scale=1.0, scalar=BIG, op0=ALU.add, op1=ALU.min,
                                                  accum_out=nmax[i % 2][:, (a > 0):(a > 0) + 1])
                last.then_inc(s["s_masked"], 1)

            def pt_evac(i):
                dve.wait_ge(s["pt_done"], i + 1)
                if i >= 2:
                    dve.wait_ge(s["pv_done"], i - 1)
                v.tensor_copy(PT[i % 2][:, :], ps_t[:, 0:384]).then_inc(s["pt_evac"], 1)

            def o_add(m):
                t = m % TT
                dve.wait_ge(s["o_done"], m + 1)
                if m >= TT:
                    dve.wait_ge(s["o_added"], m - TT + 1)
                v.tensor_tensor(acc[:, t, :], acc[:, t, :], ps_o[:, 0:D], ALU.add)\
                    .then_inc(s["o_added"], 1)

            def z_low(i):
                h, b = i // B, i % B
                dve.wait_ge(s["zhi_ready"], i + 1)
                at = (h // 2 % 2, h % 2, slice(b * S, (b + 1) * S))
                v.tensor_tensor(z_lo[at[0]][:, at[1], at[2]], ps_z[:, 0:S],
                                z_hi[at[0]][:, at[1], at[2]].bitcast(f32), ALU.subtract).then_inc(s["zlo_ready"], 1)

            def normalise(i):
                dve.wait_ge(s["exp_done"], i + 1)
                v.reciprocal(rinv[i % 2][:, :], rsum[i % 2][:, :]).then_inc(s["rinv_ready"], 1)
                dve.wait_ge(s["rinv_ready"], i + 1)
                v.tensor_scalar(Pr[i % 2][:, 0:P], Pr[i % 2][:, 0:P], rinv[i % 2][:, 0:1], None, ALU.mult)
                v.tensor_scalar(Pr[i % 2][:, P:384], Pr[i % 2][:, P:384], rinv[i % 2][:, 1:2], None, ALU.mult)\
                    .then_inc(s["p_norm"], 1)

            v.memset(eps_ln[:, :], LN_EPS).then_inc(s["eps_ready"], 1)
            v.memset(eps_rms[:, :], RMS_EPS).then_inc(s["eps_ready"], 1)
            split_x(0)
            dve.wait_ge(s["w_in0"], 16)
            chained(v.tensor_copy(qkv_hi[0][:, :], qkv_raw[0][:, :]))
            v.tensor_tensor(qkv_lo[0][:, :], qkv_raw[0][:, :], qkv_hi[0][:, :].bitcast(f32), ALU.subtract)\
                .then_inc(s["w0_split"], 1)
            split_x(1)
            dve.wait_ge(s["mask_ready"], 2)
            dve.wait_ge(s["acc_in"], 16)
            for i in range(STEPS):
                mask_max(i)
                if i >= 1:
                    pt_evac(i - 1)
                if i >= 9:
                    o_add(i - 9)
                if i >= 2:
                    z_low(i - 2)
                normalise(i)
            pt_evac(STEPS - 1)
            o_add(STEPS - 9)
            z_low(STEPS - 2)
            z_low(STEPS - 1)
            for m in range(STEPS - 8, STEPS):
                o_add(m)

            def norm_stats():
                for t in range(TT):
                    last = v.bn_stats(stats[:, t, :], acc[:, t, :])
                chained(last)
                for t in range(TT):
                    last = v.bn_aggr(mv[:, t, :], stats[:, t, :])
                return last

            def norm_apply(ready):
                for t in range(TT):
                    v.tensor_scalar(acc[:, t, :], acc[:, t, :], mv[:, t, 0:1], rstd[:, t:t + 1],
                                    ALU.subtract, ALU.mult).then_inc(ready, 1)

            dve.wait_ge(s["o_added"], STEPS)
            norm_stats().then_inc(s["ln_mv"], TT)
            dve.wait_ge(s["ln_sd"], 1)
            chained(v.reciprocal(rstd[:, :], sd[:, :]))
            norm_apply(s["x1_ready"])
            for t in range(TT):
                dve.wait_ge(s["kv_done"], 2 * t + 1)
                if t == 0:
                    dve.wait_ge(s["misc_in"], 16 * 8)
                v.tensor_tensor(k_tok[:, t, :], ps_qk[0][:, 0:D], rows_bc[:, 1, :], ALU.add).then_inc(s["k_ready"], 1)
                dve.wait_ge(s["kv_done"], 2 * t + 2)
                v.tensor_tensor(v_tok[:, t, :], ps_qk[1][:, 0:D], rows_bc[:, 2, :], ALU.add).then_inc(s["v_ready"], 1)
                dve.wait_ge(s["k_ready"], t + 1)
                v.tensor_tensor_reduce(out=sq_junk[:, :], in0=k_tok[:, t, :], in1=k_tok[:, t, :], scale=1.0,
                                       scalar=0.0, op0=ALU.mult, op1=ALU.add, accum_out=kss[:, t:t + 1])\
                    .then_inc(s["kq_ss"], 1)
            for t in range(TT):
                dve.wait_ge(s["q_done"], t + 1)
                v.tensor_tensor(q_tok[:, t, :], ps_v[:, 0:D], rows_bc[:, 0, :], ALU.add).then_inc(s["q_ready"], 1)
                dve.wait_ge(s["q_ready"], t + 1)
                dve.wait_ge(s["kq_ss"], TT + t)
                v.tensor_tensor_reduce(out=sq_junk[:, :], in0=q_tok[:, t, :], in1=q_tok[:, t, :], scale=1.0,
                                       scalar=0.0, op0=ALU.mult, op1=ALU.add, accum_out=qss[:, t:t + 1])\
                    .then_inc(s["kq_ss"], 1)
            for i in range(2):
                v.memset(QA[i][64:128, :, :].bitcast(u32), 0).then_inc(s["zero2"], 1)
            for i in range(2):
                v.memset(QB[i][0:64, :, :].bitcast(u32), 0)
            dve.wait_ge(s["rms_sd"], 1)
            v.reciprocal(krs[:, :], krs[:, :])
            chained(v.reciprocal(qrs[:, :], qrs[:, :]))
            chained(v.tensor_scalar(qrs[:, :], qrs[:, :], XSCALE, None, ALU.mult))
            dve.wait_ge(s["xt_done"], TT)
            for t in range(TT):
                v.tensor_tensor(acc[:, t, :], acc[:, t, :], rows_bc[:, 3, :], ALU.add).then_inc(s["x1b_ready"], 1)

            def make_stack(p):
                b, k, j = p // 4, p // 2 % 2, p % 2
                t = 2 * b + j
                src, r = (q_tok, qrs) if k == 0 else (k_tok, krs)
                chained(v.scalar_tensor_tensor(out=qn[:, :], in0=src[:, t, :], scalar=r[:, t:t + 1],
                                               in1=rows_bc[:, 4 + k, :], op0=ALU.mult, op1=ALU.mult))
                if p >= 2:
                    dve.wait_ge(s["stk_done"], p - 1)
                parts = stack[p % 2][:, :, :]
                if k == 0:
                    hi, lo = parts[:, :, 0:2 * XD], parts[:, :, 2 * XD:4 * XD]
                    hi = hi.rearrange("p h (a d) -> p h a d", a=2)
                    lo = lo.rearrange("p h (a d) -> p h a d", a=2)
                else:
                    four = parts.rearrange("p h (a c d) -> p h a c d", a=2, c=2)
                    hi, lo = four[:, :, :, 0, :], four[:, :, :, 1, :]
                whole = qn[:, :].rearrange("p (h d) -> p h d", h=XH).unsqueeze(2).to_broadcast([P, XH, 2, XD])
                chained(v.tensor_copy(hi, whole))
                v.tensor_tensor(lo, whole, hi.bitcast(f32), ALU.subtract).then_inc(s["stack_ready"], 1)

            def stack_evac(p):
                b, k, j = p // 4, p // 2 % 2, p % 2
                cols = slice(j * P, (j + 1) * P)
                dve.wait_ge(s["stk_done"], p + 1)
                if k == 0:
                    for q in range(2):
                        last = v.tensor_copy(QB[b % 2][64:128, 4 * q:4 * q + 4, cols],
                                             bank[6 + q][64:128, :].rearrange("p (a n) -> p a n", a=4))
                else:
                    last = v.tensor_copy(XK[b % 2][:, 4:8, cols], bank[7][:, :].rearrange("p (a n) -> p a n", a=4))
                last.then_inc(s["stk_evac_dve"], 1)

            def x_max(j):
                dve.wait_ge(s["xs_done"], j + 1)
                v.tensor_reduce(xnmax[j % 2][:, :], ps_s[j % 2][:, :].rearrange("p (a n) -> p a n", a=2), AX.X,
                                ALU.max, negate=True).then_inc(s["xmax_ready"], 1)

            def x_normalise(j):
                dve.wait_ge(s["xexp_done"], j + 1)
                v.reciprocal(xrinv[j % 2][:, :], xrsum[j % 2][:, :]).then_inc(s["xrinv_ready"], 1)
                dve.wait_ge(s["xrinv_ready"], j + 1)
                for qt in range(2):
                    last = v.tensor_scalar(xP[j % 2][:, qt, :], xP[j % 2][:, qt, :], xrinv[j % 2][:, qt:qt + 1], None,
                                           ALU.mult)
                last.then_inc(s["xp_norm"], 1)

            def xo_add(t):
                dve.wait_ge(s["xo_done"], t + 1)
                dve.wait_ge(s["x1b_ready"], TT)
                v.tensor_tensor(acc[:, t, :], acc[:, t, :], bank[6 + t % 2][:, 0:D], ALU.add).then_inc(s["xo_added"], 1)

            for p in range(4):
                make_stack(p)
                stack_evac(p)
            for j in range(ITEMS):
                b, h = j // XH, j % XH
                x_max(j)
                if b + 1 < B and h % 4 == 0:
                    make_stack(4 * (b + 1) + h // 4)
                if b + 1 < B and h % 4 == 3:
                    stack_evac(4 * (b + 1) + h // 4)
                if b >= 1 and h == 2:
                    xo_add(2 * b - 2)
                    xo_add(2 * b - 1)
                x_normalise(j)
            xo_add(TT - 2)
            xo_add(TT - 1)

            dve.wait_ge(s["xo_added"], TT)
            norm_stats().then_inc(s["ln2_chain"], 1)
            dve.wait_ge(s["ln2_sd"], 1)
            chained(v.reciprocal(rstd[:, :], sd[:, :]))
            norm_apply(s["x2_ready"])
            dve.wait_ge(s["x2_ready"], TT)
            dve.wait_ge(s["g_done"], 1)
            dve.wait_ge(s["g_in"], 32)
            bc8 = gate_b[:, :].unsqueeze(1).to_broadcast([P, TT, E])
            chained(v.tensor_tensor(logits[:, :, :], ps_t[:, 0:TT * E].rearrange("p (t e) -> p t e", t=TT), bc8, ALU.add))
            chained(v.tensor_reduce(lmax[:, :], logits[:, :, :], AX.X, ALU.max))
            for e in range(E):
                last = v.memset(iota_e[:, e:e + 1], float(e))
            last.then_inc(s["r_chain"], 2)
            v.tensor_tensor(logits[:, :, :], logits[:, :, :], lmax[:, :].unsqueeze(2).to_broadcast([P, TT, E]),
                            ALU.subtract).then_inc(s["r_chain"], 1)
            dve.wait_ge(s["gexp_done"], 1)
            chained(v.tensor_reduce(psum_[:, :], probs[:, :, :], AX.X, ALU.add))
            chained(v.reciprocal(psum_[:, :], psum_[:, :]))
            chained(v.tensor_tensor(probs[:, :, :], probs[:, :, :], psum_[:, :].unsqueeze(2).to_broadcast([P, TT, E]),
                                    ALU.mult))
            for t in range(TT):
                last = v.max(top[:, t, :], probs[:, t, :])
            chained(last)
            for t in range(TT):
                last = v.max_index(top_i[:, t, :], top[:, t, :], probs[:, t, :])
            chained(last)
            v.tensor_copy(top_f[:, :, :], top_i[:, :, 0:2])
            chained(v.tensor_tensor(w12[:, :], top[:, :, 0], top[:, :, 1], ALU.add))
            chained(v.reciprocal(w12[:, :], w12[:, :]))
            chained(v.tensor_tensor(wts[:, :, :], top[:, :, 0:2], w12[:, :].unsqueeze(2).to_broadcast([P, TT, 2]),
                                    ALU.mult))
            for k in range(2):
                dst = comb if k == 0 else oneh
                chained(v.tensor_tensor(dst[:, :, :], iota_e[:, :].unsqueeze(1).to_broadcast([P, TT, E]),
                                        top_f[:, :, k].unsqueeze(2).to_broadcast([P, TT, E]), ALU.is_equal))
                chained(v.tensor_tensor(dst[:, :, :], dst[:, :, :],
                                        wts[:, :, k].unsqueeze(2).to_broadcast([P, TT, E]), ALU.mult))
            chained(v.tensor_tensor(comb[:, :, :], comb[:, :, :], oneh[:, :, :], ALU.add))
            for u in range(TT * E):
                e, t = u // TT, u % TT
                dve.wait_ge(s["y_done"], u + 1)
                dve.wait_ge(s[f"w1_in{e % 2}"], 64 * (e // 2 + 1))
                if u >= 1:
                    dve.wait_ge(s["y_added"], u)
                v.tensor_tensor(ysum[:, :], ps_s[u % 2][:, 0:D], b2[e % 2][:, :], ALU.add).then_inc(s["y_sum"], 1)
                dve.wait_ge(s["y_sum"], u + 1)
                v.scalar_tensor_tensor(out=acc[:, t, :], in0=ysum[:, :], scalar=comb[:, t, e:e + 1],
                                       in1=acc[:, t, :], op0=ALU.mult, op1=ALU.add).then_inc(s["y_added"], 1)
            dve.wait_ge(s["y_added"], TT * E)
            norm_stats().then_inc(s["ln3_chain"], 1)
            dve.wait_ge(s["ln3_sd"], 1)
            chained(v.reciprocal(rstd[:, :], sd[:, :]))
            norm_apply(s["out_ready"])


def kernel(**inputs):
    import numpy as np
    import concourse.bacc as bacc
    from concourse.bass_utils import run_bass_kernel_spmd

    g = {k: np.asarray(a) for k, a in inputs.items()}
    P = 128

    def chunks(a):
        n = a.shape[-2] // P
        b = a.reshape(*a.shape[:-2], n, P, a.shape[-1])
        return np.moveaxis(b, -3, -2)

    x = g["x"].reshape(-1, g["x"].shape[-1])
    c = g["ctx_2048"].reshape(-1, x.shape[1])
    pairs = g["L0_attn_W_Q"].shape[0] // 2

    def per_head(w):
        t = chunks(np.swapaxes(w, 1, 2))
        t = t.reshape(pairs, 2, *t.shape[1:])
        return np.moveaxis(t, 1, 2).reshape(pairs, P, -1)

    wv = chunks(np.swapaxes(g["L0_attn_W_V"], 1, 2))
    wv = wv.reshape(pairs, 2, *wv.shape[1:])
    wv = np.transpose(wv, (0, 2, 3, 1, 4)).reshape(pairs, P, -1)
    wo = np.swapaxes(g["L0_attn_W_O"], 0, 1).reshape(pairs, 2, P, -1)
    wo = np.swapaxes(wo, 1, 2).reshape(pairs, P, -1)
    w_attn = np.concatenate([per_head(g["L0_attn_W_Q"]), per_head(g["L0_attn_W_K"]), wv, wo], axis=-1)
    w_x = np.stack([chunks(np.swapaxes(g["L0_xattn_" + n], 0, 1)) for n in ("q_w", "k_img_w", "v_img_w", "o_w")],
                   axis=1)
    laid = {
        "xT": chunks(np.swapaxes(x, 0, 1)), "x": chunks(x), "w_attn": w_attn,
        "ctxT": chunks(np.swapaxes(c, 0, 1)), "w_x": w_x,
        "q_b": g["L0_xattn_q_b"], "k_b": g["L0_xattn_k_img_b"], "v_b": g["L0_xattn_v_img_b"],
        "o_b": g["L0_xattn_o_b"], "nq": g["L0_xattn_norm_q_w"], "nk": g["L0_xattn_norm_k_img_w"],
        "gate_w": chunks(g["L0_ffn_gate_w"]), "gate_b": g["L0_ffn_gate_b"],
        "w1": chunks(g["L0_ffn_w1"]), "b1": np.moveaxis(g["L0_ffn_b1"].reshape(g["L0_ffn_b1"].shape[0], -1, P), 2, 0),
        "w2": chunks(g["L0_ffn_w2"]), "b2": g["L0_ffn_b2"],
    }
    nc = bacc.Bacc("TRN2", target_bir_lowering=False, num_devices=1)
    arrays, args = {}, []
    for name, a in laid.items():
        a = np.ascontiguousarray(a)
        arrays["in_" + name] = a
        args.append(nc.dram_tensor("in_" + name, a.shape, mybir.dt.from_np(a.dtype), kind="ExternalInput").ap())
    tiles = x.shape[0] // P
    out = nc.dram_tensor("out", (P, tiles, x.shape[1]), mybir.dt.float32, kind="ExternalOutput").ap()
    build_decoder_layer(nc, *args, out)
    r = run_bass_kernel_spmd(nc, [arrays], core_ids=[0])
    y = np.asarray(r.results[0]["out"])
    return np.ascontiguousarray(np.swapaxes(y, 0, 1)).reshape(g["x"].shape)
```

```python
import concourse.bass as bass
from concourse import mybir
from contextlib import ExitStack


def build_decoder_layer(nc, xT_d, x_d, w_attn_d, ctxT_d, w_x_d, qb_d, kb_d, vb_d, ob_d, nq_d, nk_d,
                        gate_w_d, gate_b_d, w1_d, b1_d, w2_d, b2_d, xs_d, ys_d, out_d):
    f32 = mybir.dt.float32
    f32r = mybir.dt.float32r
    bf16 = mybir.dt.bfloat16
    u32 = mybir.dt.uint32
    i32 = mybir.dt.int32
    ALU = mybir.AluOpType
    ACT = mybir.ActivationFunctionType
    AX = mybir.AxisListType

    P = 128
    D = 256
    DC = D // P
    B = x_d.shape[1] // 2
    TT = x_d.shape[1]
    N = TT * P
    S = N // B
    PAIRS = w_attn_d.shape[0]
    H = 2 * PAIRS
    DH = P
    STEPS = H * B
    XH = 16
    XD = D // XH
    ITEMS = XH * B
    E = w1_d.shape[0]
    F = w1_d.shape[3]
    FC = F // P
    SCALE = float(DH) ** -0.5
    XSCALE = float(XD) ** -0.5
    MASKED = 1e10 * SCALE
    LN_EPS = 1e-5
    RMS_EPS = 1e-6
    PART = 512
    BIG = 3.0e38
    CAP = N
    RSQRT_SEED = 1597463007.0

    ctx = ExitStack()
    with ctx:
        def sem(name):
            return ctx.enter_context(nc.semaphore(name))

        def sb(stack, name, shape, dt=f32):
            return stack.enter_context(nc.sbuf_tensor(name, shape, dt))

        acc = sb(ctx, "acc", [P, TT, D])
        ident = sb(ctx, "ident", [P, P])
        stats = sb(ctx, "stats", [P, TT, 6])
        mv = sb(ctx, "mv", [P, TT, 2])
        rstd = sb(ctx, "rstd", [P, TT])
        nt_a = sb(ctx, "nt_a", [P, TT])
        nt_b = sb(ctx, "nt_b", [P, TT])
        sd = sb(ctx, "sd", [P, TT])
        eps_ln = sb(ctx, "eps_ln", [P, 1])
        kss = sb(ctx, "kss", [P, TT])
        qss = sb(ctx, "qss", [P, TT])
        krs = sb(ctx, "krs", [P, TT])
        qrs = sb(ctx, "qrs", [P, TT])
        ctxT = sb(ctx, "ctxT", [P, DC, N])
        w_x = sb(ctx, "w_x", [P, 4, DC, D])
        rows_bc = sb(ctx, "rows_bc", [P, 5, D])
        vb_col = sb(ctx, "vb_col", [P, DC])
        w1 = [sb(ctx, f"w1_{i}", [P, DC, F]) for i in range(2)]
        w2 = [sb(ctx, f"w2_{i}", [P, FC, D]) for i in range(2)]
        b1 = sb(ctx, "b1", [P, E, FC])
        gate_w = sb(ctx, "gate_w", [P, DC, E])
        gate_b = sb(ctx, "gate_b", [P, E])

        logits = sb(ctx, "logits", [P, TT, E])
        lmax = sb(ctx, "lmax", [P, TT])
        probs = sb(ctx, "probs", [P, TT, E])
        top = sb(ctx, "top", [P, TT, 8])
        top_i = sb(ctx, "top_i", [P, TT, 8], u32)
        top_f = sb(ctx, "top_f", [P, TT, 2])
        w12 = sb(ctx, "w12", [P, TT])
        iota_e = sb(ctx, "iota_e", [P, E])
        iota_slot = sb(ctx, "iota_slot", [P, E])
        first = sb(ctx, "first", [P, TT, E])
        second = sb(ctx, "second", [P, TT, E])
        comb = sb(ctx, "comb", [P, TT, E])
        sel = sb(ctx, "sel", [P, TT + 1, E], bf16)
        before = sb(ctx, "before", [P, P], bf16)
        ones_bf = sb(ctx, "ones_bf", [P, P], bf16)
        slot = sb(ctx, "slot", [P, TT, E])
        slot_t = sb(ctx, "slot_t", [P, TT, E])
        slot_lh = sb(ctx, "slot_lh", [P, TT, 2])
        slot_i = sb(ctx, "slot_i", [P, TT, 2], i32)
        w_lh = sb(ctx, "w_lh", [P, TT, 2])
        tiles_i = sb(ctx, "tiles_i", [P, E], i32)
        tiles_f = sb(ctx, "tiles_f", [P, E])
        zeros_e = sb(ctx, "zeros_e", [P, E])
        cum_f = sb(ctx, "cum_f", [P, E])
        cum_i = sb(ctx, "cum_i", [P, E], i32)

        s1 = ExitStack()
        xT_raw = sb(s1, "xT_raw", [P, DC, N])
        xT_hi = sb(s1, "xT_hi", [P, DC, N], f32r)
        xT_lo = sb(s1, "xT_lo", [P, DC, N], f32r)
        w_raw = sb(s1, "w_raw", [P, 4, PART])
        wqk_hi = [sb(s1, f"wqk_hi{i}", [P, PART], f32r) for i in range(2)]
        wqk_lo = [sb(s1, f"wqk_lo{i}", [P, PART], f32r) for i in range(2)]
        wv_hi = sb(s1, "wv_hi", [P, PART], f32r)
        wv_lo = sb(s1, "wv_lo", [P, PART], f32r)
        wo_hi = sb(s1, "wo_hi", [P, PART], f32r)
        wo_lo = sb(s1, "wo_lo", [P, PART], f32r)
        QT = [sb(s1, f"QT{i}", [P, N]) for i in range(2)]
        KT = [sb(s1, f"KT{i}", [P, N]) for i in range(2)]
        V = sb(s1, "V", [P, TT, 2 * DH])
        Sm = [sb(s1, f"Sm{i}", [P, 384]) for i in range(2)]
        Pr = [sb(s1, f"Pr{i}", [P, 384]) for i in range(2)]
        PT = [sb(s1, f"PT{i}", [P, 384]) for i in range(2)]
        nmax = [sb(s1, f"nmax{i}", [P, 2]) for i in range(2)]
        rsum = [sb(s1, f"rsum{i}", [P, 2]) for i in range(2)]
        rinv = [sb(s1, f"rinv{i}", [P, 2]) for i in range(2)]
        z_hi = sb(s1, "z_hi", [P, 2, N], f32r)
        z_lo = sb(s1, "z_lo", [P, 2, N], f32r)
        mask = sb(s1, "mask", [P, 384])
        s1.close()

        s2 = ExitStack()
        QA = [sb(s2, f"QA{i}", [P, XH // 2, S], f32r) for i in range(2)]
        QB = [sb(s2, f"QB{i}", [P, XH // 2, S], f32r) for i in range(2)]
        Vd = [sb(s2, f"Vd{i}", [P, 2, XH, P]) for i in range(2)]
        q_tok = sb(s2, "q_tok", [P, TT, D])
        xP = [sb(s2, f"xP{i}", [P, 2, S]) for i in range(3)]
        xPT = [sb(s2, f"xPT{i}", [P, 2, S]) for i in range(2)]
        xz = [sb(s2, f"xz{i}", [P, DC, S]) for i in range(2)]
        xT1 = sb(s2, "xT1", [P, DC, N])
        XK1 = sb(s2, "XK1", [P, XH // 2, S], f32r)
        XK0 = sb(s2, "XK0", [P, XH // 2, S], f32r)
        XK = [XK0, XK1]
        k_tok = sb(s2, "k_tok", [P, TT, D])
        v_tok = sb(s2, "v_tok", [P, TT, D])
        stack = [sb(s2, f"stack{i}", [P, XH, 4 * XD], f32r) for i in range(2)]
        junk = sb(s2, "junk", [P, D])
        qn = sb(s2, "qn", [P, D])
        xnmax = [sb(s2, f"xnmax{i}", [P, 2]) for i in range(3)]
        xrsum = [sb(s2, f"xrsum{i}", [P, 2]) for i in range(3)]
        xrinv = [sb(s2, f"xrinv{i}", [P, 2]) for i in range(3)]
        s2.close()

        s3 = ExitStack()
        b2 = sb(s3, "b2", [P, E, D])
        xg = sb(s3, "xg", [P, D])
        xgT = sb(s3, "xgT", [P, DC, P])
        hT = sb(s3, "hT", [P, FC, P])
        ys = sb(s3, "ys", [P, D])
        y_lo = sb(s3, "y_lo", [P, TT, D])
        y_hi = sb(s3, "y_hi", [P, TT, D])
        s3.close()

        bank = [ctx.enter_context(nc.psum_tensor(f"bank{i}", [P, 512], f32)) for i in range(8)]
        ps_qk = bank[0:2]
        ps_s = bank[2:4]
        ps_t = bank[4]
        ps_v = bank[5]
        ps_o = bank[6]
        ps_z = bank[7]
        ps_stack = bank[0:2]
        ps_xt = bank[6:8]

        names = """x_in0 x_in1 acc_in wqk_in0 wqk_in1 wv_in wo_in misc_in
            x0_written slots_zeroed
            zeroed ident_ready mask_ready x_split wqk_hi_ready wqk_split wv_hi_ready wv_split wo_hi_ready wo_split
            qk_done qk_evac v_done v_evac s_done s_masked exp_done rinv_ready p_norm pt_done pt_evac
            pv_done zhi_ready zlo_ready o_done o_added chain
            x1_ready xt_done xt_evac
            xk_done xv_done k_ready k_ss v_ready q_done q_ready q_ss
            hi_ready stack_ready stk_done stk_evac_act stk_evac_dve qzero_ready vzero_ready vd_ready
            xs_done xmax_ready xexp_done xrinv_ready xp_norm xpt_done xpt_evac xpv_done xz_evac
            xo_done xbias_ready xo_added
            x2_ready x2t_done x2t_evac g_in g_done sub_ready gexp_done sel_ready rank_done rank_read slots_ready cum_ready
            xs_written w_in0 w_in1 b2_in xg_in xgt_done xgt_ready h_done h_gelu y_done y_evac y_stored
            ylo_in yhi_in0 yhi_in1 yhi_in2 yhi_in3 yhi_in4 yhi_in5 yhi_in6 yhi_in7 fin_stats fin_sd out_ready out_written""".split()
        s = {n: sem(n) for n in names}

        block = ctx.enter_context(nc.Block())

        def pairs_loop(eng, body):
            body(0, first_pair=True)
            with eng.Fori(1, PAIRS - 1) as p:
                body(p)
            body(PAIRS - 1, last_pair=True)

        ROUNDS = [(0, TT - 2), (TT - 2, TT)]
        STACK_MAKE = (0, 3, 8, 11)
        STACK_PE = (6, 8, 12, 14)
        STACK_EVAC = (7, 9, 13, 15)

        def stack_parts(u):
            k = u // 2 % 2
            parts = stack[u % 2][:, :, :]
            if k == 1:
                hi = parts[:, :, 0:2 * XD].rearrange("p h (a d) -> p h a d", a=2)
                lo = parts[:, :, 2 * XD:4 * XD].rearrange("p h (a d) -> p h a d", a=2)
            else:
                four = parts.rearrange("p h (a c d) -> p h a c d", a=2, c=2)
                hi, lo = four[:, :, :, 0, :], four[:, :, :, 1, :]
            whole = qn[:, :].rearrange("p (h d) -> p h d", h=XH).unsqueeze(2).to_broadcast([P, XH, 2, XD])
            return hi, lo, whole

        @block.sync
        def _(sp):
            half = N // 2
            sp.dma_start(xT_raw[:, :, 0:half], xT_d[:, :, 0:half]).then_inc(s["x_in0"], 16)
            sp.dma_start(w_raw[:, 0, :], w_attn_d[0, :, 0, :]).then_inc(s["wqk_in0"], 16)
            sp.dma_start(xT_raw[:, :, half:N], xT_d[:, :, half:N]).then_inc(s["x_in1"], 16)
            sp.dma_start(w_raw[:, 2, :], w_attn_d[0, :, 2, :]).then_inc(s["wv_in"], 16)
            sp.dma_start(w_raw[:, 1, :], w_attn_d[0, :, 1, :]).then_inc(s["wqk_in1"], 16)
            sp.dma_start(w_raw[:, 3, :], w_attn_d[0, :, 3, :]).then_inc(s["wo_in"], 16)
            sp.dma_start(acc[:, :, :], x_d).then_inc(s["acc_in"], 16)
            sp.wait_ge(s["wqk_split"], 1)
            sp.dma_start(w_raw[:, 0, :], w_attn_d[1, :, 0, :]).then_inc(s["wqk_in0"], 16)
            sp.wait_ge(s["wv_split"], 1)
            sp.dma_start(w_raw[:, 2, :], w_attn_d[1, :, 2, :]).then_inc(s["wv_in"], 16)
            sp.wait_ge(s["wqk_split"], 2)
            sp.dma_start(w_raw[:, 1, :], w_attn_d[1, :, 1, :]).then_inc(s["wqk_in1"], 16)
            sp.dma_start(ctxT[:, :, :], ctxT_d).then_inc(s["misc_in"], 16)
            sp.dma_start(w_x[:, :, :, :], w_x_d).then_inc(s["misc_in"], 16)
            sp.dma_start(vb_col[:, :], vb_d).then_inc(s["misc_in"], 16)
            for n, row in enumerate((qb_d, kb_d, ob_d, nq_d, nk_d)):
                sp.dma_start(rows_bc[:, n, :], row.partition_broadcast(P)).then_inc(s["misc_in"], 16)
            sp.dma_start(gate_w[:, :, :], gate_w_d).then_inc(s["g_in"], 16)
            sp.dma_start(gate_b[:, :], gate_b_d.partition_broadcast(P)).then_inc(s["g_in"], 16)
            sp.dma_start(b1[:, :, :], b1_d).then_inc(s["g_in"], 16)
            sp.wait_ge(s["x0_written"], 1)

            def next_parts(p):
                sp.wait_ge(s["wqk_split"], 2 * p + 3)
                sp.dma_start(w_raw[:, 0, :], w_attn_d[bass.ds(p + 2, 1), :, 0, :]).then_inc(s["wqk_in0"], 16)
                sp.wait_ge(s["wv_split"], p + 2)
                sp.dma_start(w_raw[:, 2, :], w_attn_d[bass.ds(p + 2, 1), :, 2, :]).then_inc(s["wv_in"], 16)
                sp.wait_ge(s["wo_split"], p + 1)
                sp.dma_start(w_raw[:, 3, :], w_attn_d[bass.ds(p + 1, 1), :, 3, :]).then_inc(s["wo_in"], 16)
                sp.dma_start(xs_d[bass.ds(p * N, N), :].rearrange("(a b) d -> a (b d)", a=P),
                             w1[0][:, :, :].rearrange("p c f -> p (c f)")).then_inc(s["slots_zeroed"], 16)
                sp.dma_start(ys_d[bass.ds((p + 1) * N, N), :].rearrange("(a b) d -> a (b d)", a=P),
                             w1[0][:, :, :].rearrange("p c f -> p (c f)")).then_inc(s["slots_zeroed"], 16)
                sp.wait_ge(s["wqk_split"], 2 * p + 4)
                sp.dma_start(w_raw[:, 1, :], w_attn_d[bass.ds(p + 2, 1), :, 1, :]).then_inc(s["wqk_in1"], 16)

            with sp.Fori(0, PAIRS - 2) as p:
                next_parts(p)
            sp.wait_ge(s["wo_split"], PAIRS - 1)
            sp.dma_start(w_raw[:, 3, :], w_attn_d[PAIRS - 1, :, 3, :]).then_inc(s["wo_in"], 16)
            for d, e in [(xs_d, e) for e in range(PAIRS - 2, E)] + [(ys_d, e) for e in range(PAIRS - 1, E)]:
                sp.dma_start(d[e * N:(e + 1) * N, :].rearrange("(a b) d -> a (b d)", a=P),
                             w1[0][:, :, :].rearrange("p c f -> p (c f)")).then_inc(s["slots_zeroed"], 16)
            sp.wait_ge(s["slots_zeroed"], 16 * (2 * E - 1))
            sp.wait_ge(s["y_stored"], 16)
            for e in range(2):
                sp.dma_start(w1[e][:, :, :], w1_d[e]).then_inc(s[f"w_in{e}"], 16)
                sp.dma_start(w2[e][:, :, :], w2_d[e]).then_inc(s[f"w_in{e}"], 16)
            sp.wait_ge(s["xpv_done"], ITEMS)
            sp.dma_start(b2[:, :, :], b2_d.rearrange("e d -> (e d)").partition_broadcast(P)
                         .rearrange("p (e d) -> p e d", e=E)).then_inc(s["b2_in"], 16)
            sp.wait_ge(s["cum_ready"], 1)
            sp.wait_ge(s["xs_written"], 16 * 2 * TT)
            lo = 0
            for e in range(E):
                hi = sp.value_load(cum_i[0:1, e:e + 1], min_val=1, max_val=3 * E)
                with sp.Fori(lo, hi) as i:
                    sp.wait_ge(s["xgt_done"], i + 1)
                    row = nc.s_assert_within((i - lo) * P + e * CAP, e * CAP, (e + 1) * CAP - P,
                                             skip_runtime_bounds_check_because="an expert has at most CAP tokens")
                    sp.dma_start(xg[:, :], xs_d[bass.ds(row, P), :]).then_inc(s["xg_in"], 16)
                lo = hi
            sp.wait_ge(s["xgt_done"], lo + 1)
            sp.dma_start(xg[:, :], xs_d[0:P, :]).then_inc(s["xg_in"], 16)
            for t in range(TT):
                sp.wait_ge(s["out_ready"], t + 1)
                sp.dma_start(out_d[:, t, :], acc[:, t, :]).then_inc(s["out_written"], 16)
            sp.wait_ge(s["out_written"], 16 * TT)

        @block.gpsimd
        def _(pool):
            g = nc.gpsimd
            pool.sem_inc(s["xgt_done"], 1)
            pool.sem_inc(s["h_gelu"], FC)
            pool.sem_inc(s["y_evac"], 1)
            g.memset(ident[:, :], 0.0).then_inc(s["zeroed"], 1)
            g.memset(mask[:, :], 0.0).then_inc(s["zeroed"], 1)
            g.memset(before[:, :], 0.0).then_inc(s["zeroed"], 1)
            pool.wait_ge(s["zeroed"], 3)
            g.affine_select(out=ident[:, :], in_=ident[:, :], compare_op=ALU.not_equal, fill=1.0,
                            base=0, pattern=[[-1, P]], channel_multiplier=1).then_inc(s["ident_ready"], 1)
            for at in (0, 256):
                g.affine_select(out=mask[:, at:at + P], in_=mask[:, at:at + P], compare_op=ALU.is_ge,
                                fill=MASKED, base=0, pattern=[[-1, P]],
                                channel_multiplier=1).then_inc(s["mask_ready"], 1)
            g.affine_select(out=before[:, :], in_=before[:, :], compare_op=ALU.is_ge, fill=1.0,
                            base=0, pattern=[[-1, P]], channel_multiplier=1).then_inc(s["ident_ready"], 1)
            g.memset(ones_bf[:, :], 1.0).then_inc(s["ident_ready"], 1)
            g.memset(sel[:, TT, :], 0.0).then_inc(s["ident_ready"], 1)
            g.memset(zeros_e[:, :], 0.0).then_inc(s["ident_ready"], 1)
            g.iota(iota_e[:, :], pattern=[[1, E]], base=0, channel_multiplier=0,
                   allow_small_or_imprecise_dtypes=True).then_inc(s["ident_ready"], 1)
            g.iota(iota_slot[:, :], pattern=[[CAP, E]], base=0, channel_multiplier=0,
                   allow_small_or_imprecise_dtypes=True).then_inc(s["ident_ready"], 1)
            g.memset(w1[0][:, :, :], 0.0).then_inc(s["x0_written"], 1)
            pool.wait_ge(s["x0_written"], 1)
            g.dma_start(ys_d[0:N, :].rearrange("(a b) d -> a (b d)", a=P),
                        w1[0][:, :, :].rearrange("p c f -> p (c f)")).then_inc(s["y_stored"], 16)

            def split(part, hi, lo, hi_sem, hi_count, done):
                pool.nop(nofuse=True)
                g.tensor_copy(hi[:, :], w_raw[:, part, :]).then_inc(hi_sem, 1)
                pool.wait_ge(hi_sem, hi_count)
                g.tensor_tensor(lo[:, :], w_raw[:, part, :], hi[:, :].bitcast(f32), ALU.subtract).then_inc(done, 1)

            def split_wo(p, first_pair=False):
                pool.wait_ge(s["wo_in"], 16 * p + 16)
                if not first_pair:
                    pool.wait_ge(s["o_done"], TT * p)
                split(3, wo_hi, wo_lo, s["wo_hi_ready"], p + 1, s["wo_split"])

            def split_parts(p, first_pair=False, last_pair=False):
                if last_pair:
                    split_wo(p)
                    return
                pool.wait_ge(s["wqk_in0"], 16 * p + 32)
                pool.wait_ge(s["qk_done"], 8 * p + 4)
                split(0, wqk_hi[0], wqk_lo[0], s["wqk_hi_ready"], 2 * p + 1, s["wqk_split"])
                pool.wait_ge(s["wv_in"], 16 * p + 32)
                pool.wait_ge(s["v_done"], TT * p + TT)
                split(2, wv_hi, wv_lo, s["wv_hi_ready"], p + 1, s["wv_split"])
                split_wo(p, first_pair)
                pool.wait_ge(s["wqk_in1"], 16 * p + 32)
                pool.wait_ge(s["qk_done"], 8 * p + 8)
                split(1, wqk_hi[1], wqk_lo[1], s["wqk_hi_ready"], 2 * p + 2, s["wqk_split"])

            pool.wait_ge(s["wqk_split"], 2)
            pool.wait_ge(s["wv_split"], 1)
            pairs_loop(pool, split_parts)

            pool.wait_ge(s["qk_done"], 4 * H)
            pool.wait_ge(s["v_done"], TT * PAIRS)
            pool.wait_ge(s["wo_split"], PAIRS)
            for i in range(2):
                g.memset(QA[i][:, :, :].bitcast(f32), 0.0).then_inc(s["qzero_ready"], 1)
                g.memset(QB[i][:, :, :].bitcast(f32), 0.0).then_inc(s["qzero_ready"], 1)
            pool.wait_ge(s["o_added"], STEPS)
            for i in range(2):
                g.memset(Vd[i][:, :, :, :], 0.0).then_inc(s["vzero_ready"], 1)
            pool.wait_ge(s["vzero_ready"], 2)

            def v_blocks(b):
                if b >= 2:
                    pool.wait_ge(s["xpv_done"], XH * (b - 1))
                pool.wait_ge(s["v_ready"], 2 * b + 2)
                for kc in range(2):
                    for u in range(2):
                        blocks = Vd[b % 2][:, kc, 8 * u:8 * u + 8, :].rearrange("p h n -> p (h n)")
                        diag = bass.AP(blocks.tensor, blocks.offset, [blocks.ap[0], [P + XD, 8], [1, XD]])
                        src = v_tok[:, 2 * b + kc, u * P:(u + 1) * P].rearrange("p (h d) -> p h d", h=8)
                        g.tensor_copy(diag, src).then_inc(s["vd_ready"], 1)

            def stack_low(u):
                pool.wait_ge(s["hi_ready"], u + 1)
                hi, lo, whole = stack_parts(u)
                g.tensor_tensor(lo, whole, hi.bitcast(f32), ALU.subtract).then_inc(s["stack_ready"], 1)

            v_blocks(0)
            pool.wait_ge(s["xt_done"], TT)
            for t in range(TT):
                g.tensor_tensor(acc[:, t, :], acc[:, t, :], rows_bc[:, 2, :], ALU.add).then_inc(s["xbias_ready"], 1)
            v_blocks(1)
            for b in range(1, B):
                for u in range(4):
                    stack_low(4 * b + u)
                if b + 1 < B:
                    v_blocks(b + 1)

            pool.wait_ge(s["slots_zeroed"], 16 * (2 * E - 1))
            for r, (t0, t1) in enumerate(ROUNDS):
                pool.wait_ge(s["slots_ready"], r + 1)
                for t in range(t0, t1):
                    for k in range(2):
                        g.indirect_dma_start(xs_d, bass.IndirectOffsetOnAxis(ap=slot_i[:, t, k:k + 1], axis=0),
                                             acc[:, t, :], None).then_inc(s["xs_written"], 16)
            pool.wait_ge(s["cum_ready"], 1)
            lo = 0
            for e in range(E):
                hi = pool.value_load(cum_i[0:1, e:e + 1], min_val=1, max_val=3 * E)
                if e == E - 1:
                    pool.wait_ge(s["y_stored"], lo * 16 + 16)
                    pool.nop(nofuse=True)
                    for t in range(TT):
                        g.indirect_dma_start(y_lo[:, t, :], None, ys_d,
                                             bass.IndirectOffsetOnAxis(ap=slot_i[:, t, 0:1], axis=0))\
                            .then_inc(s["ylo_in"], 16)
                with pool.Fori(lo, hi) as i:
                    pool.wait_ge(s["y_evac"], i + 2)
                    row = nc.s_assert_within((i - lo) * P + e * CAP, e * CAP, (e + 1) * CAP - P,
                                             skip_runtime_bounds_check_because="an expert has at most CAP tokens")
                    g.dma_start(ys_d[bass.ds(row, P), :], ys[:, :]).then_inc(s["y_stored"], 16)
                lo = hi
            pool.wait_ge(s["y_stored"], lo * 16 + 16)
            pool.nop(nofuse=True)
            for t in range(TT):
                g.indirect_dma_start(y_hi[:, t, :], None, ys_d,
                                     bass.IndirectOffsetOnAxis(ap=slot_i[:, t, 1:2], axis=0)).then_inc(s[f"yhi_in{t}"], 16)

        @block.tensor
        def _(pe):
            mm = nc.tensor.matmul

            def three(out, lh, ll, rh, rl, start, stop):
                mm(out, lh, rh, start=start, stop=False)
                mm(out, lh, rl, start=False, stop=False)
                return mm(out, ll, rh, start=False, stop=stop)

            def qk_unit(p, hh, u, fill=False):
                n = 8 * p + 4 * hh + u
                if u == 0:
                    pe.wait_ge(s["wqk_split"], 2 * p + hh + 1)
                if not (fill and u < 2):
                    pe.wait_ge(s["qk_evac"], n - 1)
                cols = slice(u // 2 * 512, u // 2 * 512 + 512)
                for c in range(DC):
                    a = u % 2 * 256 + c * P
                    last = three(ps_qk[u % 2][:, :], wqk_hi[hh][:, a:a + P], wqk_lo[hh][:, a:a + P],
                                 xT_hi[:, c, cols], xT_lo[:, c, cols], c == 0, c == DC - 1)
                last.then_inc(s["qk_done"], 1)

            def v_unit(p, t, fill=False):
                if t == 0:
                    pe.wait_ge(s["wv_split"], p + 1)
                if not (fill and t == 0):
                    pe.wait_ge(s["v_evac"], TT * p + t)
                for c in range(DC):
                    last = three(ps_v[:, 0:D], xT_hi[:, c, t * P:(t + 1) * P], xT_lo[:, c, t * P:(t + 1) * P],
                                 wv_hi[:, c * 256:(c + 1) * 256], wv_lo[:, c * 256:(c + 1) * 256],
                                 c == 0, c == DC - 1)
                last.then_inc(s["v_done"], 1)

            def scores(p, st, first_pair):
                hh, b = st // B, st % B
                pe.wait_ge(s["qk_evac"], 8 * p + 4 * hh + 2 * (b // 2) + 2)
                if not (first_pair and st < 2):
                    pe.wait_ge(s["s_masked"], 8 * p + st - 1)
                ps, q_, k_ = ps_s[st % 2], QT[hh], KT[hh]
                at = b * S
                mm(ps[:, 0:P], q_[:, at:at + P], k_[:, at:at + P], start=True, stop=True)
                mm(ps[:, P:P + S], q_[:, at + P:at + S], k_[:, at:at + S], start=True, stop=True)\
                    .then_inc(s["s_done"], 1)

            def transposes(i, buf, fill=False):
                pe.wait_ge(s["p_norm"], i + 1)
                if not fill:
                    pe.wait_ge(s["pt_evac"], i)
                for k in range(3):
                    last = nc.tensor.transpose(ps_t[:, k * P:(k + 1) * P], Pr[buf][:, k * P:(k + 1) * P], ident[:, :])
                last.then_inc(s["pt_done"], 1)

            def pv(p, st, fill=False):
                hh, b = st // B, st % B
                i = 8 * p + st
                pe.wait_ge(s["v_evac"], TT * p + 2 * b + 2)
                pe.wait_ge(s["pt_evac"], i + 1)
                if not fill:
                    pe.wait_ge(s["zlo_ready"], i)
                mm(ps_z[:, 0:S], V[:, 2 * b, hh * DH:(hh + 1) * DH], PT[st % 2][:, 0:S], start=True, stop=False)
                mm(ps_z[:, P:S], V[:, 2 * b + 1, hh * DH:(hh + 1) * DH], PT[st % 2][:, S:S + P],
                   start=False, stop=True).then_inc(s["pv_done"], 1)

            def o_unit(p, t, fill=False):
                if t == 0:
                    pe.wait_ge(s["wo_split"], p + 1)
                pe.wait_ge(s["zlo_ready"], 8 * p + 5 + t // 2)
                if not fill:
                    pe.wait_ge(s["o_added"], TT * p + t)
                for hh in range(2):
                    last = three(ps_o[:, 0:D], z_hi[:, hh, t * P:(t + 1) * P], z_lo[:, hh, t * P:(t + 1) * P],
                                 wo_hi[:, hh * D:(hh + 1) * D], wo_lo[:, hh * D:(hh + 1) * D], hh == 0, hh == 1)
                last.then_inc(s["o_done"], 1)

            def xk_unit(t):
                pe.wait_ge(s["misc_in"], 16 * 8)
                pe.wait_ge(s["v_evac"], TT * PAIRS)
                if t >= 1:
                    pe.wait_ge(s["k_ready"], t)
                for c in range(DC):
                    last = mm(ps_v[:, 0:D], ctxT[:, c, t * P:(t + 1) * P], w_x[:, 1, c, :],
                              start=c == 0, stop=c == DC - 1)
                last.then_inc(s["xk_done"], 1)

            def xv_unit(t):
                pe.wait_ge(s["qk_evac"], 4 * H)
                if t >= 2:
                    pe.wait_ge(s["v_ready"], t - 1)
                for c in range(DC):
                    last = mm(ps_qk[t % 2][:, 0:D], ctxT[:, c, t * P:(t + 1) * P], w_x[:, 2, c, :],
                              start=c == 0, stop=c == DC - 1)
                last.then_inc(s["xv_done"], 1)

            def attend(p, first_pair=False, last_pair=False):
                for st in range(8):
                    hh = st // B
                    prev_p, prev = (p, st - 1) if st else (p - 1, 7)
                    started = st > 0 or not first_pair
                    v_tiles = [(p, 4 + 2 * st), (p, 5 + 2 * st)] if st < 2 else \
                        [(p + 1, 2 * (st - 6)), (p + 1, 2 * (st - 6) + 1)] if st >= 6 and not last_pair else []
                    o_tiles = [(p - 1, 2 + 2 * st), (p - 1, 3 + 2 * st)] if st < 3 and not first_pair else \
                        [(p, 0), (p, 1)] if st == 7 else []
                    if v_tiles:
                        v_unit(*v_tiles[0])
                    if last_pair and 2 <= st < 6:
                        xk_unit(2 * (st - 2))
                    scores(p, st, first_pair)
                    if o_tiles:
                        o_unit(*o_tiles[0], fill=first_pair and st == 7)
                    if started:
                        transposes(8 * p + st - 1, (st - 1) % 2, fill=first_pair and st == 1)
                    if hh == 0:
                        qk_unit(p, 1, st)
                    elif not last_pair:
                        qk_unit(p + 1, 0, st - 4)
                    else:
                        xv_unit(2 * (st - 4))
                        xv_unit(2 * (st - 4) + 1)
                    if v_tiles:
                        v_unit(*v_tiles[1])
                    if last_pair and 2 <= st < 6:
                        xk_unit(2 * (st - 2) + 1)
                    if o_tiles:
                        o_unit(*o_tiles[1])
                    if started:
                        pv(prev_p, prev, fill=first_pair and st == 1)

            pe.wait_ge(s["x_split"], 2)
            for u in range(2):
                qk_unit(0, 0, u, fill=True)
            pe.wait_ge(s["x_split"], 4)
            for u in range(2, 4):
                qk_unit(0, 0, u)
            for t in range(4):
                v_unit(0, t, fill=True)
            pe.wait_ge(s["ident_ready"], 7)
            pairs_loop(pe, attend)
            transposes(STEPS - 1, 1)

            def stack_unit(u):
                pe.wait_ge(s["stack_ready"], u + 1)
                if u == 0:
                    pe.wait_ge(s["v_ready"], TT)
                else:
                    pe.wait_ge(s["stk_evac_act"], u)
                    pe.wait_ge(s["stk_evac_dve"], u)
                for hp in range(XH // 2):
                    last = nc.tensor.transpose(ps_stack[hp // 4][:, (hp % 4) * P:(hp % 4 + 1) * P],
                                               stack[u % 2][:, 2 * hp:2 * hp + 2, :]
                                               .rearrange("p a n -> p (a n)").bitcast(f32), ident[:, :])
                last.then_inc(s["stk_done"], 1)

            def xt_unit(t):
                pe.wait_ge(s["x1_ready"], t + 1)
                if t >= 2:
                    pe.wait_ge(s["xt_evac"], t - 1)
                for c in range(DC):
                    last = nc.tensor.transpose(ps_s[t % 2][:, c * P:(c + 1) * P], acc[:, t, c * P:(c + 1) * P],
                                               ident[:, :])
                last.then_inc(s["xt_done"], 1)

            def q_unit(t):
                pe.wait_ge(s["xt_evac"], t + 1)
                ps = bank[4 + t % 2] if t < 4 else bank[5]
                if t == 2 or t == 3:
                    pe.wait_ge(s["q_ready"], t - 1)
                elif t >= 4:
                    pe.wait_ge(s["q_ready"], t)
                for c in range(DC):
                    last = mm(ps[:, 0:D], xT1[:, c, t * P:(t + 1) * P], w_x[:, 0, c, :],
                              start=c == 0, stop=c == DC - 1)
                last.then_inc(s["q_done"], 1)

            def x_scores(j):
                b, h = j // XH, j % XH
                if h == 0:
                    pe.wait_ge(s["stk_evac_act"], 4 * b + 4)
                    pe.wait_ge(s["stk_evac_dve"], 4 * b + 4)
                if j >= 2:
                    pe.wait_ge(s["xexp_done"], j - 1)
                q_ = (QA, QB)[h % 2][b % 2]
                for qt in range(2):
                    last = mm(ps_s[j % 2][:, qt * S:(qt + 1) * S], q_[:, h // 2, qt * P:(qt + 1) * P],
                              XK[b % 2][:, h // 2, :], start=True, stop=True)
                last.then_inc(s["xs_done"], 1)

            def x_transposes(j):
                pe.wait_ge(s["xp_norm"], j + 1)
                if j >= 2:
                    pe.wait_ge(s["xpt_evac"], j - 1)
                for kc in range(2):
                    for qt in range(2):
                        last = nc.tensor.transpose(ps_xt[j % 2][:, kc * S + qt * P:kc * S + (qt + 1) * P],
                                                   xP[j % 3][:, qt, kc * P:(kc + 1) * P], ident[:, :])
                last.then_inc(s["xpt_done"], 1)

            def x_pv(j):
                b, h = j // XH, j % XH
                g = j // 8
                if h == 0:
                    pe.wait_ge(s["vd_ready"], 4 * b + 4)
                pe.wait_ge(s["xpt_evac"], j + 1)
                if h % 8 == 0:
                    if g < 2:
                        pe.wait_ge(s["q_ready"], 4 if g == 0 else TT)
                    else:
                        pe.wait_ge(s["xz_evac"], g - 1)
                for kc in range(2):
                    last = mm(bank[4 + g % 2][:, 0:S], Vd[b % 2][:, kc, h, :], xPT[j % 2][:, kc, :],
                              start=h % 8 == 0 and kc == 0, stop=h % 8 == 7 and kc == 1)
                last.then_inc(s["xpv_done"], 1)

            def xo_unit(t):
                b = t // 2
                pe.wait_ge(s["xz_evac"], 2 * b + 2)
                pe.wait_ge(s["stk_evac_act"], min(4 * b + 8, 4 * B))
                pe.wait_ge(s["stk_evac_dve"], min(4 * b + 8, 4 * B))
                if b == B - 1:
                    pe.wait_ge(s["rank_read"], 1)
                for c in range(DC):
                    last = mm(ps_stack[t % 2][:, 0:D], xz[b % 2][:, c, (t % 2) * P:(t % 2 + 1) * P], w_x[:, 3, c, :],
                              start=c == 0, stop=c == DC - 1)
                last.then_inc(s["xo_done"], 1)

            def x2t_unit(v):
                pe.wait_ge(s["x2_ready"], 2 * v + 2)
                if v >= 2:
                    pe.wait_ge(s["x2t_evac"], v - 1)
                for t in (2 * v, 2 * v + 1):
                    for c in range(DC):
                        at = (t % 2 * DC + c) * P
                        last = nc.tensor.transpose(ps_stack[v % 2][:, at:at + P], acc[:, t, c * P:(c + 1) * P], ident[:, :])
                last.then_inc(s["x2t_done"], 1)

            def gate_unit(r):
                t0, t1 = ROUNDS[r]
                pe.wait_ge(s["x2t_evac"], t1 // 2)
                pe.wait_ge(s["g_in"], 16 * 3)
                for t in range(t0, t1):
                    for c in range(DC):
                        last = mm(ps_stack[0][:, t * E:(t + 1) * E], xT1[:, c, t * P:(t + 1) * P], gate_w[:, c, :],
                                  start=c == 0, stop=c == DC - 1)
                last.then_inc(s["g_done"], 1)

            def rank_unit(r):
                t0, t1 = ROUNDS[r]
                end = t1 + 1 if r else t1
                pe.wait_ge(s["sel_ready"], r + 1)
                out = ps_stack[1]
                out = out[:, 0:(TT + 1) * E].rearrange("p (t e) -> p t e", e=E)
                mm(out[:, t0:end, :], before[:, :], sel[:, t0:end, :],
                   start=True, stop=False)
                for t in range(end - 1):
                    a = max(t + 1, t0)
                    last = mm(out[:, a:end, :], ones_bf[:, :], sel[:, t:t + 1, :].to_broadcast([P, end - a, E]),
                              start=False, stop=t == end - 2)
                last.then_inc(s["rank_done"], 1)

            o_unit(PAIRS - 1, 2)
            pv(PAIRS - 1, 7)
            for t in range(3, TT):
                o_unit(PAIRS - 1, t)
                if t in (4, 5):
                    stack_unit(t - 4)
            for t in range(TT):
                xt_unit(t)
                if 1 <= t < 5:
                    q_unit(t - 1)
            stack_unit(2)
            stack_unit(3)
            for j in range(ITEMS):
                b, h = j // XH, j % XH
                x_scores(j)
                if j >= 2:
                    x_transposes(j - 2)
                if b == 0 and h in (0, 2, 4, 6):
                    q_unit(4 + h // 2)
                if b >= 1 and h == 4:
                    xo_unit(2 * b - 2)
                    xo_unit(2 * b - 1)
                if b + 1 < B and h in STACK_PE:
                    if h == STACK_PE[0] and b >= 1:
                        pe.wait_ge(s["xo_added"], 2 * b)
                    stack_unit(4 * (b + 1) + STACK_PE.index(h))
                if b == B - 1:
                    if h == 8:
                        x2t_unit(0)
                    if h == 9:
                        x2t_unit(1)
                        x2t_unit(2)
                    if h == 11:
                        gate_unit(0)
                if j >= 3:
                    x_pv(j - 3)
            rank_unit(0)
            x_transposes(ITEMS - 2)
            x_pv(ITEMS - 3)
            x_transposes(ITEMS - 1)
            x_pv(ITEMS - 2)
            x_pv(ITEMS - 1)
            xo_unit(TT - 2)
            xo_unit(TT - 1)

            x2t_unit(TT // 2 - 1)
            gate_unit(1)
            rank_unit(1)

            pe.wait_ge(s["cum_ready"], 1)

            def xg_transposes(count_in):
                pe.wait_ge(s["xg_in"], count_in)
                for c in range(DC):
                    last = nc.tensor.transpose(bank[4][:, c * P:(c + 1) * P], xg[:, c * P:(c + 1) * P], ident[:, :])
                last.then_inc(s["xgt_done"], 1)

            xg_transposes(16)
            lo = 0
            for e in range(E):
                w1e, w2e = w1[e % 2], w2[e % 2]
                hi = pe.value_load(cum_i[0:1, e:e + 1], min_val=1, max_val=3 * E)
                pe.wait_ge(s[f"w_in{e % 2}"], 32 * (e // 2 + 1))
                with pe.Fori(lo, hi) as i:
                    pe.wait_ge(s["xgt_ready"], i + 1)
                    for f in range(FC):
                        pe.wait_ge(s["h_gelu"], i * FC + f + FC - 3)
                        for c in range(DC):
                            last = mm(bank[f % 4][:, 0:P], w1e[:, c, f * P:(f + 1) * P], xgT[:, c, :],
                                      start=c == 0, stop=c == DC - 1)
                        last.then_inc(s["h_done"], 1)
                    xg_transposes(i * 16 + 32)
                    pe.wait_ge(s["y_evac"], i + 1)
                    for f in range(FC):
                        pe.wait_ge(s["h_gelu"], i * FC + f + FC + 1)
                        last = mm(bank[5][:, 0:D], hT[:, f, :], w2e[:, f, :], start=f == 0, stop=f == FC - 1)
                    last.then_inc(s["y_done"], 1)
                lo = hi

        @block.scalar
        def _(act):
            A = nc.scalar.activation

            def qk_evac(p, hh, u):
                act.wait_ge(s["qk_done"], 8 * p + 4 * hh + u + 1)
                dst = (QT if u % 2 == 0 else KT)[hh][:, u // 2 * 512:u // 2 * 512 + 512]
                A(dst, ps_qk[u % 2][:, :], ACT.Copy, scale=1.0 if u % 2 == 0 else -SCALE).then_inc(s["qk_evac"], 1)

            def v_evac(p, t):
                act.wait_ge(s["v_done"], TT * p + t + 1)
                A(V[:, t, :], ps_v[:, 0:D], ACT.Copy).then_inc(s["v_evac"], 1)

            def z_high(p, st):
                hh, b = st // B, st % B
                act.wait_ge(s["pv_done"], 8 * p + st + 1)
                A(z_hi[:, hh, b * S:(b + 1) * S], ps_z[:, 0:S], ACT.Copy).then_inc(s["zhi_ready"], 1)

            def exps(p, st, first_pair):
                buf = st % 2
                act.wait_ge(s["s_masked"], 8 * p + st + 1)
                if not (first_pair and st < 2):
                    act.wait_ge(s["pt_done"], 8 * p + st - 1)
                A(Pr[buf][:, 0:P], Sm[buf][:, 0:P], ACT.Exp, bias=nmax[buf][:, 0:1], scale=-1.0,
                  accum_out=rsum[buf][:, 0:1])
                A(Pr[buf][:, P:384], Sm[buf][:, P:384], ACT.Exp, bias=nmax[buf][:, 1:2], scale=-1.0,
                  accum_out=rsum[buf][:, 1:2]).then_inc(s["exp_done"], 1)

            def k_squares(t):
                act.wait_ge(s["k_ready"], t + 1)
                if t >= 1:
                    act.wait_ge(s["k_ss"], t)
                A(junk[:, :], k_tok[:, t, :], ACT.Square, accum_out=kss[:, t:t + 1]).then_inc(s["k_ss"], 1)

            def xv_evac(t):
                act.wait_ge(s["xv_done"], t + 1)
                A(v_tok[:, t, :], ps_qk[t % 2][:, 0:D], ACT.Copy).then_inc(s["v_ready"], 1)

            def evacuate(p, first_pair=False, last_pair=False):
                for st in range(8):
                    v_tiles = [(p, 4 + 2 * st), (p, 5 + 2 * st)] if st < 2 else \
                        [(p + 1, 2 * (st - 6)), (p + 1, 2 * (st - 6) + 1)] if st >= 6 and not last_pair else []
                    if st >= 2 or not first_pair:
                        z_high(*((p, st - 2) if st >= 2 else (p - 1, st + 6)))
                    if v_tiles:
                        v_evac(*v_tiles[0])
                    if last_pair and 3 <= st < 7:
                        k_squares(2 * (st - 3))
                        k_squares(2 * (st - 3) + 1)
                    exps(p, st, first_pair)
                    if st < 4:
                        qk_evac(p, 1, st)
                    elif not last_pair:
                        qk_evac(p + 1, 0, st - 4)
                    else:
                        xv_evac(2 * (st - 4))
                        xv_evac(2 * (st - 4) + 1)
                    if v_tiles:
                        v_evac(*v_tiles[1])

            for u in range(4):
                qk_evac(0, 0, u)
            for t in range(4):
                v_evac(0, t)
            pairs_loop(act, evacuate)
            z_high(PAIRS - 1, 6)

            def stack_evac(u):
                b, k, j = u // 4, u // 2 % 2, u % 2
                cols = slice(j * P, (j + 1) * P)
                act.wait_ge(s["stk_done"], u + 1)
                if k == 1:
                    if u == 2:
                        act.wait_ge(s["qzero_ready"], 4)
                    for q in range(2):
                        last = A(QA[b % 2][0:64, 4 * q:4 * q + 4, cols],
                                 ps_stack[q][0:64, :].rearrange("p (a n) -> p a n", a=4), ACT.Copy)
                else:
                    last = A(XK[b % 2][:, 0:4, cols], ps_stack[0][:, :].rearrange("p (a n) -> p a n", a=4), ACT.Copy)
                last.then_inc(s["stk_evac_act"], 1)

            def q_squares(t):
                act.wait_ge(s["q_ready"], t + 1)
                if t >= 1:
                    act.wait_ge(s["q_ss"], t)
                else:
                    act.wait_ge(s["k_ss"], TT)
                A(junk[:, :], q_tok[:, t, :], ACT.Square, accum_out=qss[:, t:t + 1]).then_inc(s["q_ss"], 1)

            def xt_evac(t):
                act.wait_ge(s["xt_done"], t + 1)
                A(xT1[:, :, t * P:(t + 1) * P], ps_s[t % 2][:, 0:D].rearrange("p (c n) -> p c n", c=DC),
                  ACT.Copy).then_inc(s["xt_evac"], 1)

            def x_exps(j):
                act.wait_ge(s["xmax_ready"], j + 1)
                if j >= 3:
                    act.wait_ge(s["xpt_done"], j - 2)
                for qt in range(2):
                    last = A(xP[j % 3][:, qt, :], ps_s[j % 2][:, qt * S:(qt + 1) * S], ACT.Exp,
                             bias=xnmax[j % 3][:, qt:qt + 1], accum_out=xrsum[j % 3][:, qt:qt + 1])
                last.then_inc(s["xexp_done"], 1)

            def xpt_evac(j):
                act.wait_ge(s["xpt_done"], j + 1)
                if j >= 2:
                    act.wait_ge(s["xpv_done"], j - 1)
                A(xPT[j % 2][:, :, :], ps_xt[j % 2][:, :].rearrange("p (a n) -> p a n", a=2), ACT.Copy)\
                    .then_inc(s["xpt_evac"], 1)

            def xz_evac(g):
                b = g // 2
                act.wait_ge(s["xpv_done"], 8 * (g + 1))
                if b >= 2:
                    act.wait_ge(s["xo_done"], 2 * (b - 1))
                A(xz[b % 2][:, g % 2, :], bank[4 + g % 2][:, 0:S], ACT.Identity, bias=vb_col[:, g % 2:g % 2 + 1])\
                    .then_inc(s["xz_evac"], 1)

            def x2t_evac(v):
                act.wait_ge(s["x2t_done"], v + 1)
                A(xT1[:, :, 2 * v * P:(2 * v + 2) * P].rearrange("p c (t n) -> p t c n", t=2),
                  ps_stack[v % 2][:, :].rearrange("p (t c n) -> p t c n", t=2, c=DC), ACT.Copy).then_inc(s["x2t_evac"], 1)

            def gate_exp(r):
                t0, t1 = ROUNDS[r]
                act.wait_ge(s["sub_ready"], r + 1)
                A(probs[:, t0:t1, :], logits[:, t0:t1, :], ACT.Exp).then_inc(s["gexp_done"], 1)

            z_high(PAIRS - 1, 7)
            stack_evac(0)
            stack_evac(1)
            act.wait_ge(s["misc_in"], 16 * 8)
            for t in range(TT):
                xt_evac(t)
                if t == 2:
                    q_squares(0)
                    q_squares(1)
            stack_evac(2)
            stack_evac(3)
            for j in range(ITEMS):
                b, h = j // XH, j % XH
                if j >= 2:
                    xpt_evac(j - 2)
                x_exps(j)
                if b == 0 and h in (1, 3, 5, 7):
                    if h == 1:
                        q_squares(2)
                        q_squares(3)
                    q_squares(4 + h // 2)
                if b + 1 < B and h in STACK_EVAC:
                    stack_evac(4 * (b + 1) + STACK_EVAC.index(h))
                if j >= 10 and (j - 3) % 8 == 7:
                    xz_evac((j - 10) // 8)
                if b == B - 1:
                    if h in (9, 10):
                        x2t_evac(h - 9)
                    if h == 10:
                        x2t_evac(2)
                    if h == 12:
                        gate_exp(0)
            xpt_evac(ITEMS - 2)
            xpt_evac(ITEMS - 1)
            xz_evac(2 * B - 1)

            x2t_evac(TT // 2 - 1)
            gate_exp(1)
            act.wait_ge(s["cum_ready"], 1)
            act.wait_ge(s["g_in"], 16 * 3)
            lo = 0
            for e in range(E):
                hi = act.value_load(cum_i[0:1, e:e + 1], min_val=1, max_val=3 * E)
                if 1 <= e < E - 1:
                    act.wait_ge(s["y_done"], lo)
                    d = s[f"w_in{(e + 1) % 2}"]
                    act.dma_start(w1[(e + 1) % 2][:, :, :], w1_d[e + 1]).then_inc(d, 16)
                    act.dma_start(w2[(e + 1) % 2][:, :, :], w2_d[e + 1]).then_inc(d, 16)
                with act.Fori(lo, hi) as i:
                    for f in range(FC):
                        act.wait_ge(s["h_done"], i * FC + f + 1)
                        A(hT[:, f, :], bank[f % 4][:, 0:P], ACT.Gelu_apprx_tanh, bias=b1[:, e, f:f + 1])\
                            .then_inc(s["h_gelu"], 1)
                lo = hi
            for t in range(TT):
                act.wait_ge(s["fin_stats"], t + 1)
                A(sd[:, t:t + 1], mv[:, t, 1:2], ACT.Sqrt, bias=eps_ln[:, 0:1]).then_inc(s["fin_sd"], 1)

        @block.vector
        def _(dve):
            v = nc.vector
            chain_count = [0]

            def chained(ins):
                chain_count[0] += 1
                ins.then_inc(s["chain"], 1)
                dve.wait_ge(s["chain"], chain_count[0])

            def rsqrt(dst, src, scale, eps, a, z):
                x, y, t = nt_a[:, a:z], dst[:, a:z], nt_b[:, a:z]
                chained(v.tensor_scalar(x, src, scale, eps, ALU.mult, ALU.add))
                chained(v.tensor_scalar(y.bitcast(i32), x.bitcast(i32), -0.5, RSQRT_SEED, ALU.mult, ALU.add))
                for _ in range(3):
                    chained(v.tensor_tensor(t, y, y, ALU.mult))
                    chained(v.tensor_tensor(t, t, x, ALU.mult))
                    chained(v.tensor_scalar(t, t, -0.5, 1.5, ALU.mult, ALU.add))
                    chained(v.tensor_tensor(y, y, t, ALU.mult))

            def split_x(half):
                cols = slice(half * 512, (half + 1) * 512)
                dve.wait_ge(s[f"x_in{half}"], 16)
                for c in range(DC):
                    chained(v.tensor_copy(xT_hi[:, c, cols], xT_raw[:, c, cols]))
                    v.tensor_tensor(xT_lo[:, c, cols], xT_raw[:, c, cols], xT_hi[:, c, cols].bitcast(f32),
                                    ALU.subtract).then_inc(s["x_split"], 1)

            def split_w(part, hi, lo, done):
                chained(v.tensor_copy(hi[:, :], w_raw[:, part, :]))
                v.tensor_tensor(lo[:, :], w_raw[:, part, :], hi[:, :].bitcast(f32), ALU.subtract).then_inc(done, 1)

            def mask_max(p, st, first_pair):
                buf = st % 2
                dve.wait_ge(s["s_done"], 8 * p + st + 1)
                if not (first_pair and st < 2):
                    dve.wait_ge(s["exp_done"], 8 * p + st - 1)
                dve.nop(nofuse=True)
                for a, z in ((0, P), (P, 384)):
                    last = v.tensor_tensor_reduce(out=Sm[buf][:, a:z], in0=ps_s[buf][:, a:z], in1=mask[:, a:z],
                                                  scale=1.0, scalar=BIG, op0=ALU.add, op1=ALU.min,
                                                  accum_out=nmax[buf][:, (a > 0):(a > 0) + 1])
                last.then_inc(s["s_masked"], 1)

            def pt_evac(i, buf, fill=False):
                dve.wait_ge(s["pt_done"], i + 1)
                if not fill:
                    dve.wait_ge(s["pv_done"], i - 1)
                v.tensor_copy(PT[buf][:, :], ps_t[:, 0:384]).then_inc(s["pt_evac"], 1)

            def o_add(p, t, start=False):
                m = TT * p + t
                dve.wait_ge(s["o_done"], m + 1)
                if not start:
                    dve.wait_ge(s["o_added"], m)
                v.tensor_tensor(acc[:, t, :], acc[:, t, :], ps_o[:, 0:D], ALU.add).then_inc(s["o_added"], 1)

            def z_low(p, st):
                hh, b = st // B, st % B
                dve.wait_ge(s["zhi_ready"], 8 * p + st + 1)
                cols = slice(b * S, (b + 1) * S)
                v.tensor_tensor(z_lo[:, hh, cols], ps_z[:, 0:S], z_hi[:, hh, cols].bitcast(f32), ALU.subtract)\
                    .then_inc(s["zlo_ready"], 1)

            def normalise(i, buf):
                dve.wait_ge(s["exp_done"], i + 1)
                v.reciprocal(rinv[buf][:, :], rsum[buf][:, :]).then_inc(s["rinv_ready"], 1)
                dve.wait_ge(s["rinv_ready"], i + 1)
                v.tensor_scalar(Pr[buf][:, 0:P], Pr[buf][:, 0:P], rinv[buf][:, 0:1], None, ALU.mult)
                v.tensor_scalar(Pr[buf][:, P:384], Pr[buf][:, P:384], rinv[buf][:, 1:2], None, ALU.mult)\
                    .then_inc(s["p_norm"], 1)

            def k_add(t):
                dve.wait_ge(s["xk_done"], t + 1)
                if t == 0:
                    dve.wait_ge(s["misc_in"], 16 * 8)
                v.tensor_tensor(k_tok[:, t, :], ps_v[:, 0:D], rows_bc[:, 1, :], ALU.add).then_inc(s["k_ready"], 1)

            def soften(p, first_pair=False, last_pair=False):
                for st in range(8):
                    o_tiles = [(p - 1, 2 + 2 * st), (p - 1, 3 + 2 * st)] if st < 3 and not first_pair else \
                        [(p, 0), (p, 1)] if st == 7 else []
                    if 1 <= st < 4 and not first_pair:
                        o_add(p - 1, 1 + 2 * st)
                    if st == 0 and not first_pair:
                        o_add(p - 1, 1)
                    if st >= 2 or not first_pair:
                        z_low(*((p, st - 2) if st >= 2 else (p - 1, st + 6)))
                    if last_pair and 2 <= st < 6:
                        k_add(2 * (st - 2))
                    if last_pair and st == 7:
                        dve.wait_ge(s["k_ss"], TT)
                        rsqrt(krs, kss[:, :], 1.0 / D, RMS_EPS, 0, TT)
                    mask_max(p, st, first_pair)
                    if o_tiles:
                        o_add(*o_tiles[0], start=first_pair)
                    if st > 0 or not first_pair:
                        pt_evac(8 * p + st - 1, (st - 1) % 2, fill=first_pair and st < 3)
                    normalise(8 * p + st, st % 2)
                    if last_pair and 2 <= st < 6:
                        k_add(2 * (st - 2) + 1)

            v.memset(eps_ln[:, :], LN_EPS)
            split_x(0)
            dve.wait_ge(s["wqk_in0"], 16)
            split_w(0, wqk_hi[0], wqk_lo[0], s["wqk_split"])
            split_x(1)
            dve.wait_ge(s["wv_in"], 16)
            split_w(2, wv_hi, wv_lo, s["wv_split"])
            dve.wait_ge(s["wqk_in1"], 16)
            split_w(1, wqk_hi[1], wqk_lo[1], s["wqk_split"])
            dve.wait_ge(s["mask_ready"], 2)
            dve.wait_ge(s["acc_in"], 16)
            pairs_loop(dve, soften)

            def make_high(u, low_too=False):
                b, k, j = u // 4, u // 2 % 2, u % 2
                t = 2 * b + j
                src, r = (k_tok, krs) if k == 0 else (q_tok, qrs)
                if u >= 1:
                    dve.wait_ge(s["stack_ready"], u)
                chained(v.scalar_tensor_tensor(out=qn[:, :], in0=src[:, t, :], scalar=r[:, t:t + 1],
                                               in1=rows_bc[:, 4 - k, :], op0=ALU.mult, op1=ALU.mult))
                if u >= 2:
                    dve.wait_ge(s["stk_done"], u - 1)
                hi, lo, whole = stack_parts(u)
                v.tensor_copy(hi, whole).then_inc(s["hi_ready"], 1)
                if low_too:
                    dve.wait_ge(s["hi_ready"], u + 1)
                    v.tensor_tensor(lo, whole, hi.bitcast(f32), ALU.subtract).then_inc(s["stack_ready"], 1)

            def stack_evac(u):
                b, k, j = u // 4, u // 2 % 2, u % 2
                cols = slice(j * P, (j + 1) * P)
                dve.wait_ge(s["stk_done"], u + 1)
                if k == 1:
                    if u == 2:
                        dve.wait_ge(s["qzero_ready"], 4)
                    for q in range(2):
                        last = v.tensor_copy(QB[b % 2][64:128, 4 * q:4 * q + 4, cols],
                                             ps_stack[q][64:128, :].rearrange("p (a n) -> p a n", a=4))
                else:
                    last = v.tensor_copy(XK[b % 2][:, 4:8, cols], ps_stack[1][:, :].rearrange("p (a n) -> p a n", a=4))
                last.then_inc(s["stk_evac_dve"], 1)

            def row_stats(t):
                chained(v.bn_stats(stats[:, t, :], acc[:, t, :]))
                return v.bn_aggr(mv[:, t, :], stats[:, t, :])

            def norm_apply(t, ready):
                v.tensor_scalar(acc[:, t, :], acc[:, t, :], mv[:, t, 0:1], rstd[:, t:t + 1],
                                ALU.subtract, ALU.mult).then_inc(ready, 1)

            def q_add(t):
                dve.wait_ge(s["q_done"], t + 1)
                ps = bank[4 + t % 2] if t < 4 else bank[5]
                v.tensor_tensor(q_tok[:, t, :], ps[:, 0:D], rows_bc[:, 0, :], ALU.add).then_inc(s["q_ready"], 1)

            def x_max(j):
                dve.wait_ge(s["xs_done"], j + 1)
                v.tensor_reduce(xnmax[j % 3][:, :], ps_s[j % 2][:, :].rearrange("p (a n) -> p a n", a=2), AX.X,
                                ALU.max, negate=True).then_inc(s["xmax_ready"], 1)

            def x_normalise(j):
                dve.wait_ge(s["xexp_done"], j + 1)
                v.reciprocal(xrinv[j % 3][:, :], xrsum[j % 3][:, :]).then_inc(s["xrinv_ready"], 1)
                dve.wait_ge(s["xrinv_ready"], j + 1)
                for qt in range(2):
                    last = v.tensor_scalar(xP[j % 3][:, qt, :], xP[j % 3][:, qt, :], xrinv[j % 3][:, qt:qt + 1], None,
                                           ALU.mult)
                last.then_inc(s["xp_norm"], 1)

            def xo_add(t):
                dve.wait_ge(s["xo_done"], t + 1)
                dve.wait_ge(s["xbias_ready"], TT)
                v.tensor_tensor(acc[:, t, :], acc[:, t, :], ps_stack[t % 2][:, 0:D], ALU.add).then_inc(s["xo_added"], 1)
                dve.wait_ge(s["xo_added"], t + 1)
                chained(row_stats(t))

            def over_experts(a, t0, t1):
                return a.unsqueeze(2).to_broadcast([P, t1 - t0, E])

            def gate_logits(r):
                t0, t1 = ROUNDS[r]
                n = t1 - t0
                dve.wait_ge(s["g_done"], r + 1)
                chained(v.tensor_tensor(logits[:, t0:t1, :], ps_stack[0][:, t0 * E:t1 * E].rearrange("p (t e) -> p t e", t=n),
                                        gate_b[:, :].unsqueeze(1).to_broadcast([P, n, E]), ALU.add))
                chained(v.tensor_reduce(lmax[:, t0:t1], logits[:, t0:t1, :], AX.X, ALU.max))
                v.tensor_tensor(logits[:, t0:t1, :], logits[:, t0:t1, :], over_experts(lmax[:, t0:t1], t0, t1),
                                ALU.subtract).then_inc(s["sub_ready"], 1)

            def gate_top(r):
                t0, t1 = ROUNDS[r]
                dve.wait_ge(s["gexp_done"], r + 1)
                chained(v.tensor_reduce(lmax[:, t0:t1], probs[:, t0:t1, :], AX.X, ALU.add))
                chained(v.reciprocal(lmax[:, t0:t1], lmax[:, t0:t1]))
                chained(v.tensor_tensor(probs[:, t0:t1, :], probs[:, t0:t1, :], over_experts(lmax[:, t0:t1], t0, t1),
                                        ALU.mult))
                for t in range(t0, t1):
                    last = v.max(top[:, t, :], probs[:, t, :])
                chained(last)

            def gate_index(r):
                t0, t1 = ROUNDS[r]
                for t in range(t0, t1):
                    last = v.max_index(top_i[:, t, :], top[:, t, :], probs[:, t, :])
                chained(last)

            def gate_select(r):
                t0, t1 = ROUNDS[r]
                n = t1 - t0
                chained(v.tensor_copy(top_f[:, t0:t1, :], top_i[:, t0:t1, 0:2]))
                for k, oneh in enumerate((first, second)):
                    last = v.tensor_tensor(oneh[:, t0:t1, :], iota_e[:, :].unsqueeze(1).to_broadcast([P, n, E]),
                                           over_experts(top_f[:, t0:t1, k], t0, t1), ALU.is_equal)
                chained(last)
                v.tensor_tensor(sel[:, t0:t1, :], first[:, t0:t1, :], second[:, t0:t1, :], ALU.add)\
                    .then_inc(s["sel_ready"], 1)

            def gate_weights(r):
                t0, t1 = ROUNDS[r]
                chained(v.tensor_tensor(w12[:, t0:t1], top[:, t0:t1, 0], top[:, t0:t1, 1], ALU.add))
                chained(v.reciprocal(w12[:, t0:t1], w12[:, t0:t1]))
                for k, oneh in enumerate((first, second)):
                    last = v.tensor_tensor(oneh[:, t0:t1, :], oneh[:, t0:t1, :], over_experts(top[:, t0:t1, k], t0, t1),
                                           ALU.mult)
                chained(last)
                chained(v.tensor_tensor(comb[:, t0:t1, :], first[:, t0:t1, :], second[:, t0:t1, :], ALU.add))
                chained(v.tensor_tensor(comb[:, t0:t1, :], comb[:, t0:t1, :], over_experts(w12[:, t0:t1], t0, t1),
                                        ALU.mult))

            def slots(r):
                t0, t1 = ROUNDS[r]
                n = t1 - t0
                sl, st = slot[:, t0:t1, :], slot_t[:, t0:t1, :]
                dve.wait_ge(s["rank_done"], r + 1)
                last = v.tensor_tensor(sl, ps_stack[1][:, t0 * E:t1 * E].rearrange("p (t e) -> p t e", t=n),
                                       iota_slot[:, :].unsqueeze(1).to_broadcast([P, n, E]), ALU.add)
                if r == 0:
                    last.then_inc(s["rank_read"], 1)
                    dve.wait_ge(s["rank_read"], 1)
                else:
                    chained(last)
                    chained(v.tensor_scalar(tiles_i[:, :], ps_stack[1][:, TT * E:(TT + 1) * E], P / 2 - 0.5, 1.0 / P,
                                            ALU.add, ALU.mult))
                    chained(v.tensor_scalar(tiles_f[:, :], tiles_i[:, :], 1.0, None, ALU.max))
                    chained(v.tensor_tensor_scan(cum_f[:, :], tiles_f[:, :], zeros_e[:, :], 0.0, ALU.add, ALU.add))
                    v.tensor_copy(cum_i[:, :], cum_f[:, :]).then_inc(s["cum_ready"], 1)
                chained(v.tensor_scalar(st, sel[:, t0:t1, :], -4.0 * E * CAP, 4.0 * E * CAP, ALU.mult, ALU.add))
                chained(v.tensor_tensor(st, st, sl, ALU.add))
                chained(v.tensor_reduce(slot_lh[:, t0:t1, 0], st, AX.X, ALU.min))
                chained(v.tensor_tensor(st, sl, sel[:, t0:t1, :], ALU.mult))
                chained(v.tensor_reduce(slot_lh[:, t0:t1, 1], st, AX.X, ALU.max))
                v.tensor_copy(slot_i[:, t0:t1, :], slot_lh[:, t0:t1, :]).then_inc(s["slots_ready"], 1)

            def slot_weights(r):
                t0, t1 = ROUNDS[r]
                st = slot_t[:, t0:t1, :]
                for k in range(2):
                    chained(v.tensor_tensor(st, slot[:, t0:t1, :], over_experts(slot_lh[:, t0:t1, k], t0, t1),
                                            ALU.is_equal))
                    chained(v.tensor_tensor(st, st, comb[:, t0:t1, :], ALU.mult))
                    chained(v.tensor_reduce(w_lh[:, t0:t1, k], st, AX.X, ALU.add))

            o_add(PAIRS - 1, 1)
            pt_evac(STEPS - 1, 1)
            z_low(PAIRS - 1, 6)
            o_add(PAIRS - 1, 2)
            z_low(PAIRS - 1, 7)
            o_add(PAIRS - 1, 3)
            make_high(0, low_too=True)
            o_add(PAIRS - 1, 4)
            make_high(1, low_too=True)
            stack_evac(0)
            o_add(PAIRS - 1, 5)
            stack_evac(1)
            for t in range(0, 5):
                row_stats(t)
            for t in (6, 7):
                o_add(PAIRS - 1, t)
                row_stats(t - 1)
            dve.wait_ge(s["o_added"], STEPS)
            chained(row_stats(TT - 1))
            rsqrt(rstd, mv[:, :, 1], 1.0, LN_EPS, 0, TT)
            for t in range(TT):
                norm_apply(t, s["x1_ready"])
            q_add(0)
            q_add(1)
            dve.wait_ge(s["q_ss"], 2)

            def q_scale(a, z):
                rsqrt(qrs, qss[:, a:z], 1.0 / D, RMS_EPS, a, z)
                chained(v.tensor_scalar(qrs[:, a:z], qrs[:, a:z], XSCALE, None, ALU.mult))

            q_scale(0, 2)
            make_high(2, low_too=True)
            make_high(3, low_too=True)
            q_add(2)
            q_add(3)
            stack_evac(2)
            stack_evac(3)
            for j in range(ITEMS):
                b, h = j // XH, j % XH
                x_max(j)
                if j >= 1:
                    x_normalise(j - 1)
                if b == 0 and h in (1, 3, 5, 7):
                    q_add(4 + h // 2)
                if b == 0 and h == 8:
                    dve.wait_ge(s["q_ss"], TT)
                    q_scale(2, TT)
                if b + 1 < B and h in STACK_MAKE:
                    make_high(4 * (b + 1) + STACK_MAKE.index(h))
                if b + 1 < B and h in STACK_EVAC:
                    stack_evac(4 * (b + 1) + STACK_EVAC.index(h))
                if b >= 1 and h == 5:
                    xo_add(2 * b - 2)
                    xo_add(2 * b - 1)
                if b == B - 1:
                    if h == 6:
                        rsqrt(rstd, mv[:, 0:TT - 2, 1], 1.0, LN_EPS, 0, TT - 2)
                    if h in (7, 8):
                        for t in range(3 * (h - 7), 3 * (h - 6)):
                            norm_apply(t, s["x2_ready"])
                    if h == 12:
                        gate_logits(0)
                    if h == 13:
                        gate_top(0)
                    if h == 14:
                        gate_index(0)
                    if h == 15:
                        gate_select(0)
            x_normalise(ITEMS - 1)
            slots(0)
            xo_add(TT - 2)
            xo_add(TT - 1)
            rsqrt(rstd, mv[:, TT - 2:TT, 1], 1.0, LN_EPS, TT - 2, TT)
            norm_apply(TT - 2, s["x2_ready"])
            norm_apply(TT - 1, s["x2_ready"])
            gate_logits(1)
            gate_top(1)
            gate_index(1)
            gate_select(1)
            slots(1)

            def xgt_evac(count_done):
                dve.wait_ge(s["xgt_done"], count_done)
                v.tensor_copy(xgT[:, :, :], bank[4][:, 0:D].rearrange("p (c n) -> p c n", c=DC))\
                    .then_inc(s["xgt_ready"], 1)

            for r in range(2):
                gate_weights(r)
                slot_weights(r)
            dve.wait_ge(s["b2_in"], 16)
            xgt_evac(2)
            lo = 0
            for e in range(E):
                hi = dve.value_load(cum_i[0:1, e:e + 1], min_val=1, max_val=3 * E)
                with dve.Fori(lo, hi) as i:
                    xgt_evac(i + 3)
                    dve.wait_ge(s["y_done"], i + 1)
                    dve.wait_ge(s["y_stored"], i * 16 + 16)
                    v.tensor_tensor(ys[:, :], bank[5][:, 0:D], b2[:, e, :], ALU.add).then_inc(s["y_evac"], 1)
                lo = hi
            for t in range(TT):
                dve.wait_ge(s["ylo_in"], 16 * TT)
                last = v.scalar_tensor_tensor(out=acc[:, t, :], in0=y_lo[:, t, :], scalar=w_lh[:, t, 0:1],
                                              in1=acc[:, t, :], op0=ALU.mult, op1=ALU.add)
            chained(last)
            for t in range(TT):
                dve.wait_ge(s[f"yhi_in{t}"], 16)
                chained(v.scalar_tensor_tensor(out=acc[:, t, :], in0=y_hi[:, t, :], scalar=w_lh[:, t, 1:2],
                                               in1=acc[:, t, :], op0=ALU.mult, op1=ALU.add))
                row_stats(t).then_inc(s["fin_stats"], 1)
                dve.wait_ge(s["fin_sd"], t + 1)
                chained(v.reciprocal(rstd[:, t:t + 1], sd[:, t:t + 1]))
                norm_apply(t, s["out_ready"])


def kernel(**inputs):
    import numpy as np
    import concourse.bacc as bacc
    from concourse.bass_utils import run_bass_kernel_spmd

    g = {k: np.asarray(a) for k, a in inputs.items()}
    P = 128

    def chunks(a):
        n = a.shape[-2] // P
        b = a.reshape(*a.shape[:-2], n, P, a.shape[-1])
        return np.moveaxis(b, -3, -2)

    x = g["x"].reshape(-1, g["x"].shape[-1])
    c = g["ctx_2048"].reshape(-1, x.shape[1])
    pairs = g["L0_attn_W_Q"].shape[0] // 2

    def per_head(w):
        t = chunks(np.swapaxes(w, 1, 2))
        t = t.reshape(pairs, 2, *t.shape[1:])
        return np.moveaxis(t, 1, 2).reshape(pairs, P, 2, -1)

    wv = chunks(np.swapaxes(g["L0_attn_W_V"], 1, 2))
    wv = wv.reshape(pairs, 2, *wv.shape[1:])
    wv = np.transpose(wv, (0, 2, 3, 1, 4)).reshape(pairs, P, -1)
    wo = np.swapaxes(g["L0_attn_W_O"], 0, 1).reshape(pairs, 2, P, -1)
    wo = np.swapaxes(wo, 1, 2).reshape(pairs, P, -1)
    wqk = np.concatenate([per_head(g["L0_attn_W_Q"]), per_head(g["L0_attn_W_K"])], axis=-1)
    w_attn = np.concatenate([wqk, wv[:, :, None, :], wo[:, :, None, :]], axis=2)
    w_x = np.stack([chunks(np.swapaxes(g["L0_xattn_" + n], 0, 1)) for n in ("q_w", "k_img_w", "v_img_w", "o_w")],
                   axis=1)
    laid = {
        "xT": chunks(np.swapaxes(x, 0, 1)), "x": chunks(x), "w_attn": w_attn,
        "ctxT": chunks(np.swapaxes(c, 0, 1)), "w_x": w_x,
        "q_b": g["L0_xattn_q_b"], "k_b": g["L0_xattn_k_img_b"], "v_b": np.swapaxes(g["L0_xattn_v_img_b"].reshape(-1, P), 0, 1),
        "o_b": g["L0_xattn_o_b"], "nq": g["L0_xattn_norm_q_w"], "nk": g["L0_xattn_norm_k_img_w"],
        "gate_w": chunks(g["L0_ffn_gate_w"]), "gate_b": g["L0_ffn_gate_b"],
        "w1": chunks(g["L0_ffn_w1"]), "b1": np.moveaxis(g["L0_ffn_b1"].reshape(g["L0_ffn_b1"].shape[0], -1, P), 2, 0),
        "w2": chunks(g["L0_ffn_w2"]), "b2": g["L0_ffn_b2"],
    }
    nc = bacc.Bacc("TRN2", target_bir_lowering=False, num_devices=1)
    arrays, args = {}, []
    for name, a in laid.items():
        a = np.ascontiguousarray(a)
        arrays["in_" + name] = a
        args.append(nc.dram_tensor("in_" + name, a.shape, mybir.dt.from_np(a.dtype), kind="ExternalInput").ap())
    tiles = x.shape[0] // P
    slots = g["L0_ffn_w1"].shape[0] * x.shape[0]
    args.append(nc.dram_tensor("x_slots", (slots, x.shape[1]), mybir.dt.float32, kind="Internal").ap())
    args.append(nc.dram_tensor("y_slots", (slots, x.shape[1]), mybir.dt.float32, kind="Internal").ap())
    out = nc.dram_tensor("out", (P, tiles, x.shape[1]), mybir.dt.float32, kind="ExternalOutput").ap()
    build_decoder_layer(nc, *args, out)
    r = run_bass_kernel_spmd(nc, [arrays], core_ids=[0])
    y = np.asarray(r.results[0]["out"])
    return np.ascontiguousarray(np.swapaxes(y, 0, 1)).reshape(g["x"].shape)
```

```python
import concourse.bass as bass
from concourse import mybir
from contextlib import ExitStack


def build_decoder_layer(nc, xT_d, x_d, w_attn_d, ctxT_d, w_x_d, qb_d, kb_d, vb_d, ob_d, nq_d, nk_d,
                        gate_w_d, gate_b_d, w1_d, b1_d, w2_d, b2_d, xs_d, ys_d, out_d):
    f32 = mybir.dt.float32
    f32r = mybir.dt.float32r
    bf16 = mybir.dt.bfloat16
    u32 = mybir.dt.uint32
    i32 = mybir.dt.int32
    ALU = mybir.AluOpType
    ACT = mybir.ActivationFunctionType
    AX = mybir.AxisListType

    P = 128
    D = 256
    DC = D // P
    B = x_d.shape[1] // 2
    TT = x_d.shape[1]
    N = TT * P
    S = N // B
    PAIRS = w_attn_d.shape[0]
    H = 2 * PAIRS
    DH = P
    STEPS = H * B
    XH = 16
    XD = D // XH
    ITEMS = XH * B
    E = w1_d.shape[0]
    F = w1_d.shape[3]
    FC = F // P
    SCALE = float(DH) ** -0.5
    XSCALE = float(XD) ** -0.5
    MASKED = 1e10 * SCALE
    LN_EPS = 1e-5
    RMS_EPS = 1e-6
    PART = 512
    BIG = 3.0e38
    RSQRT_SEED = 1597463007.0
    AWAY = 4.0 * E * N
    CAP = N

    ctx = ExitStack()
    with ctx:
        def sem(name):
            return ctx.enter_context(nc.semaphore(name))

        def sb(stack, name, shape, dt=f32):
            return stack.enter_context(nc.sbuf_tensor(name, shape, dt))

        acc = sb(ctx, "acc", [P, TT, D])
        ident = sb(ctx, "ident", [P, P])
        stats = sb(ctx, "stats", [P, TT, 6])
        mv = sb(ctx, "mv", [P, TT, 2])
        rstd = sb(ctx, "rstd", [P, TT])
        shift = sb(ctx, "shift", [P, TT])
        warm = sb(ctx, "warm", [P, 1])
        nt_a = sb(ctx, "nt_a", [P, TT])
        nt_b = sb(ctx, "nt_b", [P, TT])
        nt_c = sb(ctx, "nt_c", [P, TT])
        eps_ln = sb(ctx, "eps_ln", [P, 1])
        eps_rms = sb(ctx, "eps_rms", [P, 1])
        kss = sb(ctx, "kss", [P, TT])
        qss = sb(ctx, "qss", [P, TT])
        krs = sb(ctx, "krs", [P, TT])
        qrs = sb(ctx, "qrs", [P, TT])
        ctxT = sb(ctx, "ctxT", [P, DC, N])
        w_x = sb(ctx, "w_x", [P, 4, DC, D])
        rows_bc = sb(ctx, "rows_bc", [P, 5, D])
        vb_col = sb(ctx, "vb_col", [P, DC])
        w1 = [sb(ctx, f"w1_{i}", [P, DC, F]) for i in range(2)]
        w2 = [sb(ctx, f"w2_{i}", [P, FC, D]) for i in range(2)]
        b1 = sb(ctx, "b1", [P, E, FC])
        gate_w = sb(ctx, "gate_w", [P, DC, E])
        gate_b = sb(ctx, "gate_b", [P, E])

        logits = sb(ctx, "logits", [P, TT, E])
        probs = sb(ctx, "probs", [P, TT, E])
        top = sb(ctx, "top", [P, TT, 8])
        top_i = sb(ctx, "top_i", [P, TT, 8], u32)
        top_f = sb(ctx, "top_f", [P, TT, 2])
        w12 = sb(ctx, "w12", [P, TT])
        iota_e = sb(ctx, "iota_e", [P, E])
        iota_slot = sb(ctx, "iota_slot", [P, E])
        first = sb(ctx, "first", [P, TT, E])
        second = sb(ctx, "second", [P, TT, E])
        comb = sb(ctx, "comb", [P, TT, E])
        sel = sb(ctx, "sel", [P, TT + 1, E], bf16)
        before = sb(ctx, "before", [P, P], bf16)
        ones_bf = sb(ctx, "ones_bf", [P, P], bf16)
        slot = sb(ctx, "slot", [P, TT, E])
        slot_t = sb(ctx, "slot_t", [P, TT, E])
        slot_u = sb(ctx, "slot_u", [P, TT, E])
        slot_lh = sb(ctx, "slot_lh", [P, TT, 2])
        slot_i = sb(ctx, "slot_i", [P, TT, 2], i32)
        w_lh = sb(ctx, "w_lh", [P, TT, 2])
        tiles_i = sb(ctx, "tiles_i", [P, E], i32)
        tiles_f = sb(ctx, "tiles_f", [P, E])
        zeros_e = sb(ctx, "zeros_e", [P, E])
        cum_f = sb(ctx, "cum_f", [P, E])
        cum_i = sb(ctx, "cum_i", [P, E], i32)

        s1 = ExitStack()
        xT_raw = sb(s1, "xT_raw", [P, DC, N])
        xT_hi = sb(s1, "xT_hi", [P, DC, N], f32r)
        xT_lo = sb(s1, "xT_lo", [P, DC, N], f32r)
        w_raw = sb(s1, "w_raw", [P, 4, PART])
        wqk_hi = [sb(s1, f"wqk_hi{i}", [P, PART], f32r) for i in range(2)]
        wqk_lo = [sb(s1, f"wqk_lo{i}", [P, PART], f32r) for i in range(2)]
        wv_hi = sb(s1, "wv_hi", [P, PART], f32r)
        wv_lo = sb(s1, "wv_lo", [P, PART], f32r)
        wo_hi = sb(s1, "wo_hi", [P, PART], f32r)
        wo_lo = sb(s1, "wo_lo", [P, PART], f32r)
        QT = [sb(s1, f"QT{i}", [P, N]) for i in range(2)]
        KT = [sb(s1, f"KT{i}", [P, N]) for i in range(2)]
        V = sb(s1, "V", [P, TT, 2 * DH])
        Sm = [sb(s1, f"Sm{i}", [P, 384]) for i in range(2)]
        Pr = [sb(s1, f"Pr{i}", [P, 384]) for i in range(2)]
        PT = [sb(s1, f"PT{i}", [P, 384]) for i in range(2)]
        nmax = [sb(s1, f"nmax{i}", [P, 2]) for i in range(2)]
        rsum = [sb(s1, f"rsum{i}", [P, 2]) for i in range(2)]
        rinv = [sb(s1, f"rinv{i}", [P, 2]) for i in range(2)]
        z_hi = sb(s1, "z_hi", [P, 2, N], f32r)
        z_lo = sb(s1, "z_lo", [P, 2, N], f32r)
        mask = sb(s1, "mask", [P, 384])
        s1.close()

        s2 = ExitStack()
        QA = [sb(s2, f"QA{i}", [P, XH // 2, S], f32r) for i in range(2)]
        QB = [sb(s2, f"QB{i}", [P, XH // 2, S], f32r) for i in range(2)]
        Vd = [sb(s2, f"Vd{i}", [P, 2, XH, P]) for i in range(2)]
        q_tok = sb(s2, "q_tok", [P, TT, D])
        xP = [sb(s2, f"xP{i}", [P, 2, S]) for i in range(3)]
        xPT = [sb(s2, f"xPT{i}", [P, 2, S]) for i in range(2)]
        xz = [sb(s2, f"xz{i}", [P, DC, S]) for i in range(2)]
        xT1 = sb(s2, "xT1", [P, DC, N])
        XK1 = sb(s2, "XK1", [P, XH // 2, S], f32r)
        XK0 = sb(s2, "XK0", [P, XH // 2, S], f32r)
        XK = [XK0, XK1]
        k_tok = sb(s2, "k_tok", [P, TT, D])
        v_tok = sb(s2, "v_tok", [P, TT, D])
        stack = [sb(s2, f"stack{i}", [P, XH, 4 * XD], f32r) for i in range(2)]
        junk = sb(s2, "junk", [P, D])
        qn = sb(s2, "qn", [P, D])
        kn = sb(s2, "kn", [P, D])
        xnmax = [sb(s2, f"xnmax{i}", [P, 2]) for i in range(3)]
        xrsum = [sb(s2, f"xrsum{i}", [P, 2]) for i in range(3)]
        xrinv = [sb(s2, f"xrinv{i}", [P, 2]) for i in range(3)]
        s2.close()

        s3 = ExitStack()
        b2 = sb(s3, "b2", [P, E, D])
        xg = sb(s3, "xg", [P, D])
        xgT = sb(s3, "xgT", [P, DC, P])
        hT = sb(s3, "hT", [P, FC, P])
        hT_hi = sb(s3, "hT_hi", [P, FC, P], f32r)
        hT_lo = sb(s3, "hT_lo", [P, FC, P], f32r)
        w2_hi = [sb(s3, f"w2_hi{i}", [P, FC, D], f32r) for i in range(2)]
        w2_lo = sb(s3, "w2_lo", [P, FC, D], f32r)
        ys = sb(s3, "ys", [P, D])
        y_lo = sb(s3, "y_lo", [P, TT, D])
        y_hi = sb(s3, "y_hi", [P, TT, D])
        s3.close()

        bank = [ctx.enter_context(nc.psum_tensor(f"bank{i}", [P, 512], f32)) for i in range(8)]
        ps_qk = bank[0:2]
        ps_s = bank[2:4]
        ps_t = bank[4]
        ps_v = bank[5]
        ps_o = bank[6]
        ps_z = bank[7]
        ps_stack = bank[0:2]
        ps_xt = bank[6:8]

        names = """x_in0 x_in1 acc_in wqk_in0 wqk_in1 wv_in wo_in misc_in
            x0_written slots_zeroed
            zeroed ident_ready mask_ready x_split wqk_hi_ready wqk_split wv_hi_ready wv_split wo_hi_ready wo_split
            qk_done qk_evac v_done v_evac s_done s_masked exp_done rinv_ready p_norm pt_done pt_evac
            pv_done zhi_ready zlo_ready o_done o_added chain
            x1_ready xt_done xt_evac
            xk_done xv_done k_ready k_ss v_ready q_done q_ready q_ss
            pool_step krs_ready stats_ready rstd_ready stack_ready stk_done stk_evac_act stk_evac_dve qzero_ready vzero_ready vd_ready
            xs_done xmax_ready xexp_done xrinv_ready xp_norm xpt_done xpt_evac xpv_done xz_evac
            xo_done xbias_ready xo_added
            x2_ready x2t_done x2t_evac g_in g_done sub_ready gexp_done sel_ready rank_done rank_read slots_ready cum_ready
            xs_written w_in0 w_in1 b2_in xg_in xgt_done xgt_ready h_done h_gelu h_hi_ready h_split w2_hi_ready w2_split y_done y_evac y_stored
            ylo_in yhi_in0 yhi_in1 yhi_in2 yhi_in3 yhi_in4 yhi_in5 yhi_in6 yhi_in7 var_ready root_ready factors_ready out_ready out_written""".split()
        s = {n: sem(n) for n in names}

        block = ctx.enter_context(nc.Block())

        def pairs_loop(eng, body):
            body(0, first_pair=True)
            with eng.Fori(1, PAIRS - 1) as p:
                body(p)
            body(PAIRS - 1, last_pair=True)

        ROUNDS = [(0, TT - 2), (TT - 2, TT)]
        H_PARTS = (0, 3, 6)
        NP = len(H_PARTS)
        STACK_AT = (6, 7, 8, 9, 11, 12, 13, 14)

        def stack_parts(u, normed):
            k = u // 2 % 2
            parts = stack[u % 2][:, :, :]
            if k == 1:
                hi = parts[:, :, 0:2 * XD].rearrange("p h (a d) -> p h a d", a=2)
                lo = parts[:, :, 2 * XD:4 * XD].rearrange("p h (a d) -> p h a d", a=2)
            else:
                four = parts.rearrange("p h (a c d) -> p h a c d", a=2, c=2)
                hi, lo = four[:, :, :, 0, :], four[:, :, :, 1, :]
            whole = normed[:, :].rearrange("p (h d) -> p h d", h=XH).unsqueeze(2).to_broadcast([P, XH, 2, XD])
            return hi, lo, whole

        @block.sync
        def _(sp):
            half = N // 2
            sp.dma_start(xT_raw[:, :, 0:half], xT_d[:, :, 0:half]).then_inc(s["x_in0"], 16)
            sp.dma_start(w_raw[:, 0, :], w_attn_d[0, :, 0, :]).then_inc(s["wqk_in0"], 16)
            sp.dma_start(xT_raw[:, :, half:N], xT_d[:, :, half:N]).then_inc(s["x_in1"], 16)
            sp.dma_start(w_raw[:, 2, :], w_attn_d[0, :, 2, :]).then_inc(s["wv_in"], 16)
            sp.dma_start(w_raw[:, 1, :], w_attn_d[0, :, 1, :]).then_inc(s["wqk_in1"], 16)
            sp.dma_start(w_raw[:, 3, :], w_attn_d[0, :, 3, :]).then_inc(s["wo_in"], 16)
            sp.dma_start(acc[:, :, :], x_d).then_inc(s["acc_in"], 16)
            sp.wait_ge(s["wqk_split"], 1)
            sp.dma_start(w_raw[:, 0, :], w_attn_d[1, :, 0, :]).then_inc(s["wqk_in0"], 16)
            sp.wait_ge(s["wv_split"], 1)
            sp.dma_start(w_raw[:, 2, :], w_attn_d[1, :, 2, :]).then_inc(s["wv_in"], 16)
            sp.wait_ge(s["wqk_split"], 2)
            sp.dma_start(w_raw[:, 1, :], w_attn_d[1, :, 1, :]).then_inc(s["wqk_in1"], 16)
            sp.dma_start(ctxT[:, :, :], ctxT_d).then_inc(s["misc_in"], 16)
            sp.dma_start(w_x[:, :, :, :], w_x_d).then_inc(s["misc_in"], 16)
            sp.dma_start(vb_col[:, :], vb_d).then_inc(s["misc_in"], 16)
            for n, row in enumerate((qb_d, kb_d, ob_d, nq_d, nk_d)):
                sp.dma_start(rows_bc[:, n, :], row.partition_broadcast(P)).then_inc(s["misc_in"], 16)
            sp.dma_start(gate_w[:, :, :], gate_w_d).then_inc(s["g_in"], 16)
            sp.dma_start(gate_b[:, :], gate_b_d.partition_broadcast(P)).then_inc(s["g_in"], 16)
            sp.dma_start(b1[:, :, :], b1_d).then_inc(s["g_in"], 16)
            sp.wait_ge(s["x0_written"], 1)

            def next_parts(p):
                sp.wait_ge(s["wqk_split"], 2 * p + 3)
                sp.dma_start(w_raw[:, 0, :], w_attn_d[bass.ds(p + 2, 1), :, 0, :]).then_inc(s["wqk_in0"], 16)
                sp.wait_ge(s["wv_split"], p + 2)
                sp.dma_start(w_raw[:, 2, :], w_attn_d[bass.ds(p + 2, 1), :, 2, :]).then_inc(s["wv_in"], 16)
                sp.wait_ge(s["wo_split"], p + 1)
                sp.dma_start(w_raw[:, 3, :], w_attn_d[bass.ds(p + 1, 1), :, 3, :]).then_inc(s["wo_in"], 16)
                sp.dma_start(xs_d[bass.ds(p * N, N), :].rearrange("(a b) d -> a (b d)", a=P),
                             w1[0][:, :, :].rearrange("p c f -> p (c f)")).then_inc(s["slots_zeroed"], 16)
                sp.dma_start(ys_d[bass.ds((p + 1) * N, N), :].rearrange("(a b) d -> a (b d)", a=P),
                             w1[0][:, :, :].rearrange("p c f -> p (c f)")).then_inc(s["slots_zeroed"], 16)
                sp.wait_ge(s["wqk_split"], 2 * p + 4)
                sp.dma_start(w_raw[:, 1, :], w_attn_d[bass.ds(p + 2, 1), :, 1, :]).then_inc(s["wqk_in1"], 16)

            with sp.Fori(0, PAIRS - 2) as p:
                next_parts(p)
            sp.wait_ge(s["wo_split"], PAIRS - 1)
            sp.dma_start(w_raw[:, 3, :], w_attn_d[PAIRS - 1, :, 3, :]).then_inc(s["wo_in"], 16)
            for d, e in [(xs_d, e) for e in range(PAIRS - 2, E)] + [(ys_d, e) for e in range(PAIRS - 1, E)]:
                sp.dma_start(d[e * N:(e + 1) * N, :].rearrange("(a b) d -> a (b d)", a=P),
                             w1[0][:, :, :].rearrange("p c f -> p (c f)")).then_inc(s["slots_zeroed"], 16)
            sp.wait_ge(s["slots_zeroed"], 16 * (2 * E - 1))
            sp.wait_ge(s["y_stored"], 16)
            for e in range(2):
                sp.dma_start(w1[e][:, :, :], w1_d[e]).then_inc(s[f"w_in{e}"], 16)
                sp.dma_start(w2[e][:, :, :], w2_d[e]).then_inc(s[f"w_in{e}"], 16)
            sp.wait_ge(s["xpv_done"], ITEMS)
            sp.dma_start(b2[:, :, :], b2_d.rearrange("e d -> (e d)").partition_broadcast(P)
                         .rearrange("p (e d) -> p e d", e=E)).then_inc(s["b2_in"], 16)
            sp.wait_ge(s["cum_ready"], 1)
            sp.wait_ge(s["xs_written"], 16 * 2 * TT)
            lo = 0
            for e in range(E):
                hi = sp.value_load(cum_i[0:1, e:e + 1], min_val=1, max_val=3 * E)
                with sp.Fori(lo, hi) as i:
                    sp.wait_ge(s["xgt_done"], i + 1)
                    row = nc.s_assert_within((i - lo) * P + e * CAP, e * CAP, (e + 1) * CAP - P,
                                             skip_runtime_bounds_check_because="an expert has at most CAP tokens")
                    sp.dma_start(xg[:, :], xs_d[bass.ds(row, P), :]).then_inc(s["xg_in"], 16)
                lo = hi
            sp.wait_ge(s["xgt_done"], lo + 1)
            sp.dma_start(xg[:, :], xs_d[0:P, :]).then_inc(s["xg_in"], 16)
            for t in range(TT):
                sp.wait_ge(s["out_ready"], t + 1)
                sp.dma_start(out_d[:, t, :], acc[:, t, :]).then_inc(s["out_written"], 16)
            sp.wait_ge(s["out_written"], 16 * TT)

        @block.gpsimd
        def _(pool):
            g = nc.gpsimd
            pool.sem_inc(s["xgt_done"], 1)
            pool.sem_inc(s["h_gelu"], FC)
            pool.sem_inc(s["h_split"], NP)
            pool.sem_inc(s["y_done"], 1)
            pool.sem_inc(s["y_evac"], 1)
            g.memset(ident[:, :], 0.0).then_inc(s["zeroed"], 1)
            g.memset(mask[:, :], 0.0).then_inc(s["zeroed"], 1)
            g.memset(before[:, :], 0.0).then_inc(s["zeroed"], 1)
            pool.wait_ge(s["zeroed"], 3)
            g.affine_select(out=ident[:, :], in_=ident[:, :], compare_op=ALU.not_equal, fill=1.0,
                            base=0, pattern=[[-1, P]], channel_multiplier=1).then_inc(s["ident_ready"], 1)
            for at in (0, 256):
                g.affine_select(out=mask[:, at:at + P], in_=mask[:, at:at + P], compare_op=ALU.is_ge,
                                fill=MASKED, base=0, pattern=[[-1, P]],
                                channel_multiplier=1).then_inc(s["mask_ready"], 1)
            g.affine_select(out=before[:, :], in_=before[:, :], compare_op=ALU.is_ge, fill=1.0,
                            base=0, pattern=[[-1, P]], channel_multiplier=1).then_inc(s["ident_ready"], 1)
            g.memset(ones_bf[:, :], 1.0).then_inc(s["ident_ready"], 1)
            g.memset(sel[:, TT, :], 0.0).then_inc(s["ident_ready"], 1)
            g.memset(zeros_e[:, :], 0.0).then_inc(s["ident_ready"], 1)
            g.iota(iota_e[:, :], pattern=[[1, E]], base=0, channel_multiplier=0,
                   allow_small_or_imprecise_dtypes=True).then_inc(s["ident_ready"], 1)
            g.iota(iota_slot[:, :], pattern=[[CAP, E]], base=0, channel_multiplier=0,
                   allow_small_or_imprecise_dtypes=True).then_inc(s["ident_ready"], 1)
            g.memset(w1[0][:, :, :], 0.0).then_inc(s["x0_written"], 1)
            pool.wait_ge(s["x0_written"], 1)
            g.dma_start(ys_d[0:N, :].rearrange("(a b) d -> a (b d)", a=P),
                        w1[0][:, :, :].rearrange("p c f -> p (c f)")).then_inc(s["y_stored"], 16)

            def split(part, hi, lo, hi_sem, hi_count, done):
                pool.nop(nofuse=True)
                g.tensor_copy(hi[:, :], w_raw[:, part, :]).then_inc(hi_sem, 1)
                pool.wait_ge(hi_sem, hi_count)
                g.tensor_tensor(lo[:, :], w_raw[:, part, :], hi[:, :].bitcast(f32), ALU.subtract).then_inc(done, 1)

            def split_wo(p, first_pair=False):
                pool.wait_ge(s["wo_in"], 16 * p + 16)
                if not first_pair:
                    pool.wait_ge(s["o_done"], TT * p)
                split(3, wo_hi, wo_lo, s["wo_hi_ready"], p + 1, s["wo_split"])

            def split_parts(p, first_pair=False, last_pair=False):
                if last_pair:
                    split_wo(p)
                    return
                pool.wait_ge(s["wqk_in0"], 16 * p + 32)
                pool.wait_ge(s["qk_done"], 8 * p + 4)
                split(0, wqk_hi[0], wqk_lo[0], s["wqk_hi_ready"], 2 * p + 1, s["wqk_split"])
                pool.wait_ge(s["wv_in"], 16 * p + 32)
                pool.wait_ge(s["v_done"], TT * p + TT)
                split(2, wv_hi, wv_lo, s["wv_hi_ready"], p + 1, s["wv_split"])
                split_wo(p, first_pair)
                pool.wait_ge(s["wqk_in1"], 16 * p + 32)
                pool.wait_ge(s["qk_done"], 8 * p + 8)
                split(1, wqk_hi[1], wqk_lo[1], s["wqk_hi_ready"], 2 * p + 2, s["wqk_split"])

            pool.wait_ge(s["wqk_split"], 2)
            pool.wait_ge(s["wv_split"], 1)
            pairs_loop(pool, split_parts)

            pool.wait_ge(s["qk_done"], 4 * H)
            pool.wait_ge(s["v_done"], TT * PAIRS)
            pool.wait_ge(s["wo_split"], PAIRS)
            for i in range(2):
                g.memset(QA[i][:, :, :].bitcast(f32), 0.0).then_inc(s["qzero_ready"], 1)
                g.memset(QB[i][:, :, :].bitcast(f32), 0.0).then_inc(s["qzero_ready"], 1)
            pool_steps = [0]

            def stepped(ins):
                pool_steps[0] += 1
                ins.then_inc(s["pool_step"], 1)
                pool.wait_ge(s["pool_step"], pool_steps[0])

            def stack_make(u):
                b, k, j = u // 4, u // 2 % 2, u % 2
                t = 2 * b + j
                src, r = (k_tok, krs) if k == 0 else (q_tok, qrs)
                pool.wait_ge(s["krs_ready"], 1)
                if u >= 1:
                    pool.wait_ge(s["stack_ready"], u)
                stepped(g.tensor_scalar(kn[:, :], src[:, t, :], r[:, t:t + 1], None, ALU.mult))
                stepped(g.tensor_tensor(kn[:, :], kn[:, :], rows_bc[:, 4 - k, :], ALU.mult))
                if u >= 2:
                    pool.wait_ge(s["stk_done"], 2 * u - 2)
                hi, lo, whole = stack_parts(u, kn)
                stepped(g.tensor_copy(hi, whole))
                g.tensor_tensor(lo, whole, hi.bitcast(f32), ALU.subtract).then_inc(s["stack_ready"], 1)

            def rsqrt(dst, src, scale, eps, a, z):
                x, xh, y, t = nt_a[:, a:z], nt_c[:, a:z], dst[:, a:z], nt_b[:, a:z]
                stepped(g.tensor_scalar(x, src, scale, eps, ALU.mult, ALU.add))
                stepped(g.tensor_scalar(xh, x, -0.5, None, ALU.mult))
                stepped(g.tensor_scalar(y.bitcast(i32), x.bitcast(i32), -0.5, RSQRT_SEED, ALU.mult, ALU.add))
                for _ in range(3):
                    stepped(g.tensor_tensor(t, y, y, ALU.mult))
                    stepped(g.tensor_tensor(t, t, xh, ALU.mult))
                    stepped(g.tensor_scalar(t, t, 1.5, None, ALU.add))
                    stepped(g.tensor_tensor(y, y, t, ALU.mult))

            def q_scale(a, z):
                pool.wait_ge(s["q_ss"], z)
                rsqrt(qrs, qss[:, a:z], 1.0 / D, RMS_EPS, a, z)
                stepped(g.tensor_scalar(qrs[:, a:z], qrs[:, a:z], XSCALE, None, ALU.mult))

            stack_make(0)
            stack_make(1)
            pool.wait_ge(s["o_added"], STEPS)
            for i in range(2):
                g.memset(Vd[i][:, :, :, :], 0.0).then_inc(s["vzero_ready"], 1)
            pool.wait_ge(s["vzero_ready"], 2)

            def v_blocks(b):
                if b >= 2:
                    pool.wait_ge(s["xpv_done"], XH * (b - 1))
                pool.wait_ge(s["v_ready"], 2 * b + 2)
                for kc in range(2):
                    for u in range(2):
                        blocks = Vd[b % 2][:, kc, 8 * u:8 * u + 8, :].rearrange("p h n -> p (h n)")
                        diag = bass.AP(blocks.tensor, blocks.offset, [blocks.ap[0], [P + XD, 8], [1, XD]])
                        src = v_tok[:, 2 * b + kc, u * P:(u + 1) * P].rearrange("p (h d) -> p h d", h=8)
                        g.tensor_copy(diag, src).then_inc(s["vd_ready"], 1)

            v_blocks(0)
            stack_make(4)
            stack_make(5)
            q_scale(2, 4)
            stack_make(6)
            stack_make(7)
            v_blocks(1)
            pool.wait_ge(s["xt_done"], TT)
            for t in range(TT):
                g.tensor_tensor(acc[:, t, :], acc[:, t, :], rows_bc[:, 2, :], ALU.add).then_inc(s["xbias_ready"], 1)
            q_scale(4, TT)
            for b in range(2, B):
                stack_make(4 * b)
                stack_make(4 * b + 1)
                v_blocks(b)
                stack_make(4 * b + 2)
                stack_make(4 * b + 3)

            pool.wait_ge(s["stats_ready"], 1)
            rsqrt(rstd, mv[:, 0:TT - 2, 1], 1.0, LN_EPS, 0, TT - 2)
            pool.sem_inc(s["rstd_ready"], 1)

            pool.wait_ge(s["slots_zeroed"], 16 * (2 * E - 1))
            for r, (t0, t1) in enumerate(ROUNDS):
                pool.wait_ge(s["slots_ready"], r + 1)
                for t in range(t0, t1):
                    for k in range(2):
                        g.indirect_dma_start(xs_d, bass.IndirectOffsetOnAxis(ap=slot_i[:, t, k:k + 1], axis=0),
                                             acc[:, t, :], None).then_inc(s["xs_written"], 16)
            pool.wait_ge(s["cum_ready"], 1)
            lo = 0
            for e in range(E):
                hi = pool.value_load(cum_i[0:1, e:e + 1], min_val=1, max_val=3 * E)
                if e == E - 1:
                    pool.wait_ge(s["y_stored"], lo * 16 + 16)
                    pool.nop(nofuse=True)
                    for t in range(TT):
                        g.indirect_dma_start(y_lo[:, t, :], None, ys_d,
                                             bass.IndirectOffsetOnAxis(ap=slot_i[:, t, 0:1], axis=0))\
                            .then_inc(s["ylo_in"], 16)
                with pool.Fori(lo, hi) as i:
                    pool.wait_ge(s["y_evac"], i + 2)
                    row = nc.s_assert_within((i - lo) * P + e * CAP, e * CAP, (e + 1) * CAP - P,
                                             skip_runtime_bounds_check_because="an expert has at most CAP tokens")
                    g.dma_start(ys_d[bass.ds(row, P), :], ys[:, :]).then_inc(s["y_stored"], 16)
                lo = hi
            pool.wait_ge(s["y_stored"], lo * 16 + 16)
            pool.nop(nofuse=True)
            for t in range(TT):
                g.indirect_dma_start(y_hi[:, t, :], None, ys_d,
                                     bass.IndirectOffsetOnAxis(ap=slot_i[:, t, 1:2], axis=0)).then_inc(s[f"yhi_in{t}"], 16)

        def o_bank(p, t):
            return ps_v if isinstance(p, int) and p == PAIRS - 1 and t >= 3 and t % 2 == 1 else ps_o

        def stack_reads(n):
            batch, m = n // 8, n % 8
            return (6 * batch + (m // 2 + 1 if m < 4 else m - 1), 6 * batch + ((m + 1) // 2 if m < 4 else m - 1))

        @block.tensor
        def _(pe):
            mm = nc.tensor.matmul

            def three(out, lh, ll, rh, rl, start, stop):
                mm(out, lh, rh, start=start, stop=False)
                mm(out, lh, rl, start=False, stop=False)
                return mm(out, ll, rh, start=False, stop=stop)

            def qk_unit(p, hh, u, fill=False):
                n = 8 * p + 4 * hh + u
                if u == 0:
                    pe.wait_ge(s["wqk_split"], 2 * p + hh + 1)
                if not (fill and u < 2):
                    pe.wait_ge(s["qk_evac"], n - 1)
                cols = slice(u // 2 * 512, u // 2 * 512 + 512)
                for c in range(DC):
                    a = u % 2 * 256 + c * P
                    last = three(ps_qk[u % 2][:, :], wqk_hi[hh][:, a:a + P], wqk_lo[hh][:, a:a + P],
                                 xT_hi[:, c, cols], xT_lo[:, c, cols], c == 0, c == DC - 1)
                last.then_inc(s["qk_done"], 1)

            def v_unit(p, t, fill=False):
                if t == 0:
                    pe.wait_ge(s["wv_split"], p + 1)
                if not (fill and t == 0):
                    pe.wait_ge(s["v_evac"], TT * p + t)
                for c in range(DC):
                    last = three(ps_v[:, 0:D], xT_hi[:, c, t * P:(t + 1) * P], xT_lo[:, c, t * P:(t + 1) * P],
                                 wv_hi[:, c * 256:(c + 1) * 256], wv_lo[:, c * 256:(c + 1) * 256],
                                 c == 0, c == DC - 1)
                last.then_inc(s["v_done"], 1)

            def scores(p, st, first_pair):
                hh, b = st // B, st % B
                pe.wait_ge(s["qk_evac"], 8 * p + 4 * hh + 2 * (b // 2) + 2)
                if not (first_pair and st < 2):
                    pe.wait_ge(s["s_masked"], 8 * p + st - 1)
                ps, q_, k_ = ps_s[st % 2], QT[hh], KT[hh]
                at = b * S
                mm(ps[:, 0:P], q_[:, at:at + P], k_[:, at:at + P], start=True, stop=True)
                mm(ps[:, P:P + S], q_[:, at + P:at + S], k_[:, at:at + S], start=True, stop=True)\
                    .then_inc(s["s_done"], 1)

            def transposes(i, buf, fill=False):
                pe.wait_ge(s["p_norm"], i + 1)
                if not fill:
                    pe.wait_ge(s["pt_evac"], i)
                for k in range(3):
                    last = nc.tensor.transpose(ps_t[:, k * P:(k + 1) * P], Pr[buf][:, k * P:(k + 1) * P], ident[:, :])
                last.then_inc(s["pt_done"], 1)

            def pv(p, st, fill=False):
                hh, b = st // B, st % B
                i = 8 * p + st
                pe.wait_ge(s["v_evac"], TT * p + 2 * b + 2)
                pe.wait_ge(s["pt_evac"], i + 1)
                if not fill:
                    pe.wait_ge(s["zlo_ready"], i)
                mm(ps_z[:, 0:S], V[:, 2 * b, hh * DH:(hh + 1) * DH], PT[st % 2][:, 0:S], start=True, stop=False)
                mm(ps_z[:, P:S], V[:, 2 * b + 1, hh * DH:(hh + 1) * DH], PT[st % 2][:, S:S + P],
                   start=False, stop=True).then_inc(s["pv_done"], 1)

            def o_unit(p, t, fill=False):
                if t == 0:
                    pe.wait_ge(s["wo_split"], p + 1)
                pe.wait_ge(s["zlo_ready"], 8 * p + 5 + t // 2)
                ps = o_bank(p, t)
                if isinstance(p, int) and p == PAIRS - 1 and t >= 3:
                    pe.wait_ge(s["k_ready"], TT)
                    pe.wait_ge(s["o_added"], TT * p + t - 1)
                elif not fill:
                    pe.wait_ge(s["o_added"], TT * p + t)
                for hh in range(2):
                    last = three(ps[:, 0:D], z_hi[:, hh, t * P:(t + 1) * P], z_lo[:, hh, t * P:(t + 1) * P],
                                 wo_hi[:, hh * D:(hh + 1) * D], wo_lo[:, hh * D:(hh + 1) * D], hh == 0, hh == 1)
                last.then_inc(s["o_done"], 1)

            def xk_unit(t):
                pe.wait_ge(s["misc_in"], 16 * 8)
                pe.wait_ge(s["v_evac"], TT * PAIRS)
                if t >= 1:
                    pe.wait_ge(s["k_ready"], t)
                for c in range(DC):
                    last = mm(ps_v[:, 0:D], ctxT[:, c, t * P:(t + 1) * P], w_x[:, 1, c, :],
                              start=c == 0, stop=c == DC - 1)
                last.then_inc(s["xk_done"], 1)

            def xv_unit(t):
                pe.wait_ge(s["qk_evac"], 4 * H)
                if t >= 2:
                    pe.wait_ge(s["v_ready"], t - 1)
                for c in range(DC):
                    last = mm(ps_qk[t % 2][:, 0:D], ctxT[:, c, t * P:(t + 1) * P], w_x[:, 2, c, :],
                              start=c == 0, stop=c == DC - 1)
                last.then_inc(s["xv_done"], 1)

            def attend(p, first_pair=False, last_pair=False):
                for st in range(8):
                    hh = st // B
                    prev_p, prev = (p, st - 1) if st else (p - 1, 7)
                    started = st > 0 or not first_pair
                    v_tiles = [(p, 4 + 2 * st), (p, 5 + 2 * st)] if st < 2 else \
                        [(p + 1, 2 * (st - 6)), (p + 1, 2 * (st - 6) + 1)] if st >= 6 and not last_pair else []
                    o_tiles = [(p - 1, 2 + 2 * st), (p - 1, 3 + 2 * st)] if st < 3 and not first_pair else \
                        [(p, 0), (p, 1)] if st == 7 else []
                    if v_tiles:
                        v_unit(*v_tiles[0])
                    if last_pair and 2 <= st < 6:
                        xk_unit(2 * (st - 2))
                    scores(p, st, first_pair)
                    if o_tiles:
                        o_unit(*o_tiles[0], fill=first_pair and st == 7)
                    if started:
                        transposes(8 * p + st - 1, (st - 1) % 2, fill=first_pair and st == 1)
                    if hh == 0:
                        qk_unit(p, 1, st)
                    elif not last_pair:
                        qk_unit(p + 1, 0, st - 4)
                    else:
                        xv_unit(2 * (st - 4))
                        xv_unit(2 * (st - 4) + 1)
                    if v_tiles:
                        v_unit(*v_tiles[1])
                    if last_pair and 2 <= st < 6:
                        xk_unit(2 * (st - 2) + 1)
                    if o_tiles:
                        o_unit(*o_tiles[1])
                    if started:
                        pv(prev_p, prev, fill=first_pair and st == 1)

            pe.wait_ge(s["x_split"], 2)
            for u in range(2):
                qk_unit(0, 0, u, fill=True)
            pe.wait_ge(s["x_split"], 4)
            for u in range(2, 4):
                qk_unit(0, 0, u)
            for t in range(4):
                v_unit(0, t, fill=True)
            pe.wait_ge(s["ident_ready"], 7)
            pairs_loop(pe, attend)
            transposes(STEPS - 1, 1)

            def stack_half(n):
                u, q = n // 2, n % 2
                pe.wait_ge(s["stack_ready"], u + 1)
                if n < 2:
                    pe.wait_ge(s["v_ready"], TT)
                else:
                    pe.wait_ge(s["stk_evac_act"], stack_reads(n - 2)[0])
                    if n > 2:
                        pe.wait_ge(s["stk_evac_dve"], stack_reads(n - 2)[1])
                for hp in range(4 * q, 4 * q + 4):
                    last = nc.tensor.transpose(ps_stack[q][:, (hp % 4) * P:(hp % 4 + 1) * P],
                                               stack[u % 2][:, 2 * hp:2 * hp + 2, :]
                                               .rearrange("p a n -> p (a n)").bitcast(f32), ident[:, :])
                last.then_inc(s["stk_done"], 1)

            def xt_unit(t):
                pe.wait_ge(s["x1_ready"], t + 1)
                if t >= 2:
                    pe.wait_ge(s["xt_evac"], t - 1)
                for c in range(DC):
                    last = nc.tensor.transpose(ps_s[t % 2][:, c * P:(c + 1) * P], acc[:, t, c * P:(c + 1) * P],
                                               ident[:, :])
                last.then_inc(s["xt_done"], 1)

            def q_unit(t):
                pe.wait_ge(s["xt_evac"], t + 1)
                ps = bank[4 + t % 2] if t < 4 else bank[5]
                if t == 2 or t == 3:
                    pe.wait_ge(s["q_ready"], t - 1)
                elif t >= 4:
                    pe.wait_ge(s["q_ready"], t)
                for c in range(DC):
                    last = mm(ps[:, 0:D], xT1[:, c, t * P:(t + 1) * P], w_x[:, 0, c, :],
                              start=c == 0, stop=c == DC - 1)
                last.then_inc(s["q_done"], 1)

            def x_scores(j):
                b, h = j // XH, j % XH
                if h == 0:
                    pe.wait_ge(s["stk_evac_act"], stack_reads(8 * b + 7)[0])
                    pe.wait_ge(s["stk_evac_dve"], stack_reads(8 * b + 7)[1])
                if j >= 2:
                    pe.wait_ge(s["xexp_done"], j - 1)
                q_ = (QA, QB)[h % 2][b % 2]
                for qt in range(2):
                    last = mm(ps_s[j % 2][:, qt * S:(qt + 1) * S], q_[:, h // 2, qt * P:(qt + 1) * P],
                              XK[b % 2][:, h // 2, :], start=True, stop=True)
                last.then_inc(s["xs_done"], 1)

            def x_transposes(j):
                pe.wait_ge(s["xp_norm"], j + 1)
                if j >= 2:
                    pe.wait_ge(s["xpt_evac"], j - 1)
                for kc in range(2):
                    for qt in range(2):
                        last = nc.tensor.transpose(ps_xt[j % 2][:, kc * S + qt * P:kc * S + (qt + 1) * P],
                                                   xP[j % 3][:, qt, kc * P:(kc + 1) * P], ident[:, :])
                last.then_inc(s["xpt_done"], 1)

            def x_pv(j):
                b, h = j // XH, j % XH
                g = j // 8
                if h == 0:
                    pe.wait_ge(s["vd_ready"], 4 * b + 4)
                pe.wait_ge(s["xpt_evac"], j + 1)
                if h % 8 == 0:
                    if g < 2:
                        pe.wait_ge(s["q_ready"], 4 if g == 0 else TT)
                    else:
                        pe.wait_ge(s["xz_evac"], g - 1)
                for kc in range(2):
                    last = mm(bank[4 + g % 2][:, 0:S], Vd[b % 2][:, kc, h, :], xPT[j % 2][:, kc, :],
                              start=h % 8 == 0 and kc == 0, stop=h % 8 == 7 and kc == 1)
                last.then_inc(s["xpv_done"], 1)

            def xo_unit(t):
                b = t // 2
                pe.wait_ge(s["xz_evac"], 2 * b + 2)
                pe.wait_ge(s["stk_evac_act"], stack_reads(8 * min(b + 1, B - 1) + 7)[0])
                pe.wait_ge(s["stk_evac_dve"], stack_reads(8 * min(b + 1, B - 1) + 7)[1])
                if b == B - 1:
                    pe.wait_ge(s["rank_read"], 1)
                for c in range(DC):
                    last = mm(ps_stack[t % 2][:, 0:D], xz[b % 2][:, c, (t % 2) * P:(t % 2 + 1) * P], w_x[:, 3, c, :],
                              start=c == 0, stop=c == DC - 1)
                last.then_inc(s["xo_done"], 1)

            def x2t_unit(v):
                pe.wait_ge(s["x2_ready"], 2 * v + 2)
                if v >= 2:
                    pe.wait_ge(s["x2t_evac"], v - 1)
                for t in (2 * v, 2 * v + 1):
                    for c in range(DC):
                        at = (t % 2 * DC + c) * P
                        last = nc.tensor.transpose(ps_stack[v % 2][:, at:at + P], acc[:, t, c * P:(c + 1) * P], ident[:, :])
                last.then_inc(s["x2t_done"], 1)

            def gate_unit(r):
                t0, t1 = ROUNDS[r]
                pe.wait_ge(s["x2t_evac"], t1 // 2)
                pe.wait_ge(s["g_in"], 16 * 3)
                for t in range(t0, t1):
                    for c in range(DC):
                        last = mm(ps_stack[0][:, t * E:(t + 1) * E], xT1[:, c, t * P:(t + 1) * P], gate_w[:, c, :],
                                  start=c == 0, stop=c == DC - 1)
                last.then_inc(s["g_done"], 1)

            def rank_unit(r):
                t0, t1 = ROUNDS[r]
                end = t1 + 1 if r else t1
                pe.wait_ge(s["sel_ready"], r + 1)
                out = ps_stack[1]
                out = out[:, 0:(TT + 1) * E].rearrange("p (t e) -> p t e", e=E)
                mm(out[:, t0:end, :], before[:, :], sel[:, t0:end, :],
                   start=True, stop=False)
                for t in range(end - 1):
                    a = max(t + 1, t0)
                    last = mm(out[:, a:end, :], ones_bf[:, :], sel[:, t:t + 1, :].to_broadcast([P, end - a, E]),
                              start=False, stop=t == end - 2)
                last.then_inc(s["rank_done"], 1)

            o_unit(PAIRS - 1, 2)
            pv(PAIRS - 1, 7)
            for t in range(3, TT):
                o_unit(PAIRS - 1, t)
            for n in range(4):
                stack_half(n)
            for t in range(TT):
                xt_unit(t)
                if 1 <= t < 5:
                    q_unit(t - 1)
            for n in range(4, 8):
                stack_half(n)
            for j in range(ITEMS):
                b, h = j // XH, j % XH
                x_scores(j)
                if j >= 2:
                    x_transposes(j - 2)
                if b == 0 and h in (0, 2, 4, 6):
                    q_unit(4 + h // 2)
                if b >= 1 and h == 4:
                    xo_unit(2 * b - 2)
                    xo_unit(2 * b - 1)
                if b + 1 < B and h in STACK_AT:
                    if h == STACK_AT[0] and b >= 1:
                        pe.wait_ge(s["xo_added"], 2 * b)
                    stack_half(8 * (b + 1) + STACK_AT.index(h))
                if b == B - 1:
                    if h == 9:
                        x2t_unit(0)
                    if h == 10:
                        x2t_unit(1)
                        x2t_unit(2)
                    if h == 12:
                        gate_unit(0)
                if j >= 3:
                    x_pv(j - 3)
            x_transposes(ITEMS - 2)
            x_pv(ITEMS - 3)
            x_transposes(ITEMS - 1)
            rank_unit(0)
            x_pv(ITEMS - 2)
            x_pv(ITEMS - 1)
            xo_unit(TT - 2)
            xo_unit(TT - 1)

            x2t_unit(TT // 2 - 1)
            gate_unit(1)
            rank_unit(1)

            pe.wait_ge(s["cum_ready"], 1)

            def xg_transposes(count_in):
                pe.wait_ge(s["xg_in"], count_in)
                for c in range(DC):
                    last = nc.tensor.transpose(bank[4][:, c * P:(c + 1) * P], xg[:, c * P:(c + 1) * P], ident[:, :])
                last.then_inc(s["xgt_done"], 1)

            xg_transposes(16)
            lo = 0
            for e in range(E):
                w1e = w1[e % 2]
                hi = pe.value_load(cum_i[0:1, e:e + 1], min_val=1, max_val=3 * E)
                pe.wait_ge(s[f"w_in{e % 2}"], 32 * (e // 2 + 1))
                with pe.Fori(lo, hi) as i:
                    pe.wait_ge(s["xgt_ready"], i + 1)
                    for f in range(FC):
                        pe.wait_ge(s["h_gelu"], i * FC + f + FC - 3)
                        for c in range(DC):
                            last = mm(bank[f % 4][:, 0:P], w1e[:, c, f * P:(f + 1) * P], xgT[:, c, :],
                                      start=c == 0, stop=c == DC - 1)
                        last.then_inc(s["h_done"], 1)
                    xg_transposes(i * 16 + 32)
                    pe.wait_ge(s["y_evac"], i + 1)
                    pe.wait_ge(s["w2_split"], e + 1)
                    for f in range(FC):
                        if f in H_PARTS:
                            pe.wait_ge(s["h_split"], i * NP + NP + 1 + H_PARTS.index(f))
                        last = three(bank[5][:, 0:D], hT_hi[:, f, :], hT_lo[:, f, :], w2_hi[e % 2][:, f, :],
                                     w2_lo[:, f, :], f == 0, f == FC - 1)
                    last.then_inc(s["y_done"], 1)
                lo = hi

        @block.scalar
        def _(act):
            A = nc.scalar.activation

            def qk_evac(p, hh, u):
                act.wait_ge(s["qk_done"], 8 * p + 4 * hh + u + 1)
                dst = (QT if u % 2 == 0 else KT)[hh][:, u // 2 * 512:u // 2 * 512 + 512]
                A(dst, ps_qk[u % 2][:, :], ACT.Copy, scale=1.0 if u % 2 == 0 else -SCALE).then_inc(s["qk_evac"], 1)

            def v_evac(p, t):
                act.wait_ge(s["v_done"], TT * p + t + 1)
                A(V[:, t, :], ps_v[:, 0:D], ACT.Copy).then_inc(s["v_evac"], 1)

            def z_high(p, st):
                hh, b = st // B, st % B
                act.wait_ge(s["pv_done"], 8 * p + st + 1)
                A(z_hi[:, hh, b * S:(b + 1) * S], ps_z[:, 0:S], ACT.Copy).then_inc(s["zhi_ready"], 1)

            def exps(p, st, first_pair):
                buf = st % 2
                act.wait_ge(s["s_masked"], 8 * p + st + 1)
                if not (first_pair and st < 2):
                    act.wait_ge(s["pt_done"], 8 * p + st - 1)
                A(Pr[buf][:, 0:P], Sm[buf][:, 0:P], ACT.Exp, bias=nmax[buf][:, 0:1], scale=-1.0,
                  accum_out=rsum[buf][:, 0:1])
                A(Pr[buf][:, P:384], Sm[buf][:, P:384], ACT.Exp, bias=nmax[buf][:, 1:2], scale=-1.0,
                  accum_out=rsum[buf][:, 1:2]).then_inc(s["exp_done"], 1)

            def k_squares(t):
                act.wait_ge(s["k_ready"], t + 1)
                if t >= 1:
                    act.wait_ge(s["k_ss"], t)
                A(junk[:, :], k_tok[:, t, :], ACT.Square, accum_out=kss[:, t:t + 1]).then_inc(s["k_ss"], 1)

            def xv_evac(t):
                act.wait_ge(s["xv_done"], t + 1)
                A(v_tok[:, t, :], ps_qk[t % 2][:, 0:D], ACT.Copy).then_inc(s["v_ready"], 1)

            def evacuate(p, first_pair=False, last_pair=False):
                for st in range(8):
                    v_tiles = [(p, 4 + 2 * st), (p, 5 + 2 * st)] if st < 2 else \
                        [(p + 1, 2 * (st - 6)), (p + 1, 2 * (st - 6) + 1)] if st >= 6 and not last_pair else []
                    if st >= 2 or not first_pair:
                        z_high(*((p, st - 2) if st >= 2 else (p - 1, st + 6)))
                    if v_tiles:
                        v_evac(*v_tiles[0])
                    if last_pair and 3 <= st < 7:
                        k_squares(2 * (st - 3))
                        k_squares(2 * (st - 3) + 1)
                    exps(p, st, first_pair)
                    if st < 4:
                        qk_evac(p, 1, st)
                    elif not last_pair:
                        qk_evac(p + 1, 0, st - 4)
                    else:
                        xv_evac(2 * (st - 4))
                        xv_evac(2 * (st - 4) + 1)
                    if v_tiles:
                        v_evac(*v_tiles[1])

            for u in range(4):
                qk_evac(0, 0, u)
            for t in range(4):
                v_evac(0, t)
            pairs_loop(act, evacuate)
            z_high(PAIRS - 1, 6)

            def stack_read(n):
                b, k, j, q = n // 8, n // 4 % 2, n // 2 % 2, n % 2
                cols = slice(j * P, (j + 1) * P)
                if k == 0 and q == 1:
                    return
                act.wait_ge(s["stk_done"], n + 1)
                if n == 4:
                    act.wait_ge(s["qzero_ready"], 4)
                dst, rows = (XK, slice(0, P)) if k == 0 else (QA, slice(0, P // 2))
                A(dst[b % 2][rows, 4 * q:4 * q + 4, cols], ps_stack[q][rows, :].rearrange("p (a n) -> p a n", a=4),
                  ACT.Copy).then_inc(s["stk_evac_act"], 1)

            def q_squares(t):
                act.wait_ge(s["q_ready"], t + 1)
                if t >= 1:
                    act.wait_ge(s["q_ss"], t)
                else:
                    act.wait_ge(s["k_ss"], TT)
                A(junk[:, :], q_tok[:, t, :], ACT.Square, accum_out=qss[:, t:t + 1]).then_inc(s["q_ss"], 1)

            def xt_evac(t):
                act.wait_ge(s["xt_done"], t + 1)
                A(xT1[:, :, t * P:(t + 1) * P], ps_s[t % 2][:, 0:D].rearrange("p (c n) -> p c n", c=DC),
                  ACT.Copy).then_inc(s["xt_evac"], 1)

            def x_exps(j):
                act.wait_ge(s["xmax_ready"], j + 1)
                if j >= 3:
                    act.wait_ge(s["xpt_done"], j - 2)
                for qt in range(2):
                    last = A(xP[j % 3][:, qt, :], ps_s[j % 2][:, qt * S:(qt + 1) * S], ACT.Exp,
                             bias=xnmax[j % 3][:, qt:qt + 1], accum_out=xrsum[j % 3][:, qt:qt + 1])
                last.then_inc(s["xexp_done"], 1)

            def xpt_evac(j):
                act.wait_ge(s["xpt_done"], j + 1)
                if j >= 2:
                    act.wait_ge(s["xpv_done"], j - 1)
                A(xPT[j % 2][:, :, :], ps_xt[j % 2][:, :].rearrange("p (a n) -> p a n", a=2), ACT.Copy)\
                    .then_inc(s["xpt_evac"], 1)

            def xz_evac(g):
                b = g // 2
                act.wait_ge(s["xpv_done"], 8 * (g + 1))
                if b >= 2:
                    act.wait_ge(s["xo_done"], 2 * (b - 1))
                A(xz[b % 2][:, g % 2, :], bank[4 + g % 2][:, 0:S], ACT.Identity, bias=vb_col[:, g % 2:g % 2 + 1])\
                    .then_inc(s["xz_evac"], 1)

            def x2t_evac(v):
                act.wait_ge(s["x2t_done"], v + 1)
                A(xT1[:, :, 2 * v * P:(2 * v + 2) * P].rearrange("p c (t n) -> p t c n", t=2),
                  ps_stack[v % 2][:, :].rearrange("p (t c n) -> p t c n", t=2, c=DC), ACT.Copy).then_inc(s["x2t_evac"], 1)

            def gate_exp():
                act.wait_ge(s["sub_ready"], 1)
                A(probs[:, :, :], logits[:, :, :], ACT.Exp).then_inc(s["gexp_done"], 1)

            def norm_root(count, a, z):
                act.wait_ge(s["var_ready"], count)
                A(rstd[:, a:z], mv[:, a:z, 1], ACT.Sqrt, bias=eps_ln[:, 0:1]).then_inc(s["root_ready"], 1)

            z_high(PAIRS - 1, 7)
            act.wait_ge(s["k_ss"], TT)
            A(krs[:, :], kss[:, :], ACT.Sqrt, scale=1.0 / D, bias=eps_rms[:, 0:1]).then_inc(s["root_ready"], 1)
            stack_read(0)
            norm_root(1, 0, TT // 2)
            stack_read(2)
            norm_root(2, TT // 2, TT)
            act.wait_ge(s["misc_in"], 16 * 8)
            for t in range(TT):
                xt_evac(t)
                if t == 2:
                    q_squares(0)
                    q_squares(1)
                    act.wait_ge(s["q_ss"], 2)
                    A(qrs[:, 0:2], qss[:, 0:2], ACT.Sqrt, scale=1.0 / D, bias=eps_rms[:, 0:1])\
                        .then_inc(s["root_ready"], 1)
                    A(warm[:, :], eps_rms[:, :], ACT.Exp)
            for n in range(4, 8):
                stack_read(n)
            for j in range(ITEMS):
                b, h = j // XH, j % XH
                if j >= 2:
                    xpt_evac(j - 2)
                x_exps(j)
                if b == 0 and h in (1, 3, 5, 7):
                    if h == 1:
                        q_squares(2)
                        q_squares(3)
                    q_squares(4 + h // 2)
                if b + 1 < B and h - 1 in STACK_AT:
                    stack_read(8 * (b + 1) + STACK_AT.index(h - 1))
                if b == B - 1:
                    if h in (10, 11):
                        x2t_evac(h - 10)
                    if h == 11:
                        x2t_evac(2)
                if j >= 10 and (j - 3) % 8 == 7:
                    xz_evac((j - 10) // 8)
            xpt_evac(ITEMS - 2)
            xpt_evac(ITEMS - 1)
            xz_evac(2 * B - 1)

            norm_root(3, TT - 2, TT)
            x2t_evac(TT // 2 - 1)
            gate_exp()
            act.wait_ge(s["cum_ready"], 1)
            act.wait_ge(s["g_in"], 16 * 3)
            def w2_high(e):
                act.wait_ge(s[f"w_in{e % 2}"], 32 * (e // 2 + 1))
                for f in range(0, FC, 2):
                    last = A(w2_hi[e % 2][:, f:f + 2, :], w2[e % 2][:, f:f + 2, :], ACT.Copy)
                last.then_inc(s["w2_hi_ready"], 1)

            w2_high(0)
            lo = 0
            for e in range(E):
                hi = act.value_load(cum_i[0:1, e:e + 1], min_val=1, max_val=3 * E)
                if 1 <= e < E - 1:
                    act.wait_ge(s["y_done"], lo + 1)
                    d = s[f"w_in{(e + 1) % 2}"]
                    act.dma_start(w1[(e + 1) % 2][:, :, :], w1_d[e + 1]).then_inc(d, 16)
                    act.dma_start(w2[(e + 1) % 2][:, :, :], w2_d[e + 1]).then_inc(d, 16)
                with act.Fori(lo, hi) as i:
                    for f in range(FC):
                        act.wait_ge(s["h_done"], i * FC + f + 1)
                        if f in H_PARTS:
                            act.wait_ge(s["h_split"], i * NP + 1 + H_PARTS.index(f))
                        A(hT[:, f, :], bank[f % 4][:, 0:P], ACT.Gelu_apprx_tanh, bias=b1[:, e, f:f + 1])\
                            .then_inc(s["h_gelu"], 1)
                if e + 1 < E:
                    w2_high(e + 1)
                lo = hi
            for g in range(TT // 2):
                norm_root(4 + g, 2 * g, 2 * g + 2)
                act.wait_ge(s["factors_ready"], g + 1)
                for t in (2 * g, 2 * g + 1):
                    A(acc[:, t, :], acc[:, t, :], ACT.Identity, scale=rstd[:, t:t + 1], bias=shift[:, t:t + 1])\
                        .then_inc(s["out_ready"], 1)

        @block.vector
        def _(dve):
            v = nc.vector
            chain_count = [0]

            def chained(ins):
                chain_count[0] += 1
                ins.then_inc(s["chain"], 1)
                dve.wait_ge(s["chain"], chain_count[0])

            def inverse(dst, count):
                dve.wait_ge(s["root_ready"], count)
                return v.reciprocal(dst, dst)

            def split_x(half):
                cols = slice(half * 512, (half + 1) * 512)
                dve.wait_ge(s[f"x_in{half}"], 16)
                for c in range(DC):
                    chained(v.tensor_copy(xT_hi[:, c, cols], xT_raw[:, c, cols]))
                    v.tensor_tensor(xT_lo[:, c, cols], xT_raw[:, c, cols], xT_hi[:, c, cols].bitcast(f32),
                                    ALU.subtract).then_inc(s["x_split"], 1)

            def split_w(part, hi, lo, done):
                chained(v.tensor_copy(hi[:, :], w_raw[:, part, :]))
                v.tensor_tensor(lo[:, :], w_raw[:, part, :], hi[:, :].bitcast(f32), ALU.subtract).then_inc(done, 1)

            def mask_max(p, st, first_pair):
                buf = st % 2
                dve.wait_ge(s["s_done"], 8 * p + st + 1)
                if not (first_pair and st < 2):
                    dve.wait_ge(s["exp_done"], 8 * p + st - 1)
                dve.nop(nofuse=True)
                for a, z in ((0, P), (P, 384)):
                    last = v.tensor_tensor_reduce(out=Sm[buf][:, a:z], in0=ps_s[buf][:, a:z], in1=mask[:, a:z],
                                                  scale=1.0, scalar=BIG, op0=ALU.add, op1=ALU.min,
                                                  accum_out=nmax[buf][:, (a > 0):(a > 0) + 1])
                last.then_inc(s["s_masked"], 1)

            def pt_evac(i, buf, fill=False):
                dve.wait_ge(s["pt_done"], i + 1)
                if not fill:
                    dve.wait_ge(s["pv_done"], i - 1)
                v.tensor_copy(PT[buf][:, :], ps_t[:, 0:384]).then_inc(s["pt_evac"], 1)

            def o_add(p, t, start=False):
                m = TT * p + t
                dve.wait_ge(s["o_done"], m + 1)
                if not start:
                    dve.wait_ge(s["o_added"], m)
                v.tensor_tensor(acc[:, t, :], acc[:, t, :], o_bank(p, t)[:, 0:D], ALU.add).then_inc(s["o_added"], 1)

            def z_low(p, st):
                hh, b = st // B, st % B
                dve.wait_ge(s["zhi_ready"], 8 * p + st + 1)
                cols = slice(b * S, (b + 1) * S)
                v.tensor_tensor(z_lo[:, hh, cols], ps_z[:, 0:S], z_hi[:, hh, cols].bitcast(f32), ALU.subtract)\
                    .then_inc(s["zlo_ready"], 1)

            def normalise(i, buf):
                dve.wait_ge(s["exp_done"], i + 1)
                v.reciprocal(rinv[buf][:, :], rsum[buf][:, :]).then_inc(s["rinv_ready"], 1)
                dve.wait_ge(s["rinv_ready"], i + 1)
                v.tensor_scalar(Pr[buf][:, 0:P], Pr[buf][:, 0:P], rinv[buf][:, 0:1], None, ALU.mult)
                v.tensor_scalar(Pr[buf][:, P:384], Pr[buf][:, P:384], rinv[buf][:, 1:2], None, ALU.mult)\
                    .then_inc(s["p_norm"], 1)

            def k_add(t):
                dve.wait_ge(s["xk_done"], t + 1)
                if t == 0:
                    dve.wait_ge(s["misc_in"], 16 * 8)
                v.tensor_tensor(k_tok[:, t, :], ps_v[:, 0:D], rows_bc[:, 1, :], ALU.add).then_inc(s["k_ready"], 1)

            def soften(p, first_pair=False, last_pair=False):
                for st in range(8):
                    o_tiles = [(p - 1, 2 + 2 * st), (p - 1, 3 + 2 * st)] if st < 3 and not first_pair else \
                        [(p, 0), (p, 1)] if st == 7 else []
                    if 1 <= st < 4 and not first_pair:
                        o_add(p - 1, 1 + 2 * st)
                    if st == 0 and not first_pair:
                        o_add(p - 1, 1)
                    if st >= 2 or not first_pair:
                        z_low(*((p, st - 2) if st >= 2 else (p - 1, st + 6)))
                    if last_pair and 2 <= st < 6:
                        k_add(2 * (st - 2))
                    mask_max(p, st, first_pair)
                    if o_tiles:
                        o_add(*o_tiles[0], start=first_pair)
                    if st > 0 or not first_pair:
                        pt_evac(8 * p + st - 1, (st - 1) % 2, fill=first_pair and st < 3)
                    normalise(8 * p + st, st % 2)
                    if last_pair and 2 <= st < 6:
                        k_add(2 * (st - 2) + 1)

            v.memset(eps_ln[:, :], LN_EPS)
            v.memset(eps_rms[:, :], RMS_EPS)
            split_x(0)
            dve.wait_ge(s["wqk_in0"], 16)
            split_w(0, wqk_hi[0], wqk_lo[0], s["wqk_split"])
            split_x(1)
            dve.wait_ge(s["wv_in"], 16)
            split_w(2, wv_hi, wv_lo, s["wv_split"])
            dve.wait_ge(s["wqk_in1"], 16)
            split_w(1, wqk_hi[1], wqk_lo[1], s["wqk_split"])
            dve.wait_ge(s["mask_ready"], 2)
            dve.wait_ge(s["acc_in"], 16)
            pairs_loop(dve, soften)

            def stack_make(u):
                t = u % 2
                dve.wait_ge(s["stack_ready"], u)
                chained(v.scalar_tensor_tensor(out=qn[:, :], in0=q_tok[:, t, :], scalar=qrs[:, t:t + 1],
                                               in1=rows_bc[:, 3, :], op0=ALU.mult, op1=ALU.mult))
                dve.wait_ge(s["stk_done"], 2 * u - 2)
                hi, lo, whole = stack_parts(u, qn)
                chained(v.tensor_copy(hi, whole))
                v.tensor_tensor(lo, whole, hi.bitcast(f32), ALU.subtract).then_inc(s["stack_ready"], 1)

            def stack_read(n):
                b, k, j, q = n // 8, n // 4 % 2, n // 2 % 2, n % 2
                cols = slice(j * P, (j + 1) * P)
                if k == 0 and q == 0:
                    return
                dve.wait_ge(s["stk_done"], n + 1)
                if n == 4:
                    dve.wait_ge(s["qzero_ready"], 4)
                dst, rows = (XK, slice(0, P)) if k == 0 else (QB, slice(P // 2, P))
                v.tensor_copy(dst[b % 2][rows, 4 * q:4 * q + 4, cols],
                              ps_stack[q][rows, :].rearrange("p (a n) -> p a n", a=4)).then_inc(s["stk_evac_dve"], 1)

            def row_stats(t):
                chained(v.bn_stats(stats[:, t, :], acc[:, t, :]))
                return v.bn_aggr(mv[:, t, :], stats[:, t, :])

            def norm_apply(t, ready):
                v.tensor_scalar(acc[:, t, :], acc[:, t, :], mv[:, t, 0:1], rstd[:, t:t + 1],
                                ALU.subtract, ALU.mult).then_inc(ready, 1)

            def q_add(t):
                dve.wait_ge(s["q_done"], t + 1)
                ps = bank[4 + t % 2] if t < 4 else bank[5]
                v.tensor_tensor(q_tok[:, t, :], ps[:, 0:D], rows_bc[:, 0, :], ALU.add).then_inc(s["q_ready"], 1)

            def x_max(j):
                dve.wait_ge(s["xs_done"], j + 1)
                v.tensor_reduce(xnmax[j % 3][:, :], ps_s[j % 2][:, :].rearrange("p (a n) -> p a n", a=2), AX.X,
                                ALU.max, negate=True).then_inc(s["xmax_ready"], 1)

            def x_normalise(j):
                dve.wait_ge(s["xexp_done"], j + 1)
                v.reciprocal(xrinv[j % 3][:, :], xrsum[j % 3][:, :]).then_inc(s["xrinv_ready"], 1)
                dve.wait_ge(s["xrinv_ready"], j + 1)
                for qt in range(2):
                    last = v.tensor_scalar(xP[j % 3][:, qt, :], xP[j % 3][:, qt, :], xrinv[j % 3][:, qt:qt + 1], None,
                                           ALU.mult)
                last.then_inc(s["xp_norm"], 1)

            def xo_add(t, stats_sem="chain"):
                dve.wait_ge(s["xo_done"], t + 1)
                dve.wait_ge(s["xbias_ready"], TT)
                v.tensor_tensor(acc[:, t, :], acc[:, t, :], ps_stack[t % 2][:, 0:D], ALU.add).then_inc(s["xo_added"], 1)
                dve.wait_ge(s["xo_added"], t + 1)
                if stats_sem == "chain":
                    chained(row_stats(t))
                else:
                    row_stats(t).then_inc(s[stats_sem], 1)

            def over_experts(a, t0, t1):
                return a.unsqueeze(2).to_broadcast([P, t1 - t0, E])

            def gate_logits(r):
                t0, t1 = ROUNDS[r]
                n = t1 - t0
                dve.wait_ge(s["g_done"], r + 1)
                chained(v.tensor_tensor(logits[:, t0:t1, :], ps_stack[0][:, t0 * E:t1 * E].rearrange("p (t e) -> p t e", t=n),
                                        gate_b[:, :].unsqueeze(1).to_broadcast([P, n, E]), ALU.add))
                for t in range(t0, t1):
                    last = v.max(top[:, t, :], logits[:, t, :])
                chained(last)

            def gate_index(r):
                t0, t1 = ROUNDS[r]
                for t in range(t0, t1):
                    last = v.max_index(top_i[:, t, :], top[:, t, :], logits[:, t, :])
                chained(last)

            def gate_select(r):
                t0, t1 = ROUNDS[r]
                n = t1 - t0
                chained(v.tensor_copy(top_f[:, t0:t1, :], top_i[:, t0:t1, 0:2]))
                for k, oneh in enumerate((first, second)):
                    last = v.tensor_tensor(oneh[:, t0:t1, :], iota_e[:, :].unsqueeze(1).to_broadcast([P, n, E]),
                                           over_experts(top_f[:, t0:t1, k], t0, t1), ALU.is_equal)
                chained(last)
                v.tensor_tensor(sel[:, t0:t1, :], first[:, t0:t1, :], second[:, t0:t1, :], ALU.add)\
                    .then_inc(s["sel_ready"], 1)

            def over_all(a):
                return a.unsqueeze(2).to_broadcast([P, TT, E])

            def gate_shift():
                v.tensor_tensor(logits[:, :, :], logits[:, :, :], over_all(top[:, :, 0]), ALU.subtract)\
                    .then_inc(s["sub_ready"], 1)

            def gate_weights():
                dve.wait_ge(s["gexp_done"], 1)
                chained(v.tensor_reduce(w12[:, :], probs[:, :, :], AX.X, ALU.add))
                chained(v.reciprocal(w12[:, :], w12[:, :]))
                chained(v.tensor_tensor(probs[:, :, :], probs[:, :, :], over_all(w12[:, :]), ALU.mult))
                chained(v.tensor_tensor(comb[:, :, :], probs[:, :, :], sel[:, 0:TT, :], ALU.mult))
                chained(v.tensor_reduce(w12[:, :], comb[:, :, :], AX.X, ALU.add))
                chained(v.reciprocal(w12[:, :], w12[:, :]))
                chained(v.tensor_tensor(comb[:, :, :], comb[:, :, :], over_all(w12[:, :]), ALU.mult))

            def slots(r):
                t0, t1 = ROUNDS[r]
                n = t1 - t0
                sl, st, st_hi = slot[:, t0:t1, :], slot_t[:, t0:t1, :], slot_u[:, t0:t1, :]
                dve.wait_ge(s["rank_done"], r + 1)
                last = v.tensor_tensor(sl, ps_stack[1][:, t0 * E:t1 * E].rearrange("p (t e) -> p t e", t=n),
                                       iota_slot[:, :].unsqueeze(1).to_broadcast([P, n, E]), ALU.add)
                if r == 0:
                    last.then_inc(s["rank_read"], 1)
                    dve.wait_ge(s["rank_read"], 1)
                else:
                    chained(last)
                v.scalar_tensor_tensor(out=st, in0=sel[:, t0:t1, :], scalar=-AWAY, in1=sl, op0=ALU.mult, op1=ALU.add)
                chained(v.scalar_tensor_tensor(out=st_hi, in0=sel[:, t0:t1, :], scalar=AWAY, in1=sl, op0=ALU.mult,
                                               op1=ALU.add))
                v.tensor_reduce(slot_lh[:, t0:t1, 0], st, AX.X, ALU.min)
                chained(v.tensor_reduce(slot_lh[:, t0:t1, 1], st_hi, AX.X, ALU.max))
                v.tensor_scalar(slot_lh[:, t0:t1, 0], slot_lh[:, t0:t1, 0], AWAY, None, ALU.add)
                chained(v.tensor_scalar(slot_lh[:, t0:t1, 1], slot_lh[:, t0:t1, 1], -AWAY, None, ALU.add))
                v.tensor_copy(slot_i[:, t0:t1, :], slot_lh[:, t0:t1, :]).then_inc(s["slots_ready"], 1)

            def count_tiles():
                chained(v.tensor_scalar(tiles_i[:, :], ps_stack[1][:, TT * E:(TT + 1) * E], P / 2 - 0.5, 1.0 / P,
                                        ALU.add, ALU.mult))
                chained(v.tensor_scalar(tiles_f[:, :], tiles_i[:, :], 1.0, None, ALU.max))
                chained(v.tensor_tensor_scan(cum_f[:, :], tiles_f[:, :], zeros_e[:, :], 0.0, ALU.add, ALU.add))
                v.tensor_copy(cum_i[:, :], cum_f[:, :]).then_inc(s["cum_ready"], 1)

            def slot_weights():
                for k in range(2):
                    chained(v.tensor_tensor(slot_t[:, :, :], slot[:, :, :], over_all(slot_lh[:, :, k]), ALU.is_equal))
                    chained(v.tensor_tensor(slot_t[:, :, :], slot_t[:, :, :], comb[:, :, :], ALU.mult))
                    chained(v.tensor_reduce(w_lh[:, :, k], slot_t[:, :, :], AX.X, ALU.add))

            def norm_half(g):
                half = range(g * TT // 2, (g + 1) * TT // 2)
                for t in half:
                    last = v.bn_stats(stats[:, t, :], acc[:, t, :])
                chained(last)
                for t in half:
                    last = v.bn_aggr(mv[:, t, :], stats[:, t, :])
                last.then_inc(s["var_ready"], 1)
                chained(inverse(rstd[:, half.start:half.stop], 2 + g))
                for t in half:
                    norm_apply(t, s["x1_ready"])

            o_add(PAIRS - 1, 1)
            pt_evac(STEPS - 1, 1)
            z_low(PAIRS - 1, 6)
            o_add(PAIRS - 1, 2)
            z_low(PAIRS - 1, 7)
            for t in range(3, TT):
                o_add(PAIRS - 1, t)
                if t == 3:
                    inverse(krs[:, :], 1).then_inc(s["krs_ready"], 1)
            stack_read(1)
            dve.wait_ge(s["o_added"], STEPS)
            norm_half(0)
            stack_read(3)
            norm_half(1)
            q_add(0)
            q_add(1)

            chained(inverse(qrs[:, 0:2], 4))
            chained(v.tensor_scalar(qrs[:, 0:2], qrs[:, 0:2], XSCALE, None, ALU.mult))
            stack_make(2)
            stack_make(3)
            q_add(2)
            q_add(3)
            for n in range(4, 8):
                stack_read(n)
            for j in range(ITEMS):
                b, h = j // XH, j % XH
                x_max(j)
                if j >= 1:
                    x_normalise(j - 1)
                if b == 0 and h in (1, 3, 5, 7):
                    q_add(4 + h // 2)
                if b + 1 < B and h - 1 in STACK_AT:
                    stack_read(8 * (b + 1) + STACK_AT.index(h - 1))
                if b >= 1 and h == 5:
                    xo_add(2 * b - 2)
                    xo_add(2 * b - 1)
                if b == B - 1:
                    if h == 6:
                        dve.sem_inc(s["stats_ready"], 1)
                    if h in (8, 9):
                        dve.wait_ge(s["rstd_ready"], 1)
                        for t in range(3 * (h - 8), 3 * (h - 7)):
                            norm_apply(t, s["x2_ready"])
                    if h == 13:
                        gate_logits(0)
                    if h == 14:
                        gate_index(0)
                    if h == 15:
                        gate_select(0)
            x_normalise(ITEMS - 1)
            slots(0)
            xo_add(TT - 2)
            xo_add(TT - 1, stats_sem="var_ready")
            chained(inverse(rstd[:, TT - 2:TT], 5))
            norm_apply(TT - 2, s["x2_ready"])
            norm_apply(TT - 1, s["x2_ready"])
            gate_logits(1)
            gate_index(1)
            gate_select(1)
            slots(1)
            count_tiles()
            gate_shift()

            def xgt_evac(count_done):
                dve.wait_ge(s["xgt_done"], count_done)
                v.tensor_copy(xgT[:, :, :], bank[4][:, 0:D].rearrange("p (c n) -> p c n", c=DC))\
                    .then_inc(s["xgt_ready"], 1)

            def w2_low(e):
                dve.wait_ge(s["w2_hi_ready"], e + 1)
                for f in range(0, FC, 2):
                    last = v.tensor_tensor(w2_lo[:, f:f + 2, :], w2[e % 2][:, f:f + 2, :],
                                           w2_hi[e % 2][:, f:f + 2, :].bitcast(f32), ALU.subtract)
                last.then_inc(s["w2_split"], 1)

            gate_weights()
            slot_weights()
            dve.wait_ge(s["b2_in"], 16)
            xgt_evac(2)
            lo = 0
            for e in range(E):
                hi = dve.value_load(cum_i[0:1, e:e + 1], min_val=1, max_val=3 * E)
                w2_low(e)
                with dve.Fori(lo, hi) as i:
                    for q in range(NP):
                        part = slice(H_PARTS[q], (H_PARTS + (FC,))[q + 1])
                        dve.wait_ge(s["h_gelu"], i * FC + FC + part.stop)
                        if q == 0:
                            dve.wait_ge(s["y_done"], i + 1)
                        v.tensor_copy(hT_hi[:, part, :], hT[:, part, :]).then_inc(s["h_hi_ready"], 1)
                        dve.wait_ge(s["h_hi_ready"], i * NP + q + 1)
                        v.tensor_tensor(hT_lo[:, part, :], hT[:, part, :], hT_hi[:, part, :].bitcast(f32),
                                        ALU.subtract).then_inc(s["h_split"], 1)
                    xgt_evac(i + 3)
                    dve.wait_ge(s["y_done"], i + 2)
                    dve.wait_ge(s["y_stored"], i * 16 + 16)
                    v.tensor_tensor(ys[:, :], bank[5][:, 0:D], b2[:, e, :], ALU.add).then_inc(s["y_evac"], 1)
                lo = hi
            for t in range(TT):
                dve.wait_ge(s["ylo_in"], 16 * TT)
                last = v.scalar_tensor_tensor(out=acc[:, t, :], in0=y_lo[:, t, :], scalar=w_lh[:, t, 0:1],
                                              in1=acc[:, t, :], op0=ALU.mult, op1=ALU.add)
            chained(last)
            def factors(g):
                two = slice(2 * g, 2 * g + 2)
                chained(inverse(rstd[:, two], 6 + g))
                v.scalar_tensor_tensor(out=shift[:, two], in0=mv[:, two, 0], scalar=-1.0, in1=rstd[:, two],
                                       op0=ALU.mult, op1=ALU.mult).then_inc(s["factors_ready"], 1)

            for g in range(TT // 2):
                pair = (2 * g, 2 * g + 1)
                for t in pair:
                    dve.wait_ge(s[f"yhi_in{t}"], 16)
                    last = v.scalar_tensor_tensor(out=acc[:, t, :], in0=y_hi[:, t, :], scalar=w_lh[:, t, 1:2],
                                                  in1=acc[:, t, :], op0=ALU.mult, op1=ALU.add)
                chained(last)
                if g >= 1:
                    factors(g - 1)
                for t in pair:
                    last = v.bn_stats(stats[:, t, :], acc[:, t, :])
                chained(last)
                for t in pair:
                    last = v.bn_aggr(mv[:, t, :], stats[:, t, :])
                last.then_inc(s["var_ready"], 1)
            factors(TT // 2 - 1)


def kernel(**inputs):
    import numpy as np
    import concourse.bacc as bacc
    from concourse.bass_utils import run_bass_kernel_spmd

    g = {k: np.asarray(a) for k, a in inputs.items()}
    P = 128

    def chunks(a):
        n = a.shape[-2] // P
        b = a.reshape(*a.shape[:-2], n, P, a.shape[-1])
        return np.moveaxis(b, -3, -2)

    x = g["x"].reshape(-1, g["x"].shape[-1])
    c = g["ctx_2048"].reshape(-1, x.shape[1])
    pairs = g["L0_attn_W_Q"].shape[0] // 2

    def per_head(w):
        t = chunks(np.swapaxes(w, 1, 2))
        t = t.reshape(pairs, 2, *t.shape[1:])
        return np.moveaxis(t, 1, 2).reshape(pairs, P, 2, -1)

    wv = chunks(np.swapaxes(g["L0_attn_W_V"], 1, 2))
    wv = wv.reshape(pairs, 2, *wv.shape[1:])
    wv = np.transpose(wv, (0, 2, 3, 1, 4)).reshape(pairs, P, -1)
    wo = np.swapaxes(g["L0_attn_W_O"], 0, 1).reshape(pairs, 2, P, -1)
    wo = np.swapaxes(wo, 1, 2).reshape(pairs, P, -1)
    wqk = np.concatenate([per_head(g["L0_attn_W_Q"]), per_head(g["L0_attn_W_K"])], axis=-1)
    w_attn = np.concatenate([wqk, wv[:, :, None, :], wo[:, :, None, :]], axis=2)
    w_x = np.stack([chunks(np.swapaxes(g["L0_xattn_" + n], 0, 1)) for n in ("q_w", "k_img_w", "v_img_w", "o_w")],
                   axis=1)
    laid = {
        "xT": chunks(np.swapaxes(x, 0, 1)), "x": chunks(x), "w_attn": w_attn,
        "ctxT": chunks(np.swapaxes(c, 0, 1)), "w_x": w_x,
        "q_b": g["L0_xattn_q_b"], "k_b": g["L0_xattn_k_img_b"], "v_b": np.swapaxes(g["L0_xattn_v_img_b"].reshape(-1, P), 0, 1),
        "o_b": g["L0_xattn_o_b"], "nq": g["L0_xattn_norm_q_w"], "nk": g["L0_xattn_norm_k_img_w"],
        "gate_w": chunks(g["L0_ffn_gate_w"]), "gate_b": g["L0_ffn_gate_b"],
        "w1": chunks(g["L0_ffn_w1"]), "b1": np.moveaxis(g["L0_ffn_b1"].reshape(g["L0_ffn_b1"].shape[0], -1, P), 2, 0),
        "w2": chunks(g["L0_ffn_w2"]), "b2": g["L0_ffn_b2"],
    }
    nc = bacc.Bacc("TRN2", target_bir_lowering=False, num_devices=1)
    arrays, args = {}, []
    for name, a in laid.items():
        a = np.ascontiguousarray(a)
        arrays["in_" + name] = a
        args.append(nc.dram_tensor("in_" + name, a.shape, mybir.dt.from_np(a.dtype), kind="ExternalInput").ap())
    tiles = x.shape[0] // P
    slots = g["L0_ffn_w1"].shape[0] * x.shape[0]
    args.append(nc.dram_tensor("x_slots", (slots, x.shape[1]), mybir.dt.float32, kind="Internal").ap())
    args.append(nc.dram_tensor("y_slots", (slots, x.shape[1]), mybir.dt.float32, kind="Internal").ap())
    out = nc.dram_tensor("out", (P, tiles, x.shape[1]), mybir.dt.float32, kind="ExternalOutput").ap()
    build_decoder_layer(nc, *args, out)
    r = run_bass_kernel_spmd(nc, [arrays], core_ids=[0])
    y = np.asarray(r.results[0]["out"])
    return np.ascontiguousarray(np.swapaxes(y, 0, 1)).reshape(g["x"].shape)
```
